# Optimizing a Trainium2 kernel written in Bass

```python
import numpy as np
import jax
import jax.numpy as jnp

def _softmax(x, axis=-1):
    return jax.nn.softmax(x, axis=axis)
def _gelu(x):
    return jax.nn.gelu(x, approximate=True)
def _silu(x):
    return jax.nn.silu(x)
def _sigmoid(x):
    return jax.nn.sigmoid(x)
def _layernorm(x, axis=-1, eps=1e-5):
    m = jnp.mean(x, axis=axis, keepdims=True)
    v = jnp.var(x, axis=axis, keepdims=True)
    return (x - m) / jnp.sqrt(v + eps)
def _scatter_add(tgt, idx, src, axis=0):
    return tgt.at[idx].add(src)
def _segment_sum(src, seg, n):
    return jax.ops.segment_sum(src, seg, n)

kernel_name = 'mk_conv_attn_hybrid_d4_conv_nchw128_9806b4'

def setup_inputs(seed: int = 0):
    np.random.seed(seed)
    _w = jnp.asarray
    def _rec_inputs():
        import jax
        import jax.numpy as jnp
        _gk = jax.random.key(seed)
        x = -0.0005207 + 1.001 * jax.random.normal(jax.random.fold_in(_gk, 1), (4, 128, 64, 64), jnp.float32)
        return x
    x = _rec_inputs()
    def _L0_conv_setup():
        import jax, jax.numpy as jnp
        import numpy as np
        G, KS = (8, 3)
        K = KS * KS
        OM = 32
        EPS = 1e-05

        def _dcnv4(x, w_value, b_value, w_off, b_off, w_out, b_out, bn_gamma, bn_beta, bn_mean, bn_var):
            N, C, H, W = x.shape
            Cg = C // G
            P = H * W
            xf = x.transpose(0, 2, 3, 1).reshape(N, P, C)
            val = xf @ w_value + b_value
            om = (xf @ w_off + b_off).reshape(N, P, G, OM)
            offset = om[..., :2 * K].reshape(N, P, G, K, 2)
            mask = om[..., 2 * K:3 * K]
            py, px = jnp.meshgrid(jnp.arange(H), jnp.arange(W), indexing='ij')
            kk = jnp.arange(KS) - (KS - 1) // 2
            ky, kx = jnp.meshgrid(kk, kk, indexing='ij')
            base_y = (py.reshape(-1)[:, None] + ky.reshape(-1)[None, :]).astype(x.dtype)
            base_x = (px.reshape(-1)[:, None] + kx.reshape(-1)[None, :]).astype(x.dtype)
            sy = base_y[None, :, None, :] + offset[..., 1]
            sx = base_x[None, :, None, :] + offset[..., 0]
            vflat = val.reshape(N, P, G, Cg).transpose(0, 2, 1, 3)

            def gather(iy, ix):
                lin = jnp.clip(iy, 0, H - 1) * W + jnp.clip(ix, 0, W - 1)
                lin = lin.transpose(0, 2, 1, 3).reshape(N, G, P * K)
                g = jnp.take_along_axis(vflat, lin[..., None], axis=2)
                return g.reshape(N, G, P, K, Cg).transpose(0, 2, 1, 3, 4)
            y0 = jnp.floor(sy)
            x0 = jnp.floor(sx)
            ty = sy - y0
            tx = sx - x0
            y0i = y0.astype(jnp.int32)
            x0i = x0.astype(jnp.int32)

            def valid(iy, ix):
                return ((iy >= 0) & (iy < H) & (ix >= 0) & (ix < W)).astype(x.dtype)
            acc = jnp.zeros((N, P, G, K, Cg), x.dtype)
            for dy, dx, wgt in ((0, 0, (1 - ty) * (1 - tx)), (0, 1, (1 - ty) * tx), (1, 0, ty * (1 - tx)), (1, 1, ty * tx)):
                iy, ix = (y0i + dy, x0i + dx)
                acc = acc + gather(iy, ix) * (wgt * valid(iy, ix))[..., None]
            out = (acc * mask[..., None]).sum(axis=3)
            out = out.reshape(N, P, C) @ w_out + b_out
            out = out.reshape(N, H, W, C).transpose(0, 3, 1, 2)
            inv = bn_gamma / jnp.sqrt(bn_var + EPS)
            out = out * inv[None, :, None, None] + (bn_beta - bn_mean * inv)[None, :, None, None]
            return out * jax.nn.sigmoid(out)
        key = jax.random.key(seed)
        ks = jax.random.split(key, 12)
        N, C, H, W = (4, 128, 64, 64)
        x = jax.random.normal(ks[0], (N, C, H, W), jnp.float32)
        w_value = jax.random.normal(ks[1], (C, C), jnp.float32) / np.sqrt(C)
        b_value = jax.random.normal(ks[2], (C,), jnp.float32) * 0.01
        w_off = jax.random.normal(ks[3], (C, G * OM), jnp.float32) * 0.02
        b_off = jax.random.normal(ks[4], (G * OM,), jnp.float32) * 0.01
        w_out = jax.random.normal(ks[5], (C, C), jnp.float32) / np.sqrt(C)
        b_out = jax.random.normal(ks[6], (C,), jnp.float32) * 0.01
        bn_gamma = jax.random.uniform(ks[7], (C,), jnp.float32, 0.5, 1.5)
        bn_beta = jax.random.normal(ks[8], (C,), jnp.float32) * 0.1
        bn_mean = jax.random.normal(ks[9], (C,), jnp.float32) * 0.1
        bn_var = jax.random.uniform(ks[10], (C,), jnp.float32, 0.5, 1.5)
        return dict(x=x, w_value=w_value, b_value=b_value, w_off=w_off, b_off=b_off, w_out=w_out, b_out=b_out, bn_gamma=bn_gamma, bn_beta=bn_beta, bn_mean=bn_mean, bn_var=bn_var)
    _L0_conv_all = _L0_conv_setup()
    _L0_conv_in = {k: v for k, v in _L0_conv_all.items() if k in ('w_value', 'b_value', 'w_off', 'b_off', 'w_out', 'b_out', 'bn_gamma', 'bn_beta', 'bn_mean', 'bn_var', )}
    del _L0_conv_all

    def _L1_conv_setup():
        import jax, jax.numpy as jnp
        import numpy as np
        from jax import lax
        B, C, H, W = (8, 128, 64, 64)
        L = H * W
        DM, DI, DS, DC, NH, HD = (32, 64, 64, 4, 1, 64)

        def _causal_dwconv1d(x, w, b):
            xc = jnp.transpose(x, (0, 2, 1))
            xc = jnp.pad(xc, ((0, 0), (0, 0), (DC - 1, 0)))
            o = lax.conv_general_dilated(xc, w[:, None, :], (1,), 'VALID', feature_group_count=w.shape[0], dimension_numbers=('NCH', 'OIH', 'NCH'))
            return jnp.transpose(o + b[None, :, None], (0, 2, 1))

        def _mamba2(u, W_in, conv_w, conv_b, dt_bias, A_log, D, norm_w, W_out):
            b, l, _ = u.shape
            zxbcdt = u @ W_in
            z = zxbcdt[..., :DI]
            xBC = zxbcdt[..., DI:DI + DI + 2 * DS]
            dt = zxbcdt[..., -NH:]
            xBC = jax.nn.silu(_causal_dwconv1d(xBC, conv_w, conv_b))
            xs = xBC[..., :DI]
            Bm = xBC[..., DI:DI + DS]
            Cm = xBC[..., DI + DS:]
            dt = jax.nn.softplus(dt + dt_bias)
            dA = jnp.exp(dt * -jnp.exp(A_log))
            xh = xs.reshape(b, l, NH, HD)
            dtx = dt[..., None] * xh

            def step(h, inp):
                dA_t, dtx_t, B_t, C_t = inp
                h = dA_t[:, :, None, None] * h + dtx_t[..., None] * B_t[:, None, None, :]
                y = jnp.einsum('bhpn,bn->bhp', h, C_t)
                return (h, y)
            h0 = jnp.zeros((b, NH, HD, DS), u.dtype)
            _, ys = lax.scan(step, h0, (jnp.moveaxis(dA, 1, 0), jnp.moveaxis(dtx, 1, 0), jnp.moveaxis(Bm, 1, 0), jnp.moveaxis(Cm, 1, 0)))
            y = jnp.moveaxis(ys, 0, 1) + D[None, None, :, None] * xh
            y = y.reshape(b, l, DI)
            y = y * jax.nn.silu(z)
            y = y * lax.rsqrt(jnp.mean(y * y, -1, keepdims=True) + 1e-05) * norm_w
            return y @ W_out

        def _forward(x, lin1_w, lin1_b, dw_w, dw_b, fc_in_w, mam_in_w, mam_conv_w, mam_conv_b, mam_dt_bias, mam_A_log, mam_D, mam_norm_w, mam_out_w, fc_out_w, bn_g, bn_b, conv4_w, conv4_b):
            b, c, h, w = x.shape
            o = jnp.einsum('bihw,io->bohw', x, lin1_w) + lin1_b[None, :, None, None]
            o = lax.conv_general_dilated(o, dw_w, (1, 1), 'SAME', feature_group_count=c, dimension_numbers=('NCHW', 'OIHW', 'NCHW')) + dw_b[None, :, None, None]
            o = jax.nn.silu(o)
            s = jnp.einsum('bcl,cd->bld', o.reshape(b, c, h * w), fc_in_w)
            y1 = _mamba2(s, mam_in_w[0], mam_conv_w[0], mam_conv_b[0], mam_dt_bias[0], mam_A_log[0], mam_D[0], mam_norm_w[0], mam_out_w[0])
            y2 = jnp.flip(_mamba2(jnp.flip(s, 1), mam_in_w[1], mam_conv_w[1], mam_conv_b[1], mam_dt_bias[1], mam_A_log[1], mam_D[1], mam_norm_w[1], mam_out_w[1]), 1)
            o = jnp.transpose((y1 + y2) @ fc_out_w, (0, 2, 1)).reshape(b, c, h, w)
            mu = jnp.mean(o, (0, 2, 3), keepdims=True)
            var = jnp.mean((o - mu) ** 2, (0, 2, 3), keepdims=True)
            o = (o - mu) * lax.rsqrt(var + 1e-05) * bn_g[None, :, None, None] + bn_b[None, :, None, None]
            g = jax.nn.sigmoid(jnp.einsum('bihw,io->bohw', o, conv4_w) + conv4_b[None, :, None, None])
            return g * x + x
        key = jax.random.key(seed)
        ks = jax.random.split(key, 12)

        def r(i, shape, s):
            return jax.random.normal(ks[i], shape, jnp.float32) * s
        return {'x': jax.random.normal(ks[0], (B, C, H, W), jnp.float32), 'lin1_w': r(1, (C, C), 0.05), 'lin1_b': jnp.zeros((C,), jnp.float32), 'dw_w': r(2, (C, 1, 3, 3), 0.1), 'dw_b': jnp.zeros((C,), jnp.float32), 'fc_in_w': r(3, (C, DM), 0.05), 'mam_in_w': r(4, (2, DM, 2 * DI + 2 * DS + NH), 0.05), 'mam_conv_w': r(5, (2, DI + 2 * DS, DC), 0.1), 'mam_conv_b': jnp.zeros((2, DI + 2 * DS), jnp.float32), 'mam_dt_bias': r(6, (2, NH), 0.1), 'mam_A_log': jnp.zeros((2, NH), jnp.float32), 'mam_D': jnp.ones((2, NH), jnp.float32), 'mam_norm_w': jnp.ones((2, DI), jnp.float32), 'mam_out_w': r(7, (2, DI, DM), 0.05), 'fc_out_w': r(8, (DM, C), 0.05), 'bn_g': jnp.ones((C,), jnp.float32), 'bn_b': jnp.zeros((C,), jnp.float32), 'conv4_w': r(9, (C, C), 0.05), 'conv4_b': jnp.zeros((C,), jnp.float32)}
    _L1_conv_all = _L1_conv_setup()
    _L1_conv_in = {k: v for k, v in _L1_conv_all.items() if k in ('lin1_w', 'lin1_b', 'dw_w', 'dw_b', 'fc_in_w', 'mam_in_w', 'mam_conv_w', 'mam_conv_b', 'mam_dt_bias', 'mam_A_log', 'mam_D', 'mam_norm_w', 'mam_out_w', 'fc_out_w', 'bn_g', 'bn_b', 'conv4_w', 'conv4_b', )}
    del _L1_conv_all

    def _L2_attn_setup():
        import jax, jax.numpy as jnp
        import numpy as np
        NUM_HEADS = 16
        N_QUBITS = 8
        LN_EPS = 1e-05

        def _layernorm(y, g, b):
            m = jnp.mean(y, axis=-1, keepdims=True)
            v = jnp.var(y, axis=-1, keepdims=True)
            return (y - m) * jax.lax.rsqrt(v + LN_EPS) * g + b

        def _quantum_attn(x, theta):
            B, S, E = x.shape
            a = x.reshape(B, S, NUM_HEADS, N_QUBITS) + theta
            cp = jnp.cumprod(jnp.cos(a), axis=-1)
            out = jnp.concatenate([cp[..., -1:], cp[..., 1:]], axis=-1)
            return out.reshape(B, S, E)

        def _quantum_ffn(x, phi):
            return jnp.cos(phi) * jnp.cos(x[..., :N_QUBITS])
        key = jax.random.key(seed)
        ks = jax.random.split(key, 8)
        B, S, E, F = (8, 4096, 128, 2048)
        return {'x': jax.random.normal(ks[0], (B, S, E), dtype=jnp.float32), 'theta_attn': jax.random.normal(ks[1], (N_QUBITS,), dtype=jnp.float32), 'phi_ffn': jax.random.normal(ks[2], (N_QUBITS,), dtype=jnp.float32), 'w1': jax.random.normal(ks[3], (F, N_QUBITS), dtype=jnp.float32) * (1.0 / np.sqrt(N_QUBITS)), 'b1': jax.random.normal(ks[4], (F,), dtype=jnp.float32) * 0.01, 'w2': jax.random.normal(ks[5], (E, F), dtype=jnp.float32) * (1.0 / np.sqrt(F)), 'b2': jax.random.normal(ks[6], (E,), dtype=jnp.float32) * 0.01, 'gamma1': jnp.ones((E,), dtype=jnp.float32), 'beta1': jnp.zeros((E,), dtype=jnp.float32), 'gamma2': jnp.ones((E,), dtype=jnp.float32), 'beta2': jnp.zeros((E,), dtype=jnp.float32)}
    _L2_attn_all = _L2_attn_setup()
    _L2_attn_in = {k: v for k, v in _L2_attn_all.items() if k in ('theta_attn', 'phi_ffn', 'w1', 'b1', 'w2', 'b2', 'gamma1', 'beta1', 'gamma2', 'beta2', )}
    del _L2_attn_all

    def _L2_ffn_setup():
        import jax, jax.numpy as jnp
        import numpy as np
        B, N, D, C, E, K = (8, 8192, 128, 128, 8, 2)
        key = jax.random.key(seed)
        k0, k1, k2 = jax.random.split(key, 3)
        x = jax.random.normal(k0, (B, N, D), dtype=jnp.float32)
        router_w = jax.random.normal(k1, (D, E), dtype=jnp.float32) * 0.05
        router_b = jnp.zeros((E,), dtype=jnp.float32)
        expert_w = jax.random.normal(k2, (E, D, C), dtype=jnp.float32) * (1.0 / np.sqrt(D))
        expert_b = jnp.zeros((E, C), dtype=jnp.float32)
        return {'x': x, 'router_w': router_w, 'router_b': router_b, 'expert_w': expert_w, 'expert_b': expert_b}
    _L2_ffn_all = _L2_ffn_setup()
    _L2_ffn_in = {k: v for k, v in _L2_ffn_all.items() if k in ('router_w', 'router_b', 'expert_w', 'expert_b', )}
    del _L2_ffn_all

    def _L3_attn_setup():
        import jax, jax.numpy as jnp
        import numpy as np
        B, S, H, A = (8, 1024, 128, 16)
        key = jax.random.key(seed)
        ks = jax.random.split(key, 5)
        scale = 1.0 / np.sqrt(2 * H)
        return {'x': jax.random.normal(ks[0], (B, S, H), dtype=jnp.float32), 'W1': jax.random.normal(ks[1], (2 * H, A), dtype=jnp.float32) * scale, 'b1': jax.random.normal(ks[2], (A,), dtype=jnp.float32) * scale, 'w2': jax.random.normal(ks[3], (A, 1), dtype=jnp.float32) * (1.0 / np.sqrt(A)), 'b2': jax.random.normal(ks[4], (1,), dtype=jnp.float32) * (1.0 / np.sqrt(A))}
    _L3_attn_all = _L3_attn_setup()
    _L3_attn_in = {k: v for k, v in _L3_attn_all.items() if k in ('W1', 'b1', 'w2', 'b2', )}
    del _L3_attn_all

    def _L3_ffn_setup():
        import jax, jax.numpy as jnp
        import numpy as np
        B, N, D, C, E, K = (8, 8192, 128, 128, 8, 2)
        key = jax.random.key(seed)
        k0, k1, k2 = jax.random.split(key, 3)
        x = jax.random.normal(k0, (B, N, D), dtype=jnp.float32)
        router_w = jax.random.normal(k1, (D, E), dtype=jnp.float32) * 0.05
        router_b = jnp.zeros((E,), dtype=jnp.float32)
        expert_w = jax.random.normal(k2, (E, D, C), dtype=jnp.float32) * (1.0 / np.sqrt(D))
        expert_b = jnp.zeros((E, C), dtype=jnp.float32)
        return {'x': x, 'router_w': router_w, 'router_b': router_b, 'expert_w': expert_w, 'expert_b': expert_b}
    _L3_ffn_all = _L3_ffn_setup()
    _L3_ffn_in = {k: v for k, v in _L3_ffn_all.items() if k in ('router_w', 'router_b', 'expert_w', 'expert_b', )}
    del _L3_ffn_all

    return {
        "x": x,
        "L0_conv_w_value": _L0_conv_in["w_value"],
        "L0_conv_b_value": _L0_conv_in["b_value"],
        "L0_conv_w_off": _L0_conv_in["w_off"],
        "L0_conv_b_off": _L0_conv_in["b_off"],
        "L0_conv_w_out": _L0_conv_in["w_out"],
        "L0_conv_b_out": _L0_conv_in["b_out"],
        "L0_conv_bn_gamma": _L0_conv_in["bn_gamma"],
        "L0_conv_bn_beta": _L0_conv_in["bn_beta"],
        "L0_conv_bn_mean": _L0_conv_in["bn_mean"],
        "L0_conv_bn_var": _L0_conv_in["bn_var"],
        "L1_conv_lin1_w": _L1_conv_in["lin1_w"],
        "L1_conv_lin1_b": _L1_conv_in["lin1_b"],
        "L1_conv_dw_w": _L1_conv_in["dw_w"],
        "L1_conv_dw_b": _L1_conv_in["dw_b"],
        "L1_conv_fc_in_w": _L1_conv_in["fc_in_w"],
        "L1_conv_mam_in_w": _L1_conv_in["mam_in_w"],
        "L1_conv_mam_conv_w": _L1_conv_in["mam_conv_w"],
        "L1_conv_mam_conv_b": _L1_conv_in["mam_conv_b"],
        "L1_conv_mam_dt_bias": _L1_conv_in["mam_dt_bias"],
        "L1_conv_mam_A_log": _L1_conv_in["mam_A_log"],
        "L1_conv_mam_D": _L1_conv_in["mam_D"],
        "L1_conv_mam_norm_w": _L1_conv_in["mam_norm_w"],
        "L1_conv_mam_out_w": _L1_conv_in["mam_out_w"],
        "L1_conv_fc_out_w": _L1_conv_in["fc_out_w"],
        "L1_conv_bn_g": _L1_conv_in["bn_g"],
        "L1_conv_bn_b": _L1_conv_in["bn_b"],
        "L1_conv_conv4_w": _L1_conv_in["conv4_w"],
        "L1_conv_conv4_b": _L1_conv_in["conv4_b"],
        "L2_attn_theta_attn": _L2_attn_in["theta_attn"],
        "L2_attn_phi_ffn": _L2_attn_in["phi_ffn"],
        "L2_attn_w1": _L2_attn_in["w1"],
        "L2_attn_b1": _L2_attn_in["b1"],
        "L2_attn_w2": _L2_attn_in["w2"],
        "L2_attn_b2": _L2_attn_in["b2"],
        "L2_attn_gamma1": _L2_attn_in["gamma1"],
        "L2_attn_beta1": _L2_attn_in["beta1"],
        "L2_attn_gamma2": _L2_attn_in["gamma2"],
        "L2_attn_beta2": _L2_attn_in["beta2"],
        "L2_ffn_router_w": _L2_ffn_in["router_w"],
        "L2_ffn_router_b": _L2_ffn_in["router_b"],
        "L2_ffn_expert_w": _L2_ffn_in["expert_w"],
        "L2_ffn_expert_b": _L2_ffn_in["expert_b"],
        "L3_attn_W1": _L3_attn_in["W1"],
        "L3_attn_b1": _L3_attn_in["b1"],
        "L3_attn_w2": _L3_attn_in["w2"],
        "L3_attn_b2": _L3_attn_in["b2"],
        "L3_ffn_router_w": _L3_ffn_in["router_w"],
        "L3_ffn_router_b": _L3_ffn_in["router_b"],
        "L3_ffn_expert_w": _L3_ffn_in["expert_w"],
        "L3_ffn_expert_b": _L3_ffn_in["expert_b"],
    }

def reference(x, L0_conv_w_value, L0_conv_b_value, L0_conv_w_off, L0_conv_b_off, L0_conv_w_out, L0_conv_b_out, L0_conv_bn_gamma, L0_conv_bn_beta, L0_conv_bn_mean, L0_conv_bn_var, L1_conv_lin1_w, L1_conv_lin1_b, L1_conv_dw_w, L1_conv_dw_b, L1_conv_fc_in_w, L1_conv_mam_in_w, L1_conv_mam_conv_w, L1_conv_mam_conv_b, L1_conv_mam_dt_bias, L1_conv_mam_A_log, L1_conv_mam_D, L1_conv_mam_norm_w, L1_conv_mam_out_w, L1_conv_fc_out_w, L1_conv_bn_g, L1_conv_bn_b, L1_conv_conv4_w, L1_conv_conv4_b, L2_attn_theta_attn, L2_attn_phi_ffn, L2_attn_w1, L2_attn_b1, L2_attn_w2, L2_attn_b2, L2_attn_gamma1, L2_attn_beta1, L2_attn_gamma2, L2_attn_beta2, L2_ffn_router_w, L2_ffn_router_b, L2_ffn_expert_w, L2_ffn_expert_b, L3_attn_W1, L3_attn_b1, L3_attn_w2, L3_attn_b2, L3_ffn_router_w, L3_ffn_router_b, L3_ffn_expert_w, L3_ffn_expert_b):
    import jax
    import jax.numpy as jnp
    def _L0_conv_ref(x, w_value, b_value, w_off, b_off, w_out, b_out, bn_gamma, bn_beta, bn_mean, bn_var):
        import jax, jax.numpy as jnp
        import numpy as np
        G, KS = (8, 3)
        K = KS * KS
        OM = 32
        EPS = 1e-05

        def _dcnv4(x, w_value, b_value, w_off, b_off, w_out, b_out, bn_gamma, bn_beta, bn_mean, bn_var):
            N, C, H, W = x.shape
            Cg = C // G
            P = H * W
            xf = x.transpose(0, 2, 3, 1).reshape(N, P, C)
            val = xf @ w_value + b_value
            om = (xf @ w_off + b_off).reshape(N, P, G, OM)
            offset = om[..., :2 * K].reshape(N, P, G, K, 2)
            mask = om[..., 2 * K:3 * K]
            py, px = jnp.meshgrid(jnp.arange(H), jnp.arange(W), indexing='ij')
            kk = jnp.arange(KS) - (KS - 1) // 2
            ky, kx = jnp.meshgrid(kk, kk, indexing='ij')
            base_y = (py.reshape(-1)[:, None] + ky.reshape(-1)[None, :]).astype(x.dtype)
            base_x = (px.reshape(-1)[:, None] + kx.reshape(-1)[None, :]).astype(x.dtype)
            sy = base_y[None, :, None, :] + offset[..., 1]
            sx = base_x[None, :, None, :] + offset[..., 0]
            vflat = val.reshape(N, P, G, Cg).transpose(0, 2, 1, 3)

            def gather(iy, ix):
                lin = jnp.clip(iy, 0, H - 1) * W + jnp.clip(ix, 0, W - 1)
                lin = lin.transpose(0, 2, 1, 3).reshape(N, G, P * K)
                g = jnp.take_along_axis(vflat, lin[..., None], axis=2)
                return g.reshape(N, G, P, K, Cg).transpose(0, 2, 1, 3, 4)
            y0 = jnp.floor(sy)
            x0 = jnp.floor(sx)
            ty = sy - y0
            tx = sx - x0
            y0i = y0.astype(jnp.int32)
            x0i = x0.astype(jnp.int32)

            def valid(iy, ix):
                return ((iy >= 0) & (iy < H) & (ix >= 0) & (ix < W)).astype(x.dtype)
            acc = jnp.zeros((N, P, G, K, Cg), x.dtype)
            for dy, dx, wgt in ((0, 0, (1 - ty) * (1 - tx)), (0, 1, (1 - ty) * tx), (1, 0, ty * (1 - tx)), (1, 1, ty * tx)):
                iy, ix = (y0i + dy, x0i + dx)
                acc = acc + gather(iy, ix) * (wgt * valid(iy, ix))[..., None]
            out = (acc * mask[..., None]).sum(axis=3)
            out = out.reshape(N, P, C) @ w_out + b_out
            out = out.reshape(N, H, W, C).transpose(0, 3, 1, 2)
            inv = bn_gamma / jnp.sqrt(bn_var + EPS)
            out = out * inv[None, :, None, None] + (bn_beta - bn_mean * inv)[None, :, None, None]
            return out * jax.nn.sigmoid(out)
        return _dcnv4(x, w_value, b_value, w_off, b_off, w_out, b_out, bn_gamma, bn_beta, bn_mean, bn_var)

    def _L1_conv_ref(x, lin1_w, lin1_b, dw_w, dw_b, fc_in_w, mam_in_w, mam_conv_w, mam_conv_b, mam_dt_bias, mam_A_log, mam_D, mam_norm_w, mam_out_w, fc_out_w, bn_g, bn_b, conv4_w, conv4_b):
        import jax, jax.numpy as jnp
        import numpy as np
        from jax import lax
        B, C, H, W = (8, 128, 64, 64)
        L = H * W
        DM, DI, DS, DC, NH, HD = (32, 64, 64, 4, 1, 64)

        def _causal_dwconv1d(x, w, b):
            xc = jnp.transpose(x, (0, 2, 1))
            xc = jnp.pad(xc, ((0, 0), (0, 0), (DC - 1, 0)))
            o = lax.conv_general_dilated(xc, w[:, None, :], (1,), 'VALID', feature_group_count=w.shape[0], dimension_numbers=('NCH', 'OIH', 'NCH'))
            return jnp.transpose(o + b[None, :, None], (0, 2, 1))

        def _mamba2(u, W_in, conv_w, conv_b, dt_bias, A_log, D, norm_w, W_out):
            b, l, _ = u.shape
            zxbcdt = u @ W_in
            z = zxbcdt[..., :DI]
            xBC = zxbcdt[..., DI:DI + DI + 2 * DS]
            dt = zxbcdt[..., -NH:]
            xBC = jax.nn.silu(_causal_dwconv1d(xBC, conv_w, conv_b))
            xs = xBC[..., :DI]
            Bm = xBC[..., DI:DI + DS]
            Cm = xBC[..., DI + DS:]
            dt = jax.nn.softplus(dt + dt_bias)
            dA = jnp.exp(dt * -jnp.exp(A_log))
            xh = xs.reshape(b, l, NH, HD)
            dtx = dt[..., None] * xh

            def step(h, inp):
                dA_t, dtx_t, B_t, C_t = inp
                h = dA_t[:, :, None, None] * h + dtx_t[..., None] * B_t[:, None, None, :]
                y = jnp.einsum('bhpn,bn->bhp', h, C_t)
                return (h, y)
            h0 = jnp.zeros((b, NH, HD, DS), u.dtype)
            _, ys = lax.scan(step, h0, (jnp.moveaxis(dA, 1, 0), jnp.moveaxis(dtx, 1, 0), jnp.moveaxis(Bm, 1, 0), jnp.moveaxis(Cm, 1, 0)))
            y = jnp.moveaxis(ys, 0, 1) + D[None, None, :, None] * xh
            y = y.reshape(b, l, DI)
            y = y * jax.nn.silu(z)
            y = y * lax.rsqrt(jnp.mean(y * y, -1, keepdims=True) + 1e-05) * norm_w
            return y @ W_out

        def _forward(x, lin1_w, lin1_b, dw_w, dw_b, fc_in_w, mam_in_w, mam_conv_w, mam_conv_b, mam_dt_bias, mam_A_log, mam_D, mam_norm_w, mam_out_w, fc_out_w, bn_g, bn_b, conv4_w, conv4_b):
            b, c, h, w = x.shape
            o = jnp.einsum('bihw,io->bohw', x, lin1_w) + lin1_b[None, :, None, None]
            o = lax.conv_general_dilated(o, dw_w, (1, 1), 'SAME', feature_group_count=c, dimension_numbers=('NCHW', 'OIHW', 'NCHW')) + dw_b[None, :, None, None]
            o = jax.nn.silu(o)
            s = jnp.einsum('bcl,cd->bld', o.reshape(b, c, h * w), fc_in_w)
            y1 = _mamba2(s, mam_in_w[0], mam_conv_w[0], mam_conv_b[0], mam_dt_bias[0], mam_A_log[0], mam_D[0], mam_norm_w[0], mam_out_w[0])
            y2 = jnp.flip(_mamba2(jnp.flip(s, 1), mam_in_w[1], mam_conv_w[1], mam_conv_b[1], mam_dt_bias[1], mam_A_log[1], mam_D[1], mam_norm_w[1], mam_out_w[1]), 1)
            o = jnp.transpose((y1 + y2) @ fc_out_w, (0, 2, 1)).reshape(b, c, h, w)
            mu = jnp.mean(o, (0, 2, 3), keepdims=True)
            var = jnp.mean((o - mu) ** 2, (0, 2, 3), keepdims=True)
            o = (o - mu) * lax.rsqrt(var + 1e-05) * bn_g[None, :, None, None] + bn_b[None, :, None, None]
            g = jax.nn.sigmoid(jnp.einsum('bihw,io->bohw', o, conv4_w) + conv4_b[None, :, None, None])
            return g * x + x
        return _forward(x, lin1_w, lin1_b, dw_w, dw_b, fc_in_w, mam_in_w, mam_conv_w, mam_conv_b, mam_dt_bias, mam_A_log, mam_D, mam_norm_w, mam_out_w, fc_out_w, bn_g, bn_b, conv4_w, conv4_b)

    def _L2_attn_ref(x, theta_attn, phi_ffn, w1, b1, w2, b2, gamma1, beta1, gamma2, beta2):
        import jax, jax.numpy as jnp
        import numpy as np
        NUM_HEADS = 16
        N_QUBITS = 8
        LN_EPS = 1e-05

        def _layernorm(y, g, b):
            m = jnp.mean(y, axis=-1, keepdims=True)
            v = jnp.var(y, axis=-1, keepdims=True)
            return (y - m) * jax.lax.rsqrt(v + LN_EPS) * g + b

        def _quantum_attn(x, theta):
            B, S, E = x.shape
            a = x.reshape(B, S, NUM_HEADS, N_QUBITS) + theta
            cp = jnp.cumprod(jnp.cos(a), axis=-1)
            out = jnp.concatenate([cp[..., -1:], cp[..., 1:]], axis=-1)
            return out.reshape(B, S, E)

        def _quantum_ffn(x, phi):
            return jnp.cos(phi) * jnp.cos(x[..., :N_QUBITS])
        attn = _quantum_attn(x, theta_attn)
        x1 = _layernorm(x + attn, gamma1, beta1)
        q = _quantum_ffn(x1, phi_ffn)
        h = jax.nn.relu(jnp.einsum('bsq,fq->bsf', q, w1) + b1)
        ffn = jnp.einsum('bsf,ef->bse', h, w2) + b2
        return _layernorm(x1 + ffn, gamma2, beta2)

    def _L2_ffn_ref(x, router_w, router_b, expert_w, expert_b):
        import jax, jax.numpy as jnp
        import numpy as np
        B, N, D, C, E, K = (8, 8192, 128, 128, 8, 2)
        router_probs = jax.nn.softmax(x @ router_w + router_b, axis=-1)
        top_p, top_i = jax.lax.top_k(router_probs, K)
        top_p = top_p / jnp.sum(top_p, axis=-1, keepdims=True)
        expert_out = jnp.einsum('bnd,edc->bnec', x, expert_w) + expert_b
        gathered = jnp.take_along_axis(expert_out, top_i[..., None], axis=2)
        return jnp.einsum('bnk,bnkc->bnc', top_p, gathered)

    def _L3_attn_ref(x, W1, b1, w2, b2):
        import jax, jax.numpy as jnp
        import numpy as np
        B, S, H, A = (8, 1024, 128, 16)
        h = x.shape[-1]
        f = jnp.einsum('bih,ha->bia', x, W1[:h])
        g = jnp.einsum('bjh,ha->bja', x, W1[h:])
        t = jnp.tanh(f[:, :, None, :] + g[:, None, :, :] + b1)
        scores = jnp.einsum('bija,a->bij', t, w2[:, 0]) + b2[0]
        n_seq = x.shape[1]
        flag = jnp.tril(jnp.ones((n_seq, n_seq), dtype=x.dtype), -1)[None, :, :]
        e = jnp.exp(scores) * flag
        denom = jnp.sum(e, axis=-1, keepdims=True) + 1e-10
        w = e / denom
        return jnp.einsum('bij,bjh->bih', w, x)

    def _L3_ffn_ref(x, router_w, router_b, expert_w, expert_b):
        import jax, jax.numpy as jnp
        import numpy as np
        B, N, D, C, E, K = (8, 8192, 128, 128, 8, 2)
        router_probs = jax.nn.softmax(x @ router_w + router_b, axis=-1)
        top_p, top_i = jax.lax.top_k(router_probs, K)
        top_p = top_p / jnp.sum(top_p, axis=-1, keepdims=True)
        expert_out = jnp.einsum('bnd,edc->bnec', x, expert_w) + expert_b
        gathered = jnp.take_along_axis(expert_out, top_i[..., None], axis=2)
        return jnp.einsum('bnk,bnkc->bnc', top_p, gathered)

    def _gn(v, G=32, eps=1e-5):
        B_, C_, H_, W_ = v.shape
        g = v.reshape(B_, G, C_ // G, H_, W_)
        m = jnp.mean(g, axis=(2, 3, 4), keepdims=True)
        s = jnp.var(g, axis=(2, 3, 4), keepdims=True)
        return ((g - m) / jnp.sqrt(s + eps)).reshape(v.shape)

    def _ln_c(v, eps=1e-6):
        m = jnp.mean(v, axis=1, keepdims=True)
        s = jnp.var(v, axis=1, keepdims=True)
        return (v - m) / jnp.sqrt(s + eps)

    def _ln_t(v, eps=1e-5):
        m = jnp.mean(v, axis=-1, keepdims=True)
        s = jnp.var(v, axis=-1, keepdims=True)
        return (v - m) / jnp.sqrt(s + eps)

    def _to_tokens(v):
        B_, C_, H_, W_ = v.shape
        return v.reshape(B_, C_, H_ * W_).transpose(0, 2, 1)
    def _from_tokens(t, like):
        B_, C_, H_, W_ = like.shape
        return t.transpose(0, 2, 1).reshape(B_, C_, H_, W_)

    x = x + _L0_conv_ref(_gn(x), L0_conv_w_value, L0_conv_b_value, L0_conv_w_off, L0_conv_b_off, L0_conv_w_out, L0_conv_b_out, L0_conv_bn_gamma, L0_conv_bn_beta, L0_conv_bn_mean, L0_conv_bn_var)
    x = _L1_conv_ref(x, L1_conv_lin1_w, L1_conv_lin1_b, L1_conv_dw_w, L1_conv_dw_b, L1_conv_fc_in_w, L1_conv_mam_in_w, L1_conv_mam_conv_w, L1_conv_mam_conv_b, L1_conv_mam_dt_bias, L1_conv_mam_A_log, L1_conv_mam_D, L1_conv_mam_norm_w, L1_conv_mam_out_w, L1_conv_fc_out_w, L1_conv_bn_g, L1_conv_bn_b, L1_conv_conv4_w, L1_conv_conv4_b)
    t = _to_tokens(x)
    t = t + _L2_attn_ref(_ln_t(t), L2_attn_theta_attn, L2_attn_phi_ffn, L2_attn_w1, L2_attn_b1, L2_attn_w2, L2_attn_b2, L2_attn_gamma1, L2_attn_beta1, L2_attn_gamma2, L2_attn_beta2)
    t = t + _L2_ffn_ref(_ln_t(t), L2_ffn_router_w, L2_ffn_router_b, L2_ffn_expert_w, L2_ffn_expert_b)
    t = t + _L3_attn_ref(_ln_t(t), L3_attn_W1, L3_attn_b1, L3_attn_w2, L3_attn_b2)
    t = t + _L3_ffn_ref(_ln_t(t), L3_ffn_router_w, L3_ffn_router_b, L3_ffn_expert_w, L3_ffn_expert_b)
    x = _from_tokens(t, x)
    return x


_drawn_inputs = setup_inputs


def setup_inputs(seed=0):
    import zlib

    import numpy as np

    out = dict(_drawn_inputs(seed))
    spreads = {'L1_conv_lin1_b': (0.0, 0.385),
     'L1_conv_dw_b': (0.0, 0.1),
     'L1_conv_mam_conv_b': (0.0, 0.1),
     'L1_conv_mam_A_log': (0.0, 0.8),
     'L1_conv_mam_D': (1.0, 0.6),
     'L1_conv_mam_norm_w': (1.0, 0.2),
     'L1_conv_bn_g': (1.0, 0.2),
     'L1_conv_bn_b': (0.0, 0.1),
     'L1_conv_conv4_b': (0.0, 0.1),
     'L2_attn_gamma1': (1.0, 0.2),
     'L2_attn_beta1': (0.0, 0.1),
     'L2_attn_gamma2': (1.0, 0.2),
     'L2_attn_beta2': (0.0, 0.1),
     'L2_ffn_router_b': (0.0, 0.1),
     'L2_ffn_expert_b': (0.0, 0.1),
     'L3_ffn_router_b': (0.0, 0.1),
     'L3_ffn_expert_b': (0.0, 0.319)}
    factors = {'L0_conv_b_value': 3.206,
     'L1_conv_mam_conv_w': 3.269,
     'L1_conv_mam_dt_bias': 8.0,
     'L2_attn_b1': 3.1,
     'L3_attn_b1': 8.0}
    for name, (base, spread) in spreads.items():
        noise = np.random.default_rng([zlib.crc32(name.encode()), seed]).standard_normal(out[name].shape)
        drawn = base * np.exp(spread * noise) if base else spread * noise
        out[name] = jnp.asarray(drawn.astype(out[name].dtype))
    for name, factor in factors.items():
        out[name] = (out[name] * factor).astype(out[name].dtype)
    return out
```

```python
from contextlib import ExitStack, contextmanager

import numpy as np
import concourse.bass as bass
from concourse import mybir

F32 = mybir.dt.float32
BF16 = mybir.dt.bfloat16
I32 = mybir.dt.int32
ACT = mybir.ActivationFunctionType
ALU = mybir.AluOpType
AX = mybir.AxisListType

P = 128
NB, HH, WW = 4, 64, 64
L = HH * WW
NT = L // P
BANK = 512
NEG = -1.0e30
G, K, OM = 8, 9, 32
REACH = HH - 1
NEAR = 3
NS = 2 * REACH + 1


def constants():
    p = np.arange(P)
    y_of = p // WW
    j = np.arange(NS + 2 * NT - 1)
    d = np.arange(NS) - REACH
    parts = {}
    parts["ident"] = np.eye(P)
    parts["gavg"] = (p[:, None] // 4 == p[None, :] // 4) * 0.25
    vx = ((p[:, None] % WW + d >= 0) & (p[:, None] % WW + d < WW)) * 1.0
    parts["vx"], parts["nvx"] = vx, -vx
    vy = y_of[:, None] + j[None, :] - REACH
    parts["vy"] = ((vy >= 0) & (vy < HH)) * 1.0
    parts["negd"] = np.broadcast_to(-d, (P, NS))
    c = np.arange(G * OM)
    k = (c % OM) // 2
    parts["koff"] = np.broadcast_to(np.where(c % OM < 2 * K, np.where(c % 2 == 0, k % 3 - 1, k // 3 - 1), 0), (P, G * OM))
    before = p[:, None] <= p[None, :]
    parts["tri_f"], parts["tri_b"] = before * 1.0, before.T * 1.0
    parts["neg_f"], parts["neg_b"] = np.where(before, 0, NEG), np.where(before.T, 0, NEG)
    parts["strict"] = (p[:, None] < p[None, :]) * 1.0
    parts["first"] = np.broadcast_to(8 - np.arange(8), (P, 8))
    w = np.arange(P)
    parts["pick"] = w[None, :] % 32 == (w[None, :] // 32) * 8 + p[:, None] // 16
    parts["eps5"] = np.full((P, 1), 1e-5)
    parts["quad"] = p[:, None] // 32 == np.arange(NB)
    return {n: np.asarray(a, np.float32) for n, a in parts.items()}


@contextmanager
def stage_semaphores(nc, tag):
    used = []

    def sem(name):
        used.append(nc.alloc_semaphore(tag + name))
        return used[-1]

    yield sem
    nc.clear_and_free_semaphores(used)
    nc.all_engine_barrier()


class Chain:

    def __init__(self, eng, sem, base=0):
        self.eng, self.sem, self.base, self.n = eng, sem, base, 0

    def __call__(self, ins):
        ins.then_inc(self.sem, 1)
        self.n += 1
        self.eng.wait_ge(self.sem, self.base + self.n)


def deform_layer(nc, d, X, C, near, far_flag):
    tag = "near_" if near else "wide_"
    D0, D1 = (REACH - NEAR, REACH + NEAR + 1) if near else (0, NS)
    ND = D1 - D0
    UT = NT // 2
    UN = UT * P
    GK = G * K
    with stage_semaphores(nc, tag) as sem, ExitStack() as ctx:
        def sb(name, shape, dt=F32):
            return ctx.enter_context(nc.sbuf_tensor(tag + name, shape, dt))

        VP = sb("values_padded", [P, 3 * L])
        XN = sb("x_normed", [P, L])
        OMT = sb("offsets_masks", [P, NT * G * OM])
        om3 = OMT[:, :].rearrange("p (t c) -> p t c", t=NT)
        AY = sb("abs_y", [P, UT, G, K])
        HY = sb("hat_y", [P, UT, G, K])
        HYM = sb("hat_y_mask_valid", [P, UT, G, K])
        AXX = sb("abs_x", [P, UT, G, K])
        HX = sb("hat_x", [P, UT, G, K])
        PP = sb("tap_weights", [P, UT * G, K])
        HYP = PP[:, :, :].rearrange("p (t g) k -> p t g k", t=UT)
        W = sb("shift_weights", [P, UT * G])
        PR = sb("weighted_values", [P, UN])
        YB, SG = PR, XN[:, 0:UN]
        WW16 = XN[:, UN:2 * UN]
        WV, WO, WF = sb("w_value", [P, P]), sb("w_out", [P, P]), sb("w_off", [P, G * OM])
        BOFF = sb("b_off", [P, G * OM])
        COL = sb("columns", [P, 6])
        INV = sb("bn_scale", [P, 1])
        BB = sb("bn_shift", [P, 1])
        T1 = sb("t1", [P, 1])
        ST = sb("stats", [P, 8, 6])
        MV = sb("mean_var", [P, 2])
        RH = sb("group_in", [P, 2])
        MG = sb("group_mean", [P, 2])
        MM = sb("group_mean2", [P, 1])
        VE = sb("group_var", [P, 1])
        SD = sb("group_std", [P, 1])
        RS = sb("group_rstd", [P, 1])
        NBI = sb("group_shift", [P, 1])
        RMX = sb("reach_by_image", [P, NB])
        RM1 = sb("reach", [P, 1])
        RMA = sb("reach_all", [P, 1])
        ZR = sb("zeros", [P, BANK], BF16)
        wp = ctx.enter_context(nc.psum_tensor(tag + "weights_spread", [P, UN], F32))
        acc = ctx.enter_context(nc.psum_tensor(tag + "out_sum", [P, UN], F32))

        loaded, cleared, bn_ready = sem("loaded"), sem("cleared"), sem("bn_ready")
        rh_ready, gst_ready, ve_ready, sd_ready = sem("rh_ready"), sem("gst_ready"), sem("ve_ready"), sem("sd_ready")
        xn_ready, val_ready, val_stored = sem("xn_ready"), sem("val_ready"), sem("val_stored")
        offs_ready, om_stored, om_ready = sem("offs_ready"), sem("om_stored"), sem("om_ready")
        ay_ready, hy_ready, hyp_ready, hym_ready = sem("ay_ready"), sem("hy_ready"), sem("hyp_ready"), sem("hym_ready")
        ax_ready, hx_ready, pp_ready, w_ready = sem("ax_ready"), sem("hx_ready"), sem("pp_ready"), sem("w_ready")
        wide_ready = sem("wide_ready")
        spread, prod_ready, mm_done, unit_done = sem("spread"), sem("prod_ready"), sem("mm_done"), sem("unit_done")
        y_ready, sig_ready, ys_ready, x_done = sem("y_ready"), sem("sig_ready"), sem("ys_ready"), sem("x_done")
        prep, flag_sem = sem("vector_prep"), sem("flag")
        sq_ready, reach_ready = sem("sq_ready"), sem("reach_ready")
        block = ctx.enter_context(nc.Block())

        cols = ("b_value", "b_out", "bn_gamma", "bn_beta", "bn_mean", "bn_var")
        n_loads = 1 + 4 + len(cols) + (1 if near else 0)

        @block.sync
        def _(sp):
            sp.dma_start(X[:, :].rearrange("p (b n) -> p b n", b=NB), d["x"].rearrange("b c h w -> c b (h w)")).then_inc(loaded, 16)
            sp.dma_start(WV[:, :], d["L0_conv_w_value"]).then_inc(loaded, 16)
            sp.dma_start(WO[:, :], d["L0_conv_w_out"]).then_inc(loaded, 16)
            sp.dma_start(WF[:, :], d["L0_conv_w_off"]).then_inc(loaded, 16)
            sp.dma_start(BOFF[:, :], d["L0_conv_b_off"].partition_broadcast(P)).then_inc(loaded, 16)
            for i, n in enumerate(cols):
                sp.dma_start(COL[:, i:i + 1], d["L0_conv_" + n].rearrange("(c a) -> c a", a=1)).then_inc(loaded, 16)
            if near:
                sp.dma_start(C["all"], d["consts"]).then_inc(loaded, 16)
            sp.wait_ge(loaded, 16 * n_loads)

        @block.gpsimd
        def _(pool):
            pool.memset(VP[:, 0:L], 0.0).then_inc(cleared, 1)
            pool.memset(VP[:, 2 * L:3 * L], 0.0).then_inc(cleared, 1)
            pool.memset(ZR[:, :], 0.0).then_inc(cleared, 1)
            if near:
                pool.wait_ge(reach_ready, 1)
                pool.partition_all_reduce(RMA[:, :], RM1[:, :], P, bass.bass_isa.ReduceOp.max).then_inc(flag_sem, 1)

        @block.vector
        def _(v):
            v.wait_ge(loaded, 16 * n_loads)
            v.wait_ge(cleared, 3)
            one = Chain(v, bn_ready)
            v.tensor_tensor(BOFF[:, :], BOFF[:, :], C["koff"], ALU.add).then_inc(prep, 1)
            one(v.tensor_scalar(T1[:, :], COL[:, 5:6], 1e-5, None, ALU.add))
            v.wait_ge(sq_ready, 1)
            one(v.reciprocal(INV[:, :], SD[:, :]))
            one(v.tensor_tensor(INV[:, :], INV[:, :], COL[:, 2:3], ALU.mult))
            one(v.tensor_tensor(BB[:, :], COL[:, 1:2], COL[:, 4:5], ALU.subtract))
            one(v.scalar_tensor_tensor(BB[:, :], BB[:, :], INV[:, 0:1], COL[:, 3:4], ALU.mult, ALU.add))
            KP = 7
            with v.Fori(0, NB) as b:
                ch = Chain(v, prep, b * KP + 1)
                for i in range(8):
                    last = v.bn_stats(ST[:, i, :], X[:, bass.ds(b * L + i * BANK, BANK)])
                ch(last)
                v.tensor_copy(VE[:, :], T1[:, :])
                ch(v.bn_aggr(MV[:, :], ST[:, :, :].rearrange("p a s -> p (a s)")))
                v.tensor_copy(RH[:, 0:1], MV[:, 0:1])
                v.scalar_tensor_tensor(RH[:, 1:2], MV[:, 0:1], MV[:, 0:1], MV[:, 1:2], ALU.mult, ALU.add).then_inc(rh_ready, 1)
                v.wait_ge(gst_ready, b + 1)
                ch(v.tensor_copy(MG[:, :], wp[:, 0:2]))
                ch(v.tensor_tensor(MM[:, :], MG[:, 0:1], MG[:, 0:1], ALU.mult))
                v.scalar_tensor_tensor(VE[:, :], MG[:, 1:2], 1e-5, MM[:, :], ALU.add, ALU.subtract).then_inc(ve_ready, 1)
                v.wait_ge(sd_ready, b + 1)
                ch(v.reciprocal(RS[:, :], SD[:, :]))
                ch(v.scalar_tensor_tensor(NBI[:, :], MG[:, 0:1], -1.0, RS[:, :], ALU.mult, ALU.mult))
                v.tensor_scalar(XN[:, :], X[:, bass.ds(b * L, L)], RS[:, 0:1], NBI[:, 0:1], ALU.mult, ALU.add).then_inc(xn_ready, 1)
                for j in range(16):
                    v.wait_ge(offs_ready, b * 16 + j + 1)
                    v.tensor_tensor(om3[:, 2 * j:2 * j + 2, :], acc[:, (j % 4) * BANK:(j % 4 + 1) * BANK].rearrange("p (t c) -> p t c", t=2),
                                    BOFF[:, :].unsqueeze(1).to_broadcast([P, 2, G * OM]), ALU.add).then_inc(om_stored, 1)
                v.wait_ge(om_stored, b * 16 + 16)
                ch(v.tensor_reduce(RMX[:, bass.ds(b, 1)], OMT[:, :].rearrange("p (a c) -> p a c", c=OM)[:, :, 0:2 * K], AX.XY, ALU.max,
                                   apply_absolute_value=True))
                v.sem_inc(om_ready, 1)
                assert ch.n == KP
                with v.Fori(0, 2) as u:
                    U = b * 2 + u
                    with v.Fori(D0, D1) as dy:
                        DD = U * ND + dy - D0
                        v.wait_ge(val_stored, b * 8 + 8)
                        v.wait_ge(hy_ready, DD + 1)
                        v.tensor_tensor(HYP[:, :, :, :], HY[:, :, :, :], OMT[:, bass.ds(u * UT * G * OM, UT * G * OM)].rearrange("p (t g c) -> p t g c", t=UT, g=G)[:, :, :, 2 * K:3 * K], ALU.mult).then_inc(hyp_ready, 1)
                        v.wait_ge(hyp_ready, DD + 1)
                        v.tensor_tensor(HYM[:, :, :, :].rearrange("p t g k -> p t (g k)"), HYP[:, :, :, :].rearrange("p t g k -> p t (g k)"),
                                        C["vy"][:, bass.ds(u * 2 * UT + dy, 2 * UT)].rearrange("p (t two) -> p t two", two=2)[:, :, 0:1].to_broadcast([P, UT, GK]), ALU.mult).then_inc(hym_ready, 1)
                        with v.Fori(D0, D1) as dx:
                            v.wait_ge(hym_ready, DD + 1)
                            S = DD * ND + dx - D0
                            v.wait_ge(hx_ready, S + 1)
                            v.tensor_tensor(PP[:, :, :].rearrange("p a k -> p (a k)"), HYM[:, :, :, :].rearrange("p t g k -> p (t g k)"), HX[:, :, :, :].rearrange("p t g k -> p (t g k)"), ALU.mult).then_inc(pp_ready, 1)
                            v.wait_ge(pp_ready, S + 1)
                            v.wait_ge(wide_ready, S * 2)
                            v.tensor_reduce(W[:, :], PP[:, :, :], AX.X, ALU.add).then_inc(w_ready, 1)
                            for h in range(2):
                                v.wait_ge(spread, S * 2 + h + 1)
                                v.wait_ge(mm_done, S * 2 + h + 1)
                                v.tensor_tensor(PR[:, h * UN // 2:(h + 1) * UN // 2], wp[:, h * UN // 2:(h + 1) * UN // 2],
                                                VP[:, bass.ds(u * UN + dy * WW + dx + (L + h * UN // 2 - REACH * WW - REACH), UN // 2)], ALU.mult).then_inc(prod_ready, 1)
                    v.wait_ge(sig_ready, U + 1)
                    v.tensor_tensor(YB[:, :], YB[:, :], SG, ALU.mult).then_inc(ys_ready, 1)
                    v.wait_ge(ys_ready, U + 1)
                    v.tensor_tensor(X[:, bass.ds(b * L + u * UN, UN)], X[:, bass.ds(b * L + u * UN, UN)], YB[:, :], ALU.add).then_inc(x_done, 1)
            if near:
                end = Chain(v, sem("vector_end"))
                end(v.tensor_reduce(RM1[:, :], RMX[:, :], AX.X, ALU.max))
                v.sem_inc(reach_ready, 1)
                v.wait_ge(flag_sem, 1)
                end(v.tensor_scalar(RM1[:, :], RMA[:, :], float(NEAR), None, ALU.is_gt))
                end(v.tensor_copy(far_flag, RM1[:, :]))

        @block.scalar
        def _(a):
            a.wait_ge(bn_ready, 1)
            a.activation(SD[:, :], T1[:, :], ACT.Sqrt).then_inc(sq_ready, 1)
            a.wait_ge(bn_ready, 5)
            with a.Fori(0, NB) as b:
                a.wait_ge(ve_ready, b + 1)
                a.activation(SD[:, :], VE[:, :], ACT.Sqrt).then_inc(sd_ready, 1)
                for j in range(8):
                    a.wait_ge(val_ready, b * 8 + j + 1)
                    a.activation(VP[:, L + j * BANK:L + (j + 1) * BANK], wp[:, (j % 4) * BANK:(j % 4 + 1) * BANK], ACT.Identity, bias=COL[:, 0:1]).then_inc(val_stored, 1)
                a.wait_ge(om_ready, b + 1)
                with a.Fori(0, 2) as u:
                    U = b * 2 + u
                    taps = OMT[:, bass.ds(u * UT * G * OM, UT * G * OM)].rearrange("p (a c) -> p a c", c=OM)
                    with a.Fori(D0, D1) as dy:
                        DD = U * ND + dy - D0
                        a.activation(AY[:, :, :, :].rearrange("p t g k -> p (t g) k"), taps[:, :, 1:2 * K:2], ACT.Abs, bias=C["negd"][:, bass.ds(dy, 1)]).then_inc(ay_ready, 1)
                        a.wait_ge(ay_ready, DD + 1)
                        a.wait_ge(hyp_ready, DD)
                        a.activation(HY[:, :, :, :], AY[:, :, :, :], ACT.Relu, bias=1.0, scale=-1.0).then_inc(hy_ready, 1)
                        with a.Fori(D0, D1) as dx:
                            S = DD * ND + dx - D0
                            a.activation(AXX[:, :, :, :].rearrange("p t g k -> p (t g) k"), taps[:, :, 0:2 * K:2], ACT.Abs, bias=C["negd"][:, bass.ds(dx, 1)]).then_inc(ax_ready, 1)
                            a.wait_ge(ax_ready, S + 1)
                            a.wait_ge(pp_ready, S)
                            a.activation(HX[:, :, :, :], AXX[:, :, :, :], ACT.Relu, bias=C["vx"][:, bass.ds(dx, 1)], scale=C["nvx"][:, bass.ds(dx, 1)]).then_inc(hx_ready, 1)
                            a.wait_ge(w_ready, S + 1)
                            a.wait_ge(spread, S * 2)
                            for h in range(2):
                                a.activation(WW16[:, h * UN // 2:(h + 1) * UN // 2].rearrange("p (a r) -> p a r", r=P // G),
                                             W[:, h * P // 2:(h + 1) * P // 2].unsqueeze(2).to_broadcast([P, P // 2, P // G]), ACT.Copy).then_inc(wide_ready, 1)
                    a.wait_ge(unit_done, U + 1)
                    a.wait_ge(x_done, U)
                    a.activation(YB[:, :], acc[:, :], ACT.Identity, bias=BB[:, 0:1], scale=INV[:, 0:1]).then_inc(y_ready, 1)
                    a.wait_ge(y_ready, U + 1)
                    a.activation(SG, YB[:, :], ACT.Sigmoid).then_inc(sig_ready, 1)

        @block.tensor
        def _(t):
            t.wait_ge(loaded, 16 * n_loads)
            t.wait_ge(cleared, 3)
            t.sem_inc(mm_done, 2)
            with t.Fori(0, NB) as b:
                t.wait_ge(rh_ready, b + 1)
                t.wait_ge(prod_ready, b * (4 * ND * ND))
                t.matmul(wp[:, 0:2], C["gavg"], RH[:, :], start=True, stop=True).then_inc(gst_ready, 1)
                t.wait_ge(xn_ready, b + 1)
                for j in range(8):
                    if j >= 4:
                        t.wait_ge(val_stored, b * 8 + j - 3)
                    t.matmul(wp[:, (j % 4) * BANK:(j % 4 + 1) * BANK], WV[:, :], XN[:, j * BANK:(j + 1) * BANK], start=True, stop=True).then_inc(val_ready, 1)
                t.wait_ge(y_ready, b * 2)
                for j in range(16):
                    if j >= 4:
                        t.wait_ge(om_stored, b * 16 + j - 3)
                    for i in range(2):
                        last = t.matmul(acc[:, (j % 4) * BANK + i * G * OM:(j % 4) * BANK + (i + 1) * G * OM], XN[:, (2 * j + i) * P:(2 * j + i + 1) * P], WF[:, :], start=True, stop=True)
                    last.then_inc(offs_ready, 1)
                with t.Fori(0, 2) as u:
                    U = b * 2 + u
                    t.wait_ge(om_stored, b * 16 + 16)
                    t.wait_ge(val_stored, b * 8 + 8)
                    t.wait_ge(y_ready, U)
                    for q in range(4):
                        t.matmul(acc[:, q * BANK:(q + 1) * BANK], ZR[:, 0:P], ZR[:, :], start=True, stop=False)
                    with t.Fori(D0, D1) as dy:
                        with t.Fori(D0, D1) as dx:
                            S = (U * ND + dy - D0) * ND + dx - D0
                            t.wait_ge(prod_ready, S * 2)
                            for i in range(UT):
                                if i % (UT // 2) == 0:
                                    t.wait_ge(wide_ready, S * 2 + 1 + i // (UT // 2))
                                last = t.transpose(wp[:, i * P:(i + 1) * P], WW16[:, i * P:(i + 1) * P], C["ident"])
                                if i % (UT // 2) == UT // 2 - 1:
                                    last.then_inc(spread, 1)
                            for h in range(2):
                                t.wait_ge(prod_ready, S * 2 + h + 1)
                                for q in range(2 * h, 2 * h + 2):
                                    last = t.matmul(acc[:, q * BANK:(q + 1) * BANK], WO[:, :], PR[:, q * BANK:(q + 1) * BANK], start=False, stop=False)
                                last.then_inc(mm_done, 1)
                    for q in range(4):
                        last = t.matmul(acc[:, q * BANK:(q + 1) * BANK], ZR[:, 0:P], ZR[:, :], start=False, stop=True)
                    last.then_inc(unit_done, 1)


DM, DI, DC = 32, 64, 4
ZW = 4 * DI
XO, BO, CO, ZO = 0, DI, 2 * DI, 3 * DI
NC = NT


def mamba_layer(nc, d, X, C):
    with stage_semaphores(nc, "l1_") as sem, ExitStack() as ctx:
        def sb(name, shape, dt=F32):
            return ctx.enter_context(nc.sbuf_tensor("l1_" + name, shape, dt))

        WP = WW + 2
        O1 = sb("lin1_padded", [P, (HH + 2) * WP])
        O1v = O1[:, :].rearrange("p (h w) -> p h w", w=WP)
        O2 = sb("conv_silu", [P, L])
        S4 = [sb("rows_fwd", [P, L + DC - 1]), sb("rows_bwd", [P, L + DC - 1])]
        S0 = [0, DC - 1]
        YST = O1[:, 0:L]
        YT = O2
        S2 = sb("scan_out", [P, L])
        LW, W4, FO = sb("lin1_w", [P, P]), sb("conv4_w", [P, P]), sb("fc_out_by_image", [P, NB, P])
        DG = sb("dw_diag", [P, 9, P])
        DW = sb("dw_w", [P, 9])
        FI = sb("fc_in_4", [P, DC, DM])
        WA = [sb("w_in_f", [P, ZW + 1]), sb("w_in_b", [P, ZW + 1])]
        CW = sb("conv_w", [P, 2, (ZW - DI) * DC])
        BI = sb("bias_rows", [P, 2, ZW])
        WOU = sb("w_out_4", [P, 4, DM])
        VEC = sb("vec", [P, 12])
        HB = sb("half_dw_b", [P, 1])
        NEA = sb("minus_exp_A", [P, 2])
        THB, VH = sb("tanh_rows", [P, 2, BANK]), sb("half_rows", [P, 2, BANK])
        DX, DE, DT, AV, NCS = (sb(n, [P, 2 * NC]) for n in ("dt_raw", "dt_exp", "dt", "decay_log", "minus_decay_sum"))
        LH, AB, XH, TH, ZS = (sb(n, [P, 2, w]) for n, w in (("rows_chunk", P), ("decay_wide", P), ("half_zxbc", ZW), ("tanh_zxbc", ZW), ("zxbc", ZW)))
        BT, CT, ECS, CE, HST = (sb(n, [DI, 2, w]) for n, w in (("B_T", P), ("C_T", P), ("decay_in", P), ("C_decayed", P), ("state", DI)))
        TM, LT, GL = (sb(n, [P, 2, P]) for n in ("decay_masked", "decay", "CB_decay"))
        BD, Y1 = sb("B_decayed", [P, 2, DI]), sb("y_plus_Dx", [P, 2, DI])
        MSQ, RST = sb("mean_square", [P, 2 * NC]), sb("rms_inv", [P, 2 * NC])
        ST = sb("stats", [P, NB * 8, 6])
        MV, SC, SH, RV = sb("bn_mean_var", [P, 2]), sb("bn_scale", [P, 1]), sb("bn_shift", [P, 1]), sb("bn_var_eps", [P, 1])
        ON, SG = sb("normed", [P, 2, BANK]), sb("gate", [P, 2, BANK])

        pa, pb = (ctx.enter_context(nc.psum_tensor("l1_p_" + n, [P, 2, BANK], F32)) for n in ("in", "scan"))
        dp = ctx.enter_context(nc.psum_tensor("l1_p_dt", [P, BANK], F32))
        zx, cr = ([pa[:, r, o:o + w] for r in range(2)] for o, w in ((0, ZW), (ZW, P)))
        btp, ctp, gp = ([pb[:, r, o:o + P] for r in range(2)] for o in (0, P, 2 * P))
        yp, hp = ([pb[:, r, o:o + DI] for r in range(2)] for o in (3 * P, 3 * P + DI))
        pf = ctx.enter_context(nc.psum_tensor("l1_p_front", [P, 2, BANK], F32))

        loaded, cleared, wprep, aprep = sem("loaded"), sem("cleared"), sem("weights_ready"), sem("A_ready")
        f_ready, f_used, o1_ready, th_front, vh_ready, o2_ready = (sem(n) for n in ("front_ready", "front_used", "o1_ready", "tanh_front", "half_front", "o2_ready"))
        s4a, s4v, dtp_ready, dx_ready, dab_ready, de_ready, ln_ready, dt_ready, av_ready, cs_ready, ncs_ready = (
            sem(n) for n in ("rows_by_scalar", "rows_by_vector", "dt_projected", "dt_biased", "dt_abs", "dt_exp", "dt_log", "dt_ready", "decay_log_ready", "decay_sum", "ncs_ready"))
        lh_ready, cr_ready, xh_ready, th_ready, zs_ready, bc_ready, bt_ready, g_ready, t_ready, lt_ready = (
            sem(n) for n in ("chunk_copied", "projected", "xh_ready", "tanh_ready", "zs_ready", "bc_transposed", "bc_ready", "g_ready", "masked", "decay_ready"))
        gl_ready, y_ready, h_ready, y1_ready, y2_ready = (sem(n) for n in ("gl_ready", "y_ready", "h_ready", "y1_ready", "y2_ready"))
        sq_ready, ms_ready, rln_ready, rs_ready, yn_ready, yt_ready, yt_stored, s2_ready, s2_stored = (
            sem(n) for n in ("squares", "mean_square_ready", "rms_log", "rms_ready", "y_normed", "y_T", "y_T_stored", "scan_projected", "scan_stored"))
        o_ready, st_ready, rv_ready, sd_ready, sc_ready, on_ready, o4_ready, sg_ready, x_done = (
            sem(n) for n in ("o_ready", "stats_ready", "bn_var", "bn_std", "bn_scale", "normed_ready", "conv4_ready", "gate_ready", "x_done"))

        block = ctx.enter_context(nc.Block())
        col = ("lin1_b", "dw_b", "bn_g", "bn_b", "conv4_b")
        n_loads = 2 + 1 + NB + DC + 2 * 3 * DC + 2 + 2 + DC * 2 + len(col) + 2 + 6

        def scan_at(dr, c):
            return c if dr == 0 else (NC - 1) - c

        @block.sync
        def _(sp):
            def load(dst, src):
                sp.dma_start(dst, src, allow_slow_non_contiguous=True).then_inc(loaded, 16)
            load(LW[:, :], d["L1_conv_lin1_w"])
            load(W4[:, :], d["L1_conv_conv4_w"])
            load(DW[:, :], d["L1_conv_dw_w"].rearrange("c a h w -> c (a h w)"))
            sp.wait_ge(cleared, 1)
            for b in range(NB):
                load(FO[32 * b:32 * b + 32, b, :], d["L1_conv_fc_out_w"])
            for j in range(DC):
                load(FI[:, j, :], d["L1_conv_fc_in_w"])
            for dr in range(2):
                for j in range(DC):
                    q, w_in = slice(32 * j, 32 * j + 32), d["L1_conv_mam_in_w"][dr]
                    load(WA[dr][q, XO:ZO], w_in[:, DI:ZW])
                    load(WA[dr][q, ZO:ZW], w_in[:, 0:DI])
                    load(WA[dr][q, ZW:ZW + 1], w_in[:, ZW:ZW + 1])
                load(CW[:, dr, :], d["L1_conv_mam_conv_w"][dr].rearrange("c j -> (c j)").partition_broadcast(P))
                load(BI[:, dr, XO:ZO], d["L1_conv_mam_conv_b"][dr].partition_broadcast(P))
                for j in range(DC):
                    load(WOU[DI * dr:DI * dr + DI, j, :], d["L1_conv_mam_out_w"][dr])
                load(VEC[DI * dr:DI * dr + DI, 5:6], d["L1_conv_mam_norm_w"][dr].rearrange("(c a) -> c a", a=1))
                load(VEC[:, 6 + dr:7 + dr], d["L1_conv_mam_dt_bias"][dr].partition_broadcast(P))
                load(VEC[:, 8 + dr:9 + dr], d["L1_conv_mam_A_log"][dr].partition_broadcast(P))
                load(VEC[:, 10 + dr:11 + dr], d["L1_conv_mam_D"][dr].partition_broadcast(P))
            for i, n in enumerate(col):
                load(VEC[:, i:i + 1], d["L1_conv_" + n].rearrange("(c a) -> c a", a=1))
            sp.wait_ge(loaded, 16 * n_loads)

        @block.gpsimd
        def _(pool):
            pool.memset(FO[:, :, :], 0.0).then_inc(cleared, 1)
            pool.memset(O1[:, :], 0.0).then_inc(cleared, 1)
            pool.memset(S2[:, :], 0.0).then_inc(cleared, 1)
            for dr in range(2):
                pool.memset(S4[dr][:, :], 0.0).then_inc(cleared, 1)
            pool.memset(BI[:, :, ZO:ZW], 0.0).then_inc(cleared, 1)
            with pool.Fori(0, NB) as b:
                with pool.Fori(0, NC) as c:
                    n = b * NC + c
                    pool.wait_ge(av_ready, b + 1)
                    pool.wait_ge(cr_ready, 2 * n)
                    for r in range(2):
                        at = scan_at(r, c)
                        pool.tensor_copy(LH[:, r, :], S4[r][:, bass.ds(S0[r] + at * P, P)])
                        pool.tensor_copy(AB[:, r, :], AV[:, bass.ds(r * NC + at, 1)].to_broadcast([P, P])).then_inc(lh_ready, 1)

        @block.vector
        def _(v):
            v.wait_ge(loaded, 16 * n_loads)
            v.wait_ge(cleared, 6)
            for k in range(9):
                v.tensor_scalar(DG[:, k, :], C["ident"], DW[:, k:k + 1], None, ALU.mult)
            for dr in range(2):
                for j in range(DC):
                    q = slice(32 * j, 32 * j + 32)
                    v.scalar_tensor_tensor(WA[dr][q, XO:ZO], WA[dr][q, XO:ZO], 0.5, CW[q, dr, :].rearrange("p (c j) -> p c j", j=DC)[:, :, j], ALU.mult, ALU.mult)
                    if j < DC - 1:
                        v.memset(WA[dr][q, ZO:ZW], 0.0)
                        v.memset(WA[dr][q, ZW:ZW + 1], 0.0)
                    else:
                        v.tensor_scalar(WA[dr][q, ZO:ZW], WA[dr][q, ZO:ZW], 0.5, None, ALU.mult)
            v.tensor_scalar(BI[:, :, :], BI[:, :, :], 0.5, None, ALU.mult)
            v.tensor_scalar(HB[:, :], VEC[:, 1:2], 0.5, None, ALU.mult).then_inc(wprep, 1)
            v.wait_ge(aprep, 1)
            v.tensor_scalar(NEA[:, :], NEA[:, :], -1.0, None, ALU.mult).then_inc(wprep, 1)
            v.wait_ge(wprep, 2)
            with v.Fori(0, NB) as b:
                for j in range(8):
                    v.wait_ge(f_ready, b * 24 + 8 + j + 1)
                    v.tensor_scalar(VH[:, j % 2, :], pf[:, j % 2, :], 0.5, HB[:, 0:1], ALU.mult, ALU.add).then_inc(vh_ready, 1)
                    v.wait_ge(th_front, b * 8 + j + 1)
                    v.scalar_tensor_tensor(O2[:, j * BANK:(j + 1) * BANK], THB[:, j % 2, :], 1.0, VH[:, j % 2, :], ALU.add, ALU.mult).then_inc(o2_ready, 1)
                for j in range(1, 8, 2):
                    v.wait_ge(f_ready, b * 24 + 16 + j + 1)
                    for i in range(DC):
                        for r, o in ((0, DC - 1 - i), (1, i)):
                            last = v.tensor_copy(S4[r][32 * i:32 * i + 32, j * BANK + o:(j + 1) * BANK + o], pf[32 * i:32 * i + 32, j % 2, :])
                    last.then_inc(s4v, 1)
                v.wait_ge(dtp_ready, b + 1)
                for r in range(2):
                    last = v.tensor_scalar(DX[:, r * NC:(r + 1) * NC], dp[:, r * NC:(r + 1) * NC], VEC[:, 6 + r:7 + r], None, ALU.add)
                last.then_inc(dx_ready, 1)
                v.wait_ge(ln_ready, b + 1)
                v.scalar_tensor_tensor(DT[:, :], DX[:, :], 0.0, DE[:, :], ALU.max, ALU.add).then_inc(dt_ready, 1)
                v.wait_ge(dt_ready, b + 1)
                for r in range(2):
                    last = v.tensor_scalar(AV[:, r * NC:(r + 1) * NC], DT[:, r * NC:(r + 1) * NC], NEA[:, r:r + 1], None, ALU.mult)
                last.then_inc(av_ready, 1)
                v.wait_ge(cs_ready, b + 1)
                v.tensor_scalar(NCS[:, :], dp[:, 2 * NC:4 * NC], -1.0, None, ALU.mult).then_inc(ncs_ready, 1)
                v.memset(HST[:, :, :], 0.0)
                with v.Fori(0, NC) as c:
                    n = 2 * (b * NC + c)
                    for r in range(2):
                        v.wait_ge(cr_ready, n + r + 1)
                        v.tensor_tensor(XH[:, r, :], zx[r], BI[:, r, :], ALU.add).then_inc(xh_ready, 1)
                    for r in range(2):
                        v.tensor_tensor(TM[:, r, :], cr[r], C["neg_" + "fb"[r]], ALU.add).then_inc(t_ready, 1)
                    for r in range(2):
                        v.wait_ge(th_ready, n + r + 1)
                        v.scalar_tensor_tensor(ZS[:, r, :], TH[:, r, :], 1.0, XH[:, r, :], ALU.add, ALU.mult).then_inc(zs_ready, 1)
                    for r in range(2):
                        last_t = P - 1 if r == 0 else 0
                        dt = DT[:, bass.ds(r * NC + scan_at(r, c), 1)]
                        v.wait_ge(g_ready, n + r + 1)
                        v.wait_ge(lt_ready, n + r + 1)
                        v.tensor_tensor(CE[:, r, :], CT[:, r, :], ECS[:, r, :], ALU.mult)
                        v.scalar_tensor_tensor(GL[:, r, :], gp[r], dt, LT[:, r, :], ALU.mult, ALU.mult)
                        v.tensor_scalar(BD[:, r, :], ZS[:, r, BO:CO], LT[:, r, last_t:last_t + 1], dt, ALU.mult, ALU.mult).then_inc(gl_ready, 1)
                    for r in range(2):
                        last_t = P - 1 if r == 0 else 0
                        v.wait_ge(y_ready, n + r + 1)
                        v.scalar_tensor_tensor(HST[:, r, :], HST[:, r, :], ECS[:, r, last_t:last_t + 1], hp[r][0:DI, :], ALU.mult, ALU.add).then_inc(h_ready, 1)
                        v.scalar_tensor_tensor(Y1[:, r, :], ZS[:, r, XO:BO], VEC[:, 10 + r:11 + r], yp[r], ALU.mult, ALU.add).then_inc(y1_ready, 1)
                    for r in range(2):
                        v.wait_ge(y1_ready, n + r + 1)
                        v.tensor_tensor(YST[:, bass.ds(scan_at(r, c) * P + r * DI, DI)], Y1[:, r, :], ZS[:, r, ZO:ZW], ALU.mult).then_inc(y2_ready, 1)
                v.wait_ge(sq_ready, b + 1)
                v.tensor_reduce(MSQ[:, :], O2[:, :].rearrange("p (a k) -> p a k", k=DI), AX.X, ALU.add).then_inc(ms_ready, 1)
                v.wait_ge(rs_ready, b + 1)
                v.tensor_tensor(YST.rearrange("p (a k) -> p a k", k=DI), YST.rearrange("p (a k) -> p a k", k=DI), RST[:, :].unsqueeze(2).to_broadcast([P, 2 * NC, DI]), ALU.mult).then_inc(yn_ready, 1)
                for j in range(8):
                    v.wait_ge(yt_ready, b * 8 + j + 1)
                    v.tensor_scalar(YT[:, j * BANK:(j + 1) * BANK], pf[:, j % 2, :], VEC[:, 5:6], None, ALU.mult).then_inc(yt_stored, 1)
                for j in range(8):
                    v.wait_ge(s2_ready, b * 8 + j + 1)
                    v.scalar_tensor_tensor(S2[:, j * BANK:(j + 1) * BANK], pf[:, j % 2, :], C["quad"][:, bass.ds(b, 1)], S2[:, j * BANK:(j + 1) * BANK], ALU.mult, ALU.add).then_inc(s2_stored, 1)
                v.wait_ge(yt_ready, b * 8 + 8)
                v.memset(O1[:, 0:L], 0.0).then_inc(x_done, 1)
            for i in range(NB * 8):
                v.wait_ge(o_ready, i + 1)
                v.bn_stats(ST[:, i, :], pf[:, i % 2, :]).then_inc(st_ready, 1)
            ch = Chain(v, st_ready, NB * 8)
            v.wait_ge(st_ready, NB * 8)
            ch(v.bn_aggr(MV[:, :], ST[:, :, :].rearrange("p a s -> p (a s)")))
            v.tensor_scalar(RV[:, :], MV[:, 1:2], 1e-5, None, ALU.add).then_inc(rv_ready, 1)
            v.wait_ge(sd_ready, 1)
            ch(v.reciprocal(SC[:, :], RV[:, :]))
            ch(v.tensor_tensor(SC[:, :], SC[:, :], VEC[:, 2:3], ALU.mult))
            ch(v.tensor_tensor(SH[:, :], SC[:, :], MV[:, 0:1], ALU.mult))
            v.tensor_tensor(SH[:, :], VEC[:, 3:4], SH[:, :], ALU.subtract).then_inc(sc_ready, 1)
            for i in range(NB * 8):
                v.wait_ge(sg_ready, i + 1)
                v.scalar_tensor_tensor(X[:, i * BANK:(i + 1) * BANK], SG[:, i % 2, :], 1.0, X[:, i * BANK:(i + 1) * BANK], ALU.add, ALU.mult).then_inc(x_done, 1)

        @block.scalar
        def _(a):
            a.wait_ge(loaded, 16 * n_loads)
            a.activation(NEA[:, :], VEC[:, 8:10], ACT.Exp).then_inc(aprep, 1)
            a.wait_ge(wprep, 2)
            with a.Fori(0, NB) as b:
                for j in range(8):
                    a.wait_ge(f_ready, b * 24 + j + 1)
                    a.activation(O1v[:, 1 + 8 * j:9 + 8 * j, 1:WW + 1], pf[:, j % 2, :].rearrange("p (h w) -> p h w", w=WW), ACT.Identity, bias=VEC[:, 0:1]).then_inc(o1_ready, 1)
                for j in range(8):
                    a.wait_ge(vh_ready, b * 8 + j + 1)
                    a.activation(THB[:, j % 2, :], VH[:, j % 2, :], ACT.Tanh).then_inc(th_front, 1)
                for j in range(0, 8, 2):
                    a.wait_ge(f_ready, b * 24 + 16 + j + 1)
                    for i in range(DC):
                        for r, o in ((0, DC - 1 - i), (1, i)):
                            last = a.activation(S4[r][32 * i:32 * i + 32, j * BANK + o:(j + 1) * BANK + o], pf[32 * i:32 * i + 32, j % 2, :], ACT.Copy)
                    last.then_inc(s4a, 1)
                a.wait_ge(dx_ready, b + 1)
                a.activation(DE[:, :], DX[:, :], ACT.Abs).then_inc(dab_ready, 1)
                a.wait_ge(dab_ready, b + 1)
                a.activation(DE[:, :], DE[:, :], ACT.Exp, scale=-1.0).then_inc(de_ready, 1)
                a.wait_ge(de_ready, b + 1)
                a.activation(DE[:, :], DE[:, :], ACT.Ln, bias=1.0).then_inc(ln_ready, 1)
                a.wait_ge(ncs_ready, b + 1)
                a.activation(RST[:, 0:1], NCS[:, 0:1], ACT.Tanh)
                with a.Fori(0, NC) as c:
                    n = 2 * (b * NC + c)
                    for r in range(2):
                        a.wait_ge(xh_ready, n + r + 1)
                        a.activation(TH[:, r, :], XH[:, r, :], ACT.Tanh).then_inc(th_ready, 1)
                    for r in range(2):
                        a.wait_ge(t_ready, n + r + 1)
                        a.activation(LT[:, r, :], TM[:, r, :], ACT.Exp, bias=NCS[:, bass.ds(r * NC + scan_at(r, c), 1)])
                        a.activation(ECS[:, r, :], cr[r][0:DI, :], ACT.Exp).then_inc(lt_ready, 1)
                    for r in range(2):
                        a.wait_ge(bc_ready, n + r + 1)
                        a.activation(BT[:, r, :], btp[r][0:DI, :], ACT.Copy)
                        a.activation(CT[:, r, :], ctp[r][0:DI, :], ACT.Copy).then_inc(bt_ready, 1)
                a.wait_ge(y2_ready, (b + 1) * 2 * NC)
                a.activation(O2[:, :], YST, ACT.Square).then_inc(sq_ready, 1)
                a.wait_ge(ms_ready, b + 1)
                a.activation(MSQ[:, :], MSQ[:, :], ACT.Ln, bias=C["eps5"], scale=1.0 / DI).then_inc(rln_ready, 1)
                a.wait_ge(rln_ready, b + 1)
                a.activation(RST[:, :], MSQ[:, :], ACT.Exp, scale=-0.5).then_inc(rs_ready, 1)
            a.wait_ge(rv_ready, 1)
            a.activation(RV[:, :], RV[:, :], ACT.Sqrt).then_inc(sd_ready, 1)
            a.wait_ge(sc_ready, 1)
            for i in range(NB * 8 + 1):
                if i < NB * 8:
                    a.wait_ge(o_ready, NB * 8 + i + 1)
                    if i >= 2:
                        a.wait_ge(o4_ready, i - 1)
                    a.activation(ON[:, i % 2, :], pf[:, i % 2, :], ACT.Identity, bias=SH[:, 0:1], scale=SC[:, 0:1]).then_inc(on_ready, 1)
                if i > 0:
                    k = i - 1
                    a.wait_ge(o4_ready, k + 1)
                    if k >= 2:
                        a.wait_ge(x_done, NB + k - 1)
                    a.activation(SG[:, k % 2, :], pa[:, k % 2, :], ACT.Sigmoid, bias=VEC[:, 4:5]).then_inc(sg_ready, 1)

        @block.tensor
        def _(t):
            t.wait_ge(loaded, 16 * n_loads)
            t.wait_ge(wprep, 2)
            with t.Fori(0, NB) as b:
                for j in range(8):
                    if j >= 2:
                        t.wait_ge(o1_ready, b * 8 + j - 1)
                    if j == 0:
                        t.wait_ge(x_done, b)
                    t.matmul(pf[:, j % 2, :], LW[:, :], X[:, bass.ds(b * L + j * BANK, BANK)], start=True, stop=True).then_inc(f_ready, 1)
                for j in range(8):
                    if j == 0:
                        t.wait_ge(o1_ready, b * 8 + 8)
                    if j >= 2:
                        t.wait_ge(o2_ready, b * 8 + j - 1)
                    for k in range(9):
                        last = t.matmul(pf[:, j % 2, :], DG[:, k, :], O1v[:, 8 * j + k // 3:8 * j + k // 3 + 8, k % 3:k % 3 + WW], start=k == 0, stop=k == 8)
                    last.then_inc(f_ready, 1)
                for j in range(8):
                    if j < 2:
                        t.wait_ge(o2_ready, b * 8 + 8)
                    else:
                        t.wait_ge(s4v if j % 2 else s4a, b * 4 + j // 2)
                    t.matmul(pf[:, j % 2, :], FI[:, :, :].rearrange("p a b -> p (a b)"), O2[:, j * BANK:(j + 1) * BANK], start=True, stop=True).then_inc(f_ready, 1)
                t.wait_ge(s4a, b * 4 + 4)
                t.wait_ge(s4v, b * 4 + 4)
                for r in range(2):
                    for c in range(NC):
                        last = t.matmul(dp[:, r * NC + c:r * NC + c + 1], S4[r][:, S0[r] + c * P:S0[r] + (c + 1) * P], WA[r][:, ZW:ZW + 1], start=True, stop=True)
                last.then_inc(dtp_ready, 1)
                t.wait_ge(av_ready, b + 1)
                for r in range(2):
                    last = t.matmul(dp[:, (2 + r) * NC:(3 + r) * NC], C["tri_" + "fb"[r]], AV[:, r * NC:(r + 1) * NC], start=True, stop=True)
                last.then_inc(cs_ready, 1)
                with t.Fori(0, NC) as c:
                    n = 2 * (b * NC + c)
                    for r in range(2):
                        t.wait_ge(lh_ready, n + r + 1)
                        t.matmul(zx[r], LH[:, r, :], WA[r][:, 0:ZW], start=True, stop=True)
                        t.matmul(cr[r], AB[:, r, :], C["tri_" + "fb"[r]], start=True, stop=True).then_inc(cr_ready, 1)
                    for r in range(2):
                        t.wait_ge(zs_ready, n + r + 1)
                        t.transpose(btp[r], ZS[:, r, BO:BO + P], C["ident"])
                        t.transpose(ctp[r], ZS[:, r, CO:CO + P], C["ident"]).then_inc(bc_ready, 1)
                    for r in range(2):
                        t.wait_ge(bt_ready, n + r + 1)
                        t.matmul(gp[r], BT[:, r, :], CT[:, r, :], start=True, stop=True).then_inc(g_ready, 1)
                    for r in range(2):
                        t.wait_ge(gl_ready, n + r + 1)
                        t.wait_ge(h_ready, n)
                        t.matmul(yp[r], GL[:, r, :], ZS[:, r, XO:BO], start=True, stop=False)
                        t.matmul(yp[r], CE[:, r, :], HST[:, r, :], start=False, stop=True)
                        t.matmul(hp[r][0:DI, :], BD[:, r, :], ZS[:, r, XO:BO], start=True, stop=True).then_inc(y_ready, 1)
                for j in range(8):
                    if j < 2:
                        t.wait_ge(yn_ready, b + 1)
                    else:
                        t.wait_ge(yt_stored, b * 8 + j - 1)
                    for i in range(4):
                        last = t.transpose(pf[:, j % 2, i * P:(i + 1) * P], YST[:, (4 * j + i) * P:(4 * j + i + 1) * P], C["ident"])
                    last.then_inc(yt_ready, 1)
                for j in range(8):
                    if j < 2:
                        t.wait_ge(yt_stored, b * 8 + 8)
                    else:
                        t.wait_ge(s2_stored, b * 8 + j - 1)
                    t.matmul(pf[:, j % 2, :], WOU[:, :, :].rearrange("p a b -> p (a b)"), YT[:, j * BANK:(j + 1) * BANK], start=True, stop=True).then_inc(s2_ready, 1)
            t.wait_ge(s2_stored, NB * 8)
            for turn in range(2):
                for i in range(NB * 8):
                    if turn == 0 and i >= 2:
                        t.wait_ge(st_ready, i - 1)
                    if turn == 1:
                        t.wait_ge(sc_ready, 1)
                        if i >= 2:
                            t.wait_ge(on_ready, i - 1)
                    t.matmul(pf[:, i % 2, :], FO[:, i // 8, :], S2[:, (i % 8) * BANK:(i % 8 + 1) * BANK], start=True, stop=True).then_inc(o_ready, 1)
                    if turn == 1:
                        if i >= 2:
                            t.wait_ge(sg_ready, i - 1)
                        t.wait_ge(on_ready, i + 1)
                        t.matmul(pa[:, i % 2, :], W4[:, :], ON[:, i % 2, :], start=True, stop=True).then_inc(o4_ready, 1)


TT = NB * NT
GT = 8
GW = GT * P
NG = TT // GT
INV2PI, TWOPI = float(1.0 / (2.0 * np.pi)), 6.283185
ROUND = 1.5 * 2.0 ** 23


class Norm:

    def __init__(self, sb):
        self.stats = sb("norm_stats", [P, TT * 6])
        self.mean2, self.diff, self.var, self.std, self.scale, self.shift = (
            sb("norm_" + n, [P, TT]) for n in ("mean2", "diff", "var", "std", "scale", "shift"))

    def vector(self, v, ch, var_ready, std_ready, eps=1e-5, turn=1):
        st = self.stats[:, :].rearrange("p (t s) -> p t s", s=6)
        ch(v.tensor_tensor(self.mean2[:, :], st[:, :, 1], st[:, :, 4], ALU.add))
        ch(v.tensor_tensor(self.diff[:, :], st[:, :, 1], st[:, :, 4], ALU.subtract))
        ch(v.tensor_tensor(self.var[:, :], st[:, :, 2], st[:, :, 5], ALU.add))
        ch(v.tensor_tensor(self.diff[:, :], self.diff[:, :], self.diff[:, :], ALU.mult))
        ch(v.tensor_scalar(self.var[:, :], self.var[:, :], 1.0 / P, eps, ALU.mult, ALU.add))
        v.scalar_tensor_tensor(self.var[:, :], self.diff[:, :], 0.25, self.var[:, :], ALU.mult, ALU.add).then_inc(var_ready, 1)
        v.wait_ge(std_ready, turn)
        ch(v.reciprocal(self.scale[:, :], self.std[:, :]))
        ch(v.scalar_tensor_tensor(self.shift[:, :], self.mean2[:, :], -0.5, self.scale[:, :], ALU.mult, ALU.mult))

    def scalar(self, a, var_ready, std_ready, turn=1):
        a.wait_ge(var_ready, turn)
        a.activation(self.std[:, :], self.var[:, :], ACT.Sqrt).then_inc(std_ready, 1)

    def apply(self, a, dst, src, tile, k):
        return a.activation(dst, src, ACT.Identity, bias=self.shift[:, bass.ds(tile + k, 1)], scale=self.scale[:, bass.ds(tile + k, 1)])


def to_tokens(nc, T, C, N):
    with stage_semaphores(nc, "tr_") as sem, ExitStack() as ctx:
        XB = ctx.enter_context(nc.sbuf_tensor("tr_block", [P, 2, BANK], F32))
        tp = ctx.enter_context(nc.psum_tensor("tr_psum", [P, 2, BANK], F32))
        copied, turned, stored, chain, var_ready, std_ready = (sem(n) for n in ("copied", "turned", "stored", "vector", "var", "std"))
        with nc.Block() as block:
            @block.gpsimd
            def _(pool):
                with pool.Fori(0, TT // 8) as i:
                    for r in range(2):
                        pool.wait_ge(turned, i * 2)
                        pool.tensor_copy(XB[:, r, :], T[:, bass.ds(i * 2 * BANK + r * BANK, BANK)]).then_inc(copied, 1)

            @block.tensor
            def _(t):
                with t.Fori(0, TT // 8) as i:
                    for r in range(2):
                        t.wait_ge(copied, i * 2 + r + 1)
                        t.wait_ge(stored, i * 2)
                        for k in range(4):
                            last = t.transpose(tp[:, r, k * P:(k + 1) * P], XB[:, r, k * P:(k + 1) * P], C["ident"])
                        last.then_inc(turned, 1)

            @block.vector
            def _(v):
                with v.Fori(0, TT // 8) as i:
                    for r in range(2):
                        v.wait_ge(turned, i * 2 + r + 1)
                        for k in range(4):
                            v.bn_stats(N.stats[:, bass.ds((i * 8 + r * 4 + k) * 6, 6)], tp[:, r, k * P:(k + 1) * P])
                        v.tensor_copy(T[:, bass.ds(i * 2 * BANK + r * BANK, BANK)], tp[:, r, :]).then_inc(stored, 1)
                v.wait_ge(stored, TT // 4)
                N.vector(v, Chain(v, chain), var_ready, std_ready)

            @block.scalar
            def _(a):
                N.scalar(a, var_ready, std_ready)


def quantum_layer(nc, d, T, C, N):
    nf = 2048 // P
    with stage_semaphores(nc, "qa_") as sem, ExitStack() as ctx:
        def sb(name, shape, dt=F32):
            return ctx.enter_context(nc.sbuf_tensor("qa_" + name, shape, dt))

        V = sb("x1", [P, TT * P])
        Q9 = sb("q_and_one", [P, TT * 9])
        q9 = Q9[:, :].rearrange("p (t k) -> p t k", k=9)
        U, A, KR, CS = (sb(n, [P, 2, GW]) for n in ("normed", "angle", "turns", "cosine"))
        QT = sb("q_T", [9, 2, BANK])
        W1S, W1T = sb("w1_b1", [P, nf, 9]), sb("w1_T", [9, nf, P])
        W2S, W2T = V[:, 0:nf * P], sb("w2_T", [P, nf, P])
        HR = KR[:, :, :].rearrange("p a (b n) -> p (a b) n", n=BANK)
        FS = A
        TH8, PH8, CP8, PK8 = (sb(n, [P, 8]) for n in ("theta", "phi", "cos_phi", "phi_turns"))
        G1, B1, G2, B2R = (sb(n, [P, P]) for n in ("gamma1", "beta1", "gamma2", "beta2"))
        B2 = sb("b2", [P, 1])
        QS = sb("q_block", [P, 2, 36])
        hp = ctx.enter_context(nc.psum_tensor("qa_hidden", [P, 4, BANK], F32))
        fo = ctx.enter_context(nc.psum_tensor("qa_out", [P, 2, BANK], F32))
        qp, fp = (ctx.enter_context(nc.psum_tensor("qa_" + n, [P, BANK], F32)) for n in ("q_turned", "out_turned"))
        loaded, w_turned, w_stored, weights_ready = sem("loaded"), sem("w_turned"), sem("w_stored"), sem("weights_ready")

        with nc.Block() as block:
            @block.sync
            def _(sp):
                def load(dst, src):
                    sp.dma_start(dst, src, allow_slow_non_contiguous=True).then_inc(loaded, 16)
                load(W2S, d["L2_attn_w2"])
                load(W1S[:, :, 0:8], d["L2_attn_w1"].rearrange("(n p) k -> p n k", p=P))
                load(W1S[:, :, 8:9], d["L2_attn_b1"].rearrange("(n p a) -> p n a", p=P, a=1))
                load(B2[:, :], d["L2_attn_b2"].rearrange("(c a) -> c a", a=1))
                load(TH8[:, :], d["L2_attn_theta_attn"].partition_broadcast(P))
                load(PH8[:, :], d["L2_attn_phi_ffn"].partition_broadcast(P))
                for dst, n in ((G1, "gamma1"), (B1, "beta1"), (G2, "gamma2"), (B2R, "beta2")):
                    load(dst[:, :], d["L2_attn_" + n].partition_broadcast(P))
                sp.wait_ge(loaded, 160)

            @block.tensor
            def _(t):
                t.wait_ge(loaded, 160)
                for i in range(nf // 4):
                    if i >= 2:
                        t.wait_ge(w_stored, 2 * (i - 1))
                    for k in range(4):
                        t.transpose(hp[:, i % 2, k * P:(k + 1) * P], W2S[:, (4 * i + k) * P:(4 * i + k + 1) * P], C["ident"])
                        last = t.transpose(hp[0:9, 2 + i % 2, k * P:(k + 1) * P], W1S[:, 4 * i + k, :], C["ident"])
                    last.then_inc(w_turned, 1)

            @block.vector
            def _(v):
                v.wait_ge(loaded, 160)
                ch = Chain(v, weights_ready)
                v.tensor_scalar(TH8[:, :], TH8[:, :], INV2PI, 0.25, ALU.mult, ALU.add)
                ch(v.tensor_scalar(PH8[:, :], PH8[:, :], INV2PI, 0.25, ALU.mult, ALU.add))
                ch(v.tensor_scalar(PK8[:, :], PH8[:, :], ROUND, ROUND, ALU.add, ALU.subtract))
                ch(v.tensor_tensor(PH8[:, :], PH8[:, :], PK8[:, :], ALU.subtract))
                v.memset(q9[:, :, 8:9], 1.0)
                for i in range(nf // 4):
                    v.wait_ge(w_turned, i + 1)
                    v.tensor_copy(W2T[:, 4 * i:4 * i + 4, :].rearrange("p a b -> p (a b)"), hp[:, i % 2, :]).then_inc(w_stored, 1)
                    v.tensor_copy(W1T[:, 4 * i:4 * i + 4, :].rearrange("p a b -> p (a b)"), hp[0:9, 2 + i % 2, :]).then_inc(w_stored, 1)

            @block.scalar
            def _(a):
                a.wait_ge(weights_ready, 3)
                a.activation(CP8[:, :], PH8[:, :], ACT.Sin, scale=TWOPI)

        u_ready, r_ready, cs_ready, cp_ready, cp_step, v_ready, chain, va, sa = (
            sem(n) for n in ("u_ready", "angle_ready", "cosine_ready", "products_ready", "product_step", "v_ready", "vector_angle", "var1", "std1"))
        c2, c2s = sem("vector_norm1"), sem("v_sum")

        with nc.Block() as block:
            @block.scalar
            def _(a):
                a.activation(CS[:, 0, 0:1], CP8[:, 0:1], ACT.Sin)
                with a.Fori(0, NG // 2) as i:
                    a.wait_ge(v_ready, i * 2)
                    for r in range(2):
                        for k in range(GT):
                            last = N.apply(a, U[:, r, k * P:(k + 1) * P], T[:, bass.ds((i * 2 + r) * GW + k * P, P)], (i * 2 + r) * GT, k)
                        last.then_inc(u_ready, 1)
                    for r in range(2):
                        a.wait_ge(r_ready, i * 2 + r + 1)
                        a.activation(CS[:, r, :], A[:, r, :], ACT.Sin, scale=TWOPI).then_inc(cs_ready, 1)
                N.scalar(a, va, sa)

            @block.gpsimd
            def _(pool):
                with pool.Fori(0, NG // 2) as i:
                    for r in range(2):
                        pool.wait_ge(cs_ready, i * 2 + r + 1)
                        c = CS[:, r, :].rearrange("p (a k) -> p a k", k=8)
                        for k in range(1, 8):
                            last = pool.tensor_tensor(c[:, :, k], c[:, :, k], c[:, :, k - 1], ALU.mult)
                            if k < 7:
                                last.then_inc(cp_step, 1)
                                pool.wait_ge(cp_step, (i * 2 + r) * 6 + k)
                        last.then_inc(cp_ready, 1)

            @block.vector
            def _(v):
                with v.Fori(0, NG // 2) as i:
                    ch = Chain(v, chain, i * 4)
                    for r in range(2):
                        v.wait_ge(u_ready, i * 2 + r + 1)
                        ch(v.scalar_tensor_tensor(A[:, r, :].rearrange("p (a k) -> p a k", k=8), U[:, r, :].rearrange("p (a k) -> p a k", k=8), INV2PI,
                                                  TH8[:, :].unsqueeze(1).to_broadcast([P, GW // 8, 8]), ALU.mult, ALU.add))
                        ch(v.tensor_scalar(KR[:, r, :], A[:, r, :], ROUND, ROUND, ALU.add, ALU.subtract))
                        v.tensor_tensor(A[:, r, :], A[:, r, :], KR[:, r, :], ALU.subtract).then_inc(r_ready, 1)
                    for r in range(2):
                        n = i * 2 + r
                        v.wait_ge(cp_ready, n + 1)
                        u, c = (z[:, r, :].rearrange("p (a k) -> p a k", k=8) for z in (U, CS))
                        w = V[:, bass.ds(n * GW, GW)].rearrange("p (a k) -> p a k", k=8)
                        v.tensor_tensor(w[:, :, 0:1], u[:, :, 0:1], c[:, :, 7:8], ALU.add)
                        v.tensor_tensor(w[:, :, 1:8], u[:, :, 1:8], c[:, :, 1:8], ALU.add).then_inc(c2s, 1)
                        v.wait_ge(c2s, n + 1)
                        for k in range(GT):
                            last = v.bn_stats(N.stats[:, bass.ds((n * GT + k) * 6, 6)], V[:, bass.ds(n * GW + k * P, P)])
                        last.then_inc(v_ready, 1)
                v.wait_ge(v_ready, NG)
                N.vector(v, Chain(v, c2), va, sa)

        w_ready, x1_ready, g_step, qr, qk, qs_ready = (sem(n) for n in ("w_ready", "x1_ready", "scaled", "q_angle", "q_turns", "q_sine"))
        CQ, KQ = CS[:, :, :].rearrange("p a n -> p (a n)")[:, 0:TT * 8], A[:, :, :].rearrange("p a n -> p (a n)")[:, 0:TT * 8]

        with nc.Block() as block:
            @block.scalar
            def _(a):
                with a.Fori(0, NG // 2) as i:
                    a.wait_ge(x1_ready, i * 2)
                    for r in range(2):
                        for k in range(GT):
                            last = N.apply(a, U[:, r, k * P:(k + 1) * P], V[:, bass.ds((i * 2 + r) * GW + k * P, P)], (i * 2 + r) * GT, k)
                        last.then_inc(w_ready, 1)
                a.wait_ge(qr, 1)
                a.activation(KQ, CQ, ACT.Sin, scale=TWOPI).then_inc(qs_ready, 1)

            @block.vector
            def _(v):
                with v.Fori(0, NG // 2) as i:
                    for r in range(2):
                        n = i * 2 + r
                        u = U[:, r, :].rearrange("p (t c) -> p t c", c=P)
                        w = V[:, bass.ds(n * GW, GW)].rearrange("p (t c) -> p t c", c=P)
                        v.wait_ge(w_ready, n + 1)
                        v.tensor_tensor(u, u, G1[:, :].unsqueeze(1).to_broadcast([P, GT, P]), ALU.mult).then_inc(g_step, 1)
                        v.wait_ge(g_step, 2 * n + 1)
                        v.tensor_tensor(w, u, B1[:, :].unsqueeze(1).to_broadcast([P, GT, P]), ALU.add).then_inc(g_step, 1)
                        v.wait_ge(g_step, 2 * n + 2)
                        v.tensor_scalar(CQ[:, bass.ds(n * GT * 8, GT * 8)].rearrange("p (t k) -> p t k", k=8), w[:, :, 0:8], INV2PI, 0.25, ALU.mult, ALU.add).then_inc(x1_ready, 1)
                v.wait_ge(x1_ready, NG)
                v.tensor_scalar(KQ, CQ, ROUND, ROUND, ALU.add, ALU.subtract).then_inc(qk, 1)
                v.wait_ge(qk, 1)
                v.tensor_tensor(CQ, CQ, KQ, ALU.subtract).then_inc(qr, 1)
                v.wait_ge(qs_ready, 1)
                v.tensor_tensor(q9[:, :, 0:8], KQ.rearrange("p (t k) -> p t k", k=8), CP8[:, :].unsqueeze(1).to_broadcast([P, TT, 8]), ALU.mult)

        qb_ready, qt_turned, qt_ready, h_ready, ha, hv, fo_ready, fs_ready, ft_ready, v2_ready, c4, vb, sb_ = (
            sem(n) for n in ("q_copied", "q_turned", "q_T_ready", "hidden", "hidden_by_scalar", "hidden_by_vector", "ffn_out", "ffn_stored", "ffn_turned", "x1_ffn", "vector_norm2", "var2", "std2"))
        vsum = sem("x1_sum")

        with nc.Block() as block:
            @block.gpsimd
            def _(pool):
                with pool.Fori(0, TT // 8) as i:
                    pool.wait_ge(qt_turned, i * 2)
                    for r in range(2):
                        pool.tensor_copy(QS[:, r, :], Q9[:, bass.ds((i * 2 + r) * 36, 36)]).then_inc(qb_ready, 1)

            @block.tensor
            def _(t):
                with t.Fori(0, TT // 8) as i:
                    for r in range(2):
                        n = i * 2 + r
                        t.wait_ge(qt_ready, n)
                        t.wait_ge(qb_ready, n + 1)
                        for k in range(4):
                            last = t.transpose(qp[0:9, k * P:(k + 1) * P], QS[:, r, 9 * k:9 * k + 9], C["ident"])
                        last.then_inc(qt_turned, 1)
                        t.wait_ge(qt_ready, n + 1)
                        for f in range(nf + 2):
                            if f < nf:
                                if f >= 4:
                                    t.wait_ge(hv if f % 2 else ha, n * 8 + f // 2 - 1)
                                else:
                                    t.wait_ge(hv if f % 2 else ha, n * 8)
                                t.matmul(hp[:, f % 4, :], W1T[:, f, :], QT[:, r, :], start=True, stop=True).then_inc(h_ready, 1)
                            if f >= 2:
                                g = f - 2
                                t.wait_ge(hv if g % 2 else ha, n * 8 + g // 2 + 1)
                                if g == 0:
                                    t.wait_ge(fs_ready, i * 2)
                                last = t.matmul(fo[:, r, :], W2T[:, g, :], HR[:, g % 4, :], start=g == 0, stop=g == nf - 1)
                        last.then_inc(fo_ready, 1)
                        t.wait_ge(fs_ready, n + 1)
                        t.wait_ge(v2_ready, n)
                        for k in range(4):
                            last = t.transpose(fp[:, k * P:(k + 1) * P], FS[:, r, k * P:(k + 1) * P], C["ident"])
                        last.then_inc(ft_ready, 1)

            @block.scalar
            def _(a):
                with a.Fori(0, TT // 8) as i:
                    for r in range(2):
                        n = i * 2 + r
                        a.wait_ge(qt_turned, n + 1)
                        a.activation(QT[:, r, :], qp[0:9, :], ACT.Copy).then_inc(qt_ready, 1)
                        for f in range(0, nf, 2):
                            a.wait_ge(h_ready, n * nf + f + 1)
                            a.activation(HR[:, f % 4, :], hp[:, f % 4, :], ACT.Relu).then_inc(ha, 1)
                        a.wait_ge(fo_ready, n + 1)
                        a.activation(FS[:, r, 0:BANK], fo[:, r, :], ACT.Identity, bias=B2[:, 0:1]).then_inc(fs_ready, 1)
                N.scalar(a, vb, sb_)

            @block.vector
            def _(v):
                with v.Fori(0, TT // 8) as i:
                    for r in range(2):
                        n = i * 2 + r
                        for f in range(1, nf, 2):
                            v.wait_ge(h_ready, n * nf + f + 1)
                            v.tensor_scalar(HR[:, f % 4, :], hp[:, f % 4, :], 0.0, None, ALU.max).then_inc(hv, 1)
                        v.wait_ge(ft_ready, n + 1)
                        v.tensor_tensor(V[:, bass.ds(n * BANK, BANK)], V[:, bass.ds(n * BANK, BANK)], fp[:, :], ALU.add).then_inc(vsum, 1)
                        v.wait_ge(vsum, n + 1)
                        for k in range(4):
                            last = v.bn_stats(N.stats[:, bass.ds((n * 4 + k) * 6, 6)], V[:, bass.ds(n * BANK + k * P, P)])
                        last.then_inc(v2_ready, 1)
                v.wait_ge(v2_ready, TT // 4)
                N.vector(v, Chain(v, c4), vb, sb_)

        w5, g5, x5, c5, vc, sc = (sem(n) for n in ("out_normed", "out_step", "out_added", "vector_norm3", "var3", "std3"))

        with nc.Block() as block:
            @block.scalar
            def _(a):
                with a.Fori(0, NG // 2) as i:
                    a.wait_ge(x5, i * 2)
                    for r in range(2):
                        for k in range(GT):
                            last = N.apply(a, U[:, r, k * P:(k + 1) * P], V[:, bass.ds((i * 2 + r) * GW + k * P, P)], (i * 2 + r) * GT, k)
                        last.then_inc(w5, 1)
                N.scalar(a, vc, sc)

            @block.vector
            def _(v):
                with v.Fori(0, NG // 2) as i:
                    for r in range(2):
                        n = i * 2 + r
                        ch = Chain(v, g5, n * 3)
                        u = U[:, r, :].rearrange("p (t c) -> p t c", c=P)
                        w = T[:, bass.ds(n * GW, GW)]
                        v.wait_ge(w5, n + 1)
                        ch(v.tensor_tensor(u, u, G2[:, :].unsqueeze(1).to_broadcast([P, GT, P]), ALU.mult))
                        ch(v.tensor_tensor(u, u, B2R[:, :].unsqueeze(1).to_broadcast([P, GT, P]), ALU.add))
                        ch(v.tensor_tensor(w, w, U[:, r, :], ALU.add))
                        for k in range(GT):
                            last = v.bn_stats(N.stats[:, bass.ds((n * GT + k) * 6, 6)], T[:, bass.ds(n * GW + k * P, P)])
                        last.then_inc(x5, 1)
                v.wait_ge(x5, NG)
                N.vector(v, Chain(v, c5), vc, sc)


EX = 8
BIG = 1.0e30


def moe_layer(nc, d, T, C, N, tag, last_norm):
    with stage_semaphores(nc, tag) as sem, ExitStack() as ctx:
        def sb(name, shape, dt=F32):
            return ctx.enter_context(nc.sbuf_tensor(tag + name, shape, dt))

        UT = sb("normed_T", [P, TT * P])
        UN, UB = sb("normed", [P, 2, BANK]), sb("normed_T_block", [P, 2, BANK])
        RW, RB, EW = sb("router_w", [P, EX]), sb("router_b", [P, EX]), sb("expert_w", [P, EX, P])
        EB, EH, ER = sb("expert_b", [3, EX * P]), sb("expert_b_part", [3, EX * P], BF16), sb("expert_b_parts", [3, EX * P], BF16)
        ON = sb("ones", [3, P], BF16)
        LG, S1, S2, TMP = (sb(n, [P, TT * EX]) for n in ("logits", "first", "second", "scratch"))
        M1, M2, F1 = (sb(n, [P, TT]) for n in ("max1", "max2", "pick"))
        PRD, HS, RD = sb("weighted", [P, 2, EX * P]), sb("half_sum", [P, 2, EX * P // 2]), sb("moe_out", [P, 2, P])
        lg3, s13, s23, tm3 = (z[:, :].rearrange("p (t e) -> p t e", e=EX) for z in (LG, S1, S2, TMP))
        up = ctx.enter_context(nc.psum_tensor(tag + "turned", [P, 2, BANK], F32))
        lp = ctx.enter_context(nc.psum_tensor(tag + "logit_sums", [P, 2, BANK], F32))
        ep = ctx.enter_context(nc.psum_tensor(tag + "experts", [P, 2, 2, BANK], F32))
        loaded, prep, un_ready, turned, ub_ready, lp_ready, lg_ready, kept = (
            sem(n) for n in ("loaded", "bias_parts", "un_ready", "turned", "ut_ready", "logits", "logits_ready", "ut_kept"))

        with nc.Block() as block:
            @block.sync
            def _(sp):
                for dst, src in ((RW[:, :], d[tag + "router_w"]), (RB[:, :], d[tag + "router_b"].partition_broadcast(P)),
                                 (EW[:, :, :], d[tag + "expert_w"].rearrange("e d c -> d e c")),
                                 (EB[:, :], d[tag + "expert_b"].rearrange("e c -> (e c)").partition_broadcast(3))):
                    sp.dma_start(dst, src).then_inc(loaded, 16)
                sp.wait_ge(loaded, 64)

            @block.scalar
            def _(a):
                with a.Fori(0, TT // 8) as i:
                    for r in range(2):
                        a.wait_ge(turned, i * 2)
                        for k in range(4):
                            last = N.apply(a, UN[:, r, k * P:(k + 1) * P], T[:, bass.ds((i * 2 + r) * BANK + k * P, P)], (i * 2 + r) * 4, k)
                        last.then_inc(un_ready, 1)

            @block.tensor
            def _(t):
                t.wait_ge(loaded, 64)
                with t.Fori(0, TT // 8) as i:
                    for r in range(2):
                        n = i * 2 + r
                        t.wait_ge(un_ready, n + 1)
                        for k in range(4):
                            last = t.transpose(up[:, r, k * P:(k + 1) * P], UN[:, r, k * P:(k + 1) * P], C["ident"])
                        last.then_inc(turned, 1)
                    for r in range(2):
                        n = i * 2 + r
                        t.wait_ge(ub_ready, n + 1)
                        for k in range(4):
                            last = t.matmul(lp[:, r, k * EX:(k + 1) * EX], UB[:, r, k * P:(k + 1) * P], RW[:, :], start=True, stop=True)
                        last.then_inc(lp_ready, 1)

            @block.gpsimd
            def _(pool):
                with pool.Fori(0, TT // 8) as i:
                    for r in range(2):
                        pool.wait_ge(ub_ready, i * 2 + r + 1)
                        pool.tensor_copy(UT[:, bass.ds((i * 2 + r) * BANK, BANK)], UB[:, r, :]).then_inc(kept, 1)

            @block.vector
            def _(v):
                v.wait_ge(loaded, 64)
                ch = Chain(v, prep)
                v.memset(ON[:, :], 1.0)
                ch(v.tensor_copy(EH[:, :], EB[:, :]))
                ch(v.tensor_scalar(ER[:, :], EH[:, :], C["ident"][0:3, 0:1], None, ALU.mult))
                for k in (1, 2):
                    ch(v.tensor_tensor(EB[:, :], EB[:, :], EH[:, :], ALU.subtract))
                    ch(v.tensor_copy(EH[:, :], EB[:, :]))
                    ch(v.scalar_tensor_tensor(ER[:, :], EH[:, :], C["ident"][0:3, k:k + 1], ER[:, :], ALU.mult, ALU.add))
                with v.Fori(0, TT // 8) as i:
                    for r in range(2):
                        n = i * 2 + r
                        v.wait_ge(turned, n + 1)
                        v.wait_ge(kept, i * 2)
                        v.wait_ge(lp_ready, i * 2)
                        v.tensor_copy(UB[:, r, :], up[:, r, :]).then_inc(ub_ready, 1)
                    for r in range(2):
                        n = i * 2 + r
                        v.wait_ge(lp_ready, n + 1)
                        v.tensor_tensor(LG[:, bass.ds(n * 4 * EX, 4 * EX)].rearrange("p (t e) -> p t e", e=EX), lp[:, r, 0:4 * EX].rearrange("p (t e) -> p t e", e=EX),
                                        RB[:, :].unsqueeze(1).to_broadcast([P, 4, EX]), ALU.add).then_inc(lg_ready, 1)

        chain, diff_ready, e_ready, gates = sem("gate_steps"), sem("gate_diff"), sem("gate_exp"), sem("gates_ready")

        with nc.Block() as block:
            def wide(m):
                return m[:, :].unsqueeze(2).to_broadcast([P, TT, EX])

            @block.vector
            def _(v):
                ch = Chain(v, chain)
                for sel, top in ((s13, M1), (s23, M2)):
                    ch(v.tensor_reduce(top[:, :], lg3, AX.X, ALU.max))
                    ch(v.tensor_tensor(sel, lg3, wide(top), ALU.is_equal))
                    ch(v.tensor_tensor(sel, sel, C["first"].unsqueeze(1).to_broadcast([P, TT, EX]), ALU.mult))
                    ch(v.tensor_reduce(F1[:, :], sel, AX.X, ALU.max))
                    ch(v.tensor_tensor(sel, sel, wide(F1), ALU.is_equal))
                    if top is M1:
                        ch(v.scalar_tensor_tensor(LG[:, :], S1[:, :], -BIG, LG[:, :], ALU.mult, ALU.add))
                v.tensor_tensor(M2[:, :], M2[:, :], M1[:, :], ALU.subtract).then_inc(diff_ready, 1)
                v.wait_ge(e_ready, 1)
                ch(v.tensor_scalar(F1[:, :], M1[:, :], 1.0, None, ALU.add))
                ch(v.reciprocal(F1[:, :], F1[:, :]))
                ch(v.tensor_tensor(M2[:, :], M1[:, :], F1[:, :], ALU.mult))
                ch(v.tensor_tensor(s13, s13, wide(F1), ALU.mult))
                ch(v.tensor_tensor(s23, s23, wide(M2), ALU.mult))
                v.tensor_tensor(LG[:, :], S1[:, :], S2[:, :], ALU.add).then_inc(gates, 1)

            @block.scalar
            def _(a):
                a.wait_ge(diff_ready, 1)
                a.activation(M1[:, :], M2[:, :], ACT.Exp).then_inc(e_ready, 1)

        copied, e_out, wv, wa, hs_ready, rd_ready, t_ready, st_ready, c2, vv, ss = (
            sem(n) for n in ("copied", "experts_out", "weighted_by_vector", "weighted_by_scalar", "half_sums", "moe_out", "t_ready", "stats_ready", "vector_norm", "var", "std"))

        with nc.Block() as block:
            @block.gpsimd
            def _(pool):
                with pool.Fori(0, TT // 8) as i:
                    pool.wait_ge(e_out, i * 8)
                    for r in range(2):
                        pool.tensor_copy(UB[:, r, :], UT[:, bass.ds((i * 2 + r) * BANK, BANK)]).then_inc(copied, 1)
                    for k in range(8):
                        n = i * 8 + k
                        q = k % 2
                        pool.wait_ge(wv, n + 1)
                        pool.wait_ge(wa, n + 1)
                        pool.wait_ge(rd_ready, i * 8 + max(k - 1, 0))
                        pool.tensor_tensor(HS[:, q, :], PRD[:, q, 0:BANK], PRD[:, q, BANK:2 * BANK], ALU.add).then_inc(hs_ready, 1)

            @block.tensor
            def _(t):
                with t.Fori(0, TT // 8) as i:
                    for k in range(8):
                        n = i * 8 + k
                        if k % 4 == 0:
                            t.wait_ge(copied, i * 2 + k // 4 + 1)
                        t.wait_ge(wv, i * 8 + max(k - 1, 0))
                        t.wait_ge(wa, i * 8 + max(k - 1, 0))
                        for h in range(2):
                            t.matmul(ep[:, k % 2, h, :], UB[:, k // 4, (k % 4) * P:(k % 4 + 1) * P], EW[:, 4 * h:4 * h + 4, :].rearrange("p e c -> p (e c)"), start=True, stop=False)
                            last = t.matmul(ep[:, k % 2, h, :], ON[:, :], ER[:, h * BANK:(h + 1) * BANK], start=False, stop=True)
                        last.then_inc(e_out, 1)

            @block.scalar
            def _(a):
                with a.Fori(0, TT // 8) as i:
                    for k in range(8):
                        n = i * 8 + k
                        a.wait_ge(e_out, n + 1)
                        a.wait_ge(hs_ready, i * 8 + max(k - 1, 0))
                        for e in range(4, 8):
                            last = a.activation(PRD[:, k % 2, e * P:(e + 1) * P], ep[:, k % 2, 1, (e - 4) * P:(e - 3) * P], ACT.Copy, scale=LG[:, bass.ds(n * EX + e, 1)])
                        last.then_inc(wa, 1)
                if last_norm:
                    N.scalar(a, vv, ss)

            @block.vector
            def _(v):
                with v.Fori(0, TT // 8) as i:
                    for k in range(8 + 1):
                        if k < 8:
                            n = i * 8 + k
                            v.wait_ge(e_out, n + 1)
                            v.wait_ge(hs_ready, i * 8 + max(k - 1, 0))
                            v.tensor_tensor(PRD[:, k % 2, 0:BANK].rearrange("p (e c) -> p e c", c=P), ep[:, k % 2, 0, :].rearrange("p (e c) -> p e c", c=P),
                                            LG[:, bass.ds(n * EX, 4)].unsqueeze(2).to_broadcast([P, 4, P]), ALU.mult).then_inc(wv, 1)
                        if k > 0:
                            q = (k - 1) % 2
                            n = i * 8 + k - 1
                            v.wait_ge(hs_ready, n + 1)
                            v.tensor_reduce(RD[:, q, :], HS[:, q, :].rearrange("p (e c) -> p c e", c=P), AX.X, ALU.add).then_inc(rd_ready, 1)
                            v.wait_ge(rd_ready, n + 1)
                            v.tensor_tensor(T[:, bass.ds(n * P, P)], T[:, bass.ds(n * P, P)], RD[:, q, :], ALU.add).then_inc(t_ready, 1)
                            if last_norm:
                                v.wait_ge(t_ready, n + 1)
                                v.bn_stats(N.stats[:, bass.ds(n * 6, 6)], T[:, bass.ds(n * P, P)]).then_inc(st_ready, 1)
                if last_norm:
                    v.wait_ge(st_ready, TT)
                    N.vector(v, Chain(v, c2), vv, ss)


CHUNK = 2 * BANK
CT_ = CHUNK // P
NCH = L // CHUNK


def additive_attention_layer(nc, d, T, C, N):
    tag = "aa_"
    with stage_semaphores(nc, tag) as sem, ExitStack() as ctx:
        def sb(name, shape, dt=F32):
            return ctx.enter_context(nc.sbuf_tensor(tag + name, shape, dt))

        UN, UT, FR = sb("normed", [P, L]), sb("normed_T", [P, L]), sb("f_8_times", [P, L])
        GB = sb("g_bias", [P, L // 8])
        NR = 4
        TH = sb("tanh", [P, NR, CHUNK])
        ET = sb("weights", [P, 2, CHUNK])
        DEN, DR, OT = sb("denominators", [P, CHUNK]), sb("denominators_inv", [P, CHUNK]), sb("out_T", [P, CHUNK])
        UBK = sb("normed_block", [P, 2, P])
        WF, WG = sb("w_f", [P, 8, 16]), sb("w_g", [P, 8, P])
        W2C, B1C, B2C = sb("w2_col", [P, 1]), sb("b1_col", [P, 1]), sb("b2_col", [P, 1])
        W2S = sb("w2_spread", [P, 4, 32])
        ONE = sb("ones", [P, P])
        ZR = sb("zeros", [P, BANK], BF16)
        sp_ = ctx.enter_context(nc.psum_tensor(tag + "scores", [P, 2, CHUNK], F32))
        op = ctx.enter_context(nc.psum_tensor(tag + "out_sum", [P, CHUNK], F32))
        dp = ctx.enter_context(nc.psum_tensor(tag + "den_sum", [P, 2, BANK], F32))

        loaded, cleared, wready = sem("loaded"), sem("cleared"), sem("weights_ready")
        un_ready, un_turned, ut_ready, f_ready, f_stored, g_sum, g_ready = (sem(n) for n in ("un_ready", "un_turned", "ut_ready", "f_ready", "f_stored", "g_sum", "g_ready"))
        ub_ready, th_ready, th_used, e_ready, em_ready, o_done = (sem(n) for n in ("keys_copied", "tanh_ready", "tanh_used", "exp_ready", "weights_summed", "tile_added"))
        masked, den_zero, o_ready, den_ready, dr_ready, dr_step, ot_ready, ot_turned, t_ready, st_ready, c2, vv, ss = (
            sem(n) for n in ("masked", "den_zero", "chunk_out", "den_ready", "den_inv", "den_step", "ot_ready", "ot_turned", "t_ready", "stats_ready", "vector_norm", "var", "std"))
        TILES = sum((c + 1) * CT_ for c in range(NCH))

        def plan(c):
            return sum((x + 1) * CT_ for x in range(c)), c * CT_

        with nc.Block() as block:
            @block.sync
            def _(sp):
                def load(dst, src):
                    sp.dma_start(dst, src, allow_slow_non_contiguous=True).then_inc(loaded, 16)
                w1 = d["L3_attn_W1"]
                sp.wait_ge(cleared, 1)
                for j in range(8):
                    load(WF[:, j, :], w1[0:P, :])
                    load(WG[:, j, 16 * j:16 * j + 16], w1[P:2 * P, :])
                    load(B1C[16 * j:16 * j + 16, :], d["L3_attn_b1"].rearrange("(c a) -> c a", a=1))
                    load(W2C[16 * j:16 * j + 16, :], d["L3_attn_w2"])
                load(B2C[:, :], d["L3_attn_b2"].partition_broadcast(P))
                sp.wait_ge(loaded, 16 * 33)

            @block.gpsimd
            def _(pool):
                pool.memset(WG[:, :, :], 0.0).then_inc(cleared, 1)
                pool.memset(ONE[:, :], 1.0).then_inc(cleared, 1)
                pool.memset(ZR[:, :], 0.0).then_inc(cleared, 1)
                pool.wait_ge(cleared, 3)
                with pool.Fori(0, NB) as b:
                    for c in range(NCH):
                        first, full = plan(c)
                        n0 = b * TILES + first
                        if full:
                            with pool.Fori(0, full, 2) as j:
                                pool.wait_ge(un_ready, (b + 1) * 8)
                                pool.wait_ge(o_done, n0 + j)
                                for r in range(2):
                                    pool.tensor_copy(UBK[:, r, :], UN[:, bass.ds(j * P + r * P, P)]).then_inc(ub_ready, 1)
                        for j in range(CT_):
                            rows = UN[:, (full + j) * P:(full + j + 1) * P]
                            pool.wait_ge(un_ready, (b + 1) * 8)
                            if j % 2 == 0:
                                pool.wait_ge(o_done, n0 + full + j)
                            pool.tensor_tensor(UBK[:, j % 2, :], rows, ONE[:, :], ALU.mult).then_inc(ub_ready, 1)

            @block.scalar
            def _(a):
                a.wait_ge(loaded, 16 * 33)
                a.activation(GB[:, 0:1], B2C[:, :], ACT.Exp)
                with a.Fori(0, NB) as b:
                    a.wait_ge(o_ready, b * NCH)
                    for q in range(8):
                        for k in range(4):
                            last = N.apply(a, UN[:, (4 * q + k) * P:(4 * q + k + 1) * P], T[:, bass.ds(b * L + (4 * q + k) * P, P)], b * NT, 4 * q + k)
                        last.then_inc(un_ready, 1)
                    a.wait_ge(g_ready, b + 1)
                    a.wait_ge(f_stored, (b + 1) * 8)

                    def exps(n, q, lo):
                        a.wait_ge(th_used, n * 16 + 16 + NR)
                        a.activation(ET[:, q, 0:CHUNK - lo], sp_[:, q, 0:CHUNK - lo], ACT.Exp, bias=B2C[:, 0:1]).then_inc(e_ready, 1)

                    def order():
                        return [4 * q + t for t in range(4) for q in range(4)]

                    for c in range(NCH):
                        first, full = plan(c)
                        n0 = b * TILES + first
                        if full:
                            with a.Fori(0, full, 4) as j:
                                for r in range(4):
                                    for s_, blk in enumerate(order()):
                                        if s_ == 4 and r > 0:
                                            a.wait_ge(o_done, n0 + j + max(r - 2, 0))
                                            exps(n0 + j + r - 1, (r - 1) % 2, 0)
                                        m = (n0 + j + r) * 16 + s_
                                        a.wait_ge(th_used, m + 1)
                                        a.activation(TH[:, s_ % NR, :], FR[:, c * CHUNK:(c + 1) * CHUNK], ACT.Tanh, bias=GB[:, bass.ds((j + r) * 16 + blk, 1)]).then_inc(th_ready, 1)
                                a.wait_ge(o_done, n0 + j + 2)
                                exps(n0 + j + 3, 1, 0)
                        for j in range(CT_ + 1):
                            for s_, blk in enumerate(order()):
                                if j < CT_:
                                    m = (n0 + full + j) * 16 + s_
                                    lo = j * P
                                    if s_ == 4 and j > 0:
                                        a.wait_ge(o_done, n0 + full + max(j - 2, 0))
                                        exps(n0 + full + j - 1, (j - 1) % 2, (j - 1) * P)
                                    a.wait_ge(th_used, m + 1)
                                    a.activation(TH[:, s_ % NR, 0:CHUNK - lo], FR[:, c * CHUNK + lo:(c + 1) * CHUNK], ACT.Tanh, bias=GB[:, (full + j) * 16 + blk:(full + j) * 16 + blk + 1]).then_inc(th_ready, 1)
                            if j == CT_:
                                a.wait_ge(o_done, n0 + full + j - 2)
                                exps(n0 + full + j - 1, (j - 1) % 2, (j - 1) * P)
                N.scalar(a, vv, ss)

            @block.tensor
            def _(t):
                t.wait_ge(loaded, 16 * 33)
                t.wait_ge(cleared, 3)
                t.wait_ge(wready, 4)
                t.sem_inc(th_used, NR)
                with t.Fori(0, NB) as b:
                    for q in range(8):
                        t.wait_ge(un_ready, b * 8 + q + 1)
                        if q >= 2:
                            t.wait_ge(ut_ready, b * 8 + q - 1)
                        elif q == 0:
                            t.wait_ge(t_ready, b * 2 * NCH)
                        for k in range(4):
                            last = t.transpose(dp[:, q % 2, k * P:(k + 1) * P], UN[:, (4 * q + k) * P:(4 * q + k + 1) * P], C["ident"])
                        last.then_inc(un_turned, 1)
                    t.wait_ge(ut_ready, b * 8 + 8)
                    for q in range(8):
                        if q >= 2:
                            t.wait_ge(f_stored, b * 8 + q - 1)
                        t.matmul(dp[:, q % 2, :], WF[:, :, :].rearrange("p j a -> p (j a)"), UT[:, q * BANK:(q + 1) * BANK], start=True, stop=True).then_inc(f_ready, 1)
                    t.wait_ge(f_stored, b * 8 + 8)
                    for j in range(8):
                        last = t.matmul(dp[:, 0, :], WG[:, j, :], UT[:, j:L:8], start=j == 0, stop=j == 7)
                    last.then_inc(g_sum, 1)

                    def scores(n, q4, lo):
                        w = CHUNK - lo
                        for s_ in range(16):
                            tt, q = s_ // 4, s_ % 4
                            t.wait_ge(th_ready, n * 16 + s_ + 1)
                            for h in range(0, w, BANK):
                                e = min(w, h + BANK)
                                last = t.matmul(sp_[32 * q:32 * q + 32, q4, h:e], W2S[:, tt, :], TH[:, s_ % NR, h:e], start=tt == 0, stop=tt == 3, tile_position=(0, 32 * q))
                            last.then_inc(th_used, 1)
                            yield s_

                    def add_tile(n, q4, lo):
                        t.wait_ge(em_ready, n + 1)
                        t.wait_ge(ub_ready, n + 1)
                        for h in range(2):
                            s0 = max(lo, h * BANK)
                            if s0 < (h + 1) * BANK:
                                last = t.matmul(op[:, s0:(h + 1) * BANK], UBK[:, q4, :], ET[:, q4, s0 - lo:(h + 1) * BANK - lo], start=False, stop=False)
                        last.then_inc(o_done, 1)

                    for c in range(NCH):
                        first, full = plan(c)
                        n0 = b * TILES + first
                        t.wait_ge(ot_ready, b * NCH + c)
                        t.wait_ge(g_ready, b + 1)
                        for h in range(2):
                            t.matmul(op[:, h * BANK:(h + 1) * BANK], ZR[:, 0:P], ZR[:, :], start=True, stop=False)
                        if full:
                            with t.Fori(0, full, 4) as j:
                                for r in range(4):
                                    for s_ in scores(n0 + j + r, r % 2, 0):
                                        if s_ == 11 and r > 0:
                                            add_tile(n0 + j + r - 1, (r - 1) % 2, 0)
                                add_tile(n0 + j + 3, 1, 0)
                        for j in range(CT_):
                            for s_ in scores(n0 + full + j, j % 2, j * P):
                                if s_ == 11 and j > 0:
                                    add_tile(n0 + full + j - 1, (j - 1) % 2, (j - 1) * P)
                        add_tile(n0 + full + CT_ - 1, (CT_ - 1) % 2, (CT_ - 1) * P)
                        for h in range(2):
                            last = t.matmul(op[:, h * BANK:(h + 1) * BANK], ZR[:, 0:P], ZR[:, :], start=False, stop=True)
                        last.then_inc(o_ready, 1)
                        t.wait_ge(t_ready, (b * NCH + c) * 2)
                        for h in range(2):
                            last = t.matmul(dp[:, h, :], ONE[:, :], DEN[:, h * BANK:(h + 1) * BANK], start=True, stop=True)
                        last.then_inc(den_ready, 1)
                        t.wait_ge(ot_ready, b * NCH + c + 1)
                        for h in range(2):
                            for k in range(4):
                                last = t.transpose(dp[:, h, k * P:(k + 1) * P], OT[:, (4 * h + k) * P:(4 * h + k + 1) * P], C["ident"])
                            last.then_inc(ot_turned, 1)

            @block.vector
            def _(v):
                v.wait_ge(loaded, 16 * 33)
                for k in range(4):
                    v.tensor_scalar(W2S[:, k, :], C["pick"][:, 32 * k:32 * k + 32], W2C[:, 0:1], None, ALU.mult).then_inc(wready, 1)
                with v.Fori(0, NB) as b:
                    for q in range(8):
                        v.wait_ge(un_turned, b * 8 + q + 1)
                        v.tensor_copy(UT[:, q * BANK:(q + 1) * BANK], dp[:, q % 2, :]).then_inc(ut_ready, 1)
                    for q in range(8):
                        v.wait_ge(f_ready, b * 8 + q + 1)
                        v.tensor_copy(FR[:, q * BANK:(q + 1) * BANK], dp[:, q % 2, :]).then_inc(f_stored, 1)
                    v.wait_ge(g_sum, b + 1)
                    v.tensor_scalar(GB[:, :], dp[:, 0, :], B1C[:, 0:1], None, ALU.add).then_inc(g_ready, 1)

                    def sum_tile(n, q, lo):
                        v.tensor_tensor(DEN[:, lo:CHUNK], DEN[:, lo:CHUNK], ET[:, q, 0:CHUNK - lo], ALU.add).then_inc(em_ready, 1)

                    for c in range(NCH):
                        first, full = plan(c)
                        n0 = b * TILES + first
                        v.wait_ge(den_ready, b * NCH + c)
                        v.memset(DEN[:, :], 0.0).then_inc(den_zero, 1)
                        if full:
                            with v.Fori(0, full, 2) as j:
                                for r in range(2):
                                    v.wait_ge(den_zero, b * NCH + c + 1)
                                    v.wait_ge(e_ready, n0 + j + r + 1)
                                    v.wait_ge(em_ready, n0 + j + r)
                                    sum_tile(n0 + j + r, r, 0)
                        for j in range(CT_):
                            n = n0 + full + j
                            v.wait_ge(e_ready, n + 1)
                            v.wait_ge(em_ready, n)
                            v.wait_ge(den_zero, b * NCH + c + 1)
                            v.tensor_tensor(ET[:, j % 2, 0:P], ET[:, j % 2, 0:P], C["strict"], ALU.mult).then_inc(masked, 1)
                            v.wait_ge(masked, (b * NCH + c) * CT_ + j + 1)
                            sum_tile(n, j % 2, j * P)
                        v.wait_ge(den_ready, b * NCH + c + 1)
                        ch = Chain(v, dr_step, (b * NCH + c) * 2)
                        ch(v.tensor_scalar(DR[:, :], dp[:, :, :].rearrange("p a n -> p (a n)"), 1e-10, None, ALU.add))
                        ch(v.reciprocal(DR[:, :], DR[:, :]))
                        v.wait_ge(o_ready, b * NCH + c + 1)
                        v.tensor_tensor(OT[:, :], op[:, :], DR[:, :], ALU.mult).then_inc(ot_ready, 1)
                        for h in range(2):
                            at = b * L + c * CHUNK + h * BANK
                            v.wait_ge(ot_turned, (b * NCH + c) * 2 + h + 1)
                            v.tensor_tensor(T[:, bass.ds(at, BANK)], T[:, bass.ds(at, BANK)], dp[:, h, :], ALU.add).then_inc(t_ready, 1)
                            v.wait_ge(t_ready, (b * NCH + c) * 2 + h + 1)
                            for k in range(4):
                                last = v.bn_stats(N.stats[:, bass.ds((b * NT + c * CT_ + 4 * h + k) * 6, 6)], T[:, bass.ds(at + k * P, P)])
                            last.then_inc(st_ready, 1)
                v.wait_ge(st_ready, 2 * NB * NCH)
                N.vector(v, Chain(v, c2), vv, ss)


def to_channels(nc, T, C, out):
    with stage_semaphores(nc, "out_") as sem, ExitStack() as ctx:
        XB = ctx.enter_context(nc.sbuf_tensor("out_block", [P, 2, BANK], F32))
        tp = ctx.enter_context(nc.psum_tensor("out_psum", [P, 2, BANK], F32))
        copied, turned, stored, sent = (sem(n) for n in ("copied", "turned", "stored", "sent"))
        with nc.Block() as block:
            @block.gpsimd
            def _(pool):
                with pool.Fori(0, TT // 8) as i:
                    for r in range(2):
                        pool.wait_ge(turned, i * 2)
                        pool.tensor_copy(XB[:, r, :], T[:, bass.ds(i * 2 * BANK + r * BANK, BANK)]).then_inc(copied, 1)

            @block.tensor
            def _(t):
                with t.Fori(0, TT // 8) as i:
                    for r in range(2):
                        t.wait_ge(copied, i * 2 + r + 1)
                        t.wait_ge(stored, i * 2)
                        for k in range(4):
                            last = t.transpose(tp[:, r, k * P:(k + 1) * P], XB[:, r, k * P:(k + 1) * P], C["ident"])
                        last.then_inc(turned, 1)

            @block.vector
            def _(v):
                with v.Fori(0, TT // 8) as i:
                    for r in range(2):
                        v.wait_ge(turned, i * 2 + r + 1)
                        v.tensor_copy(T[:, bass.ds(i * 2 * BANK + r * BANK, BANK)], tp[:, r, :]).then_inc(stored, 1)

            @block.sync
            def _(sp):
                for b in range(NB):
                    sp.wait_ge(stored, (b + 1) * NT // 4)
                    sp.dma_start(out.rearrange("b c h w -> b c (h w)")[b], T[:, b * L:(b + 1) * L]).then_inc(sent, 16)
                sp.wait_ge(sent, 16 * NB)


STAGE = 9


def build(nc, d, out, offsets, stage=STAGE):
    with ExitStack() as ctx:
        X = ctx.enter_context(nc.sbuf_tensor("x_rows", [P, NB * L], F32))
        n_c = sum(n for _, n in offsets.values())
        CT = ctx.enter_context(nc.sbuf_tensor("consts_sb", [P, n_c], F32))
        C = {n: CT[:, o:o + w] for n, (o, w) in offsets.items()}
        C["all"] = CT[:, :]
        FLAG = ctx.enter_context(nc.sbuf_tensor("far_flag", [P, 1], I32))
        deform_layer(nc, d, X, C, True, FLAG[:, :])
        far = nc.values_load(FLAG[0:1, 0:1], min_val=0, max_val=1)
        with nc.If(far > 0):
            deform_layer(nc, d, X, C, False, None)
        if stage >= 1:
            mamba_layer(nc, d, X, C)
        if stage >= 2:
            N = Norm(lambda n, shape: ctx.enter_context(nc.sbuf_tensor(n, shape, F32)))
            to_tokens(nc, X, C, N)
            quantum_layer(nc, d, X, C, N)
        if stage >= 3:
            moe_layer(nc, d, X, C, N, "L2_ffn_", True)
        if stage >= 4:
            additive_attention_layer(nc, d, X, C, N)
        if stage >= 5:
            moe_layer(nc, d, X, C, N, "L3_ffn_", False)
        if stage >= 2:
            to_channels(nc, X, C, out)
        else:
            stored = ctx.enter_context(nc.semaphore("stored"))
            with nc.Block() as block:
                @block.sync
                def _(sp):
                    sp.dma_start(out.rearrange("b c h w -> c b (h w)"), X[:, :].rearrange("p (b n) -> p b n", b=NB)).then_inc(stored, 16)
                    sp.wait_ge(stored, 16)


def kernel(**inputs):
    import concourse.bacc as _bacc
    from concourse.bass_utils import run_bass_kernel_spmd as _run

    nc = _bacc.Bacc("TRN2", target_bir_lowering=False, num_devices=1)
    arrays, d = {}, {}
    parts = constants()
    offsets, at = {}, 0
    for n, a in parts.items():
        offsets[n] = (at, a.shape[1])
        at += a.shape[1]
    arrays["in_consts"] = np.concatenate(list(parts.values()), axis=1)
    for n, a in inputs.items():
        arrays["in_" + n] = np.ascontiguousarray(a)
    for n, a in arrays.items():
        d[n[3:]] = nc.dram_tensor(n, a.shape, F32, kind="ExternalInput").ap()
    out = nc.dram_tensor("out_x", inputs["x"].shape, F32, kind="ExternalOutput").ap()
    build(nc, d, out, offsets)
    r = _run(nc, [arrays], core_ids=[0])
    return r.results[0]["out_x"]
```

```python
from contextlib import ExitStack, contextmanager

import numpy as np
import concourse.bass as bass
from concourse import mybir

F32 = mybir.dt.float32
BF16 = mybir.dt.bfloat16
I32 = mybir.dt.int32
ACT = mybir.ActivationFunctionType
ALU = mybir.AluOpType
AX = mybir.AxisListType

P = 128
NB, HH, WW = 4, 64, 64
L = HH * WW
NT = L // P
BANK = 512
NEG = -1.0e30
G, K, OM = 8, 9, 32
REACH = HH - 1
NEAR = 3
NS = 2 * REACH + 1


def constants():
    p = np.arange(P)
    y_of = p // WW
    j = np.arange(NS + 2 * NT - 1)
    d = np.arange(NS) - REACH
    parts = {}
    parts["ident"] = np.eye(P)
    parts["gavg"] = (p[:, None] // 4 == p[None, :] // 4) * 0.25
    vx = ((p[:, None] % WW + d >= 0) & (p[:, None] % WW + d < WW)) * 1.0
    parts["vx"], parts["nvx"] = vx, -vx
    vy = y_of[:, None] + j[None, :] - REACH
    parts["vy"] = ((vy >= 0) & (vy < HH)) * 1.0
    parts["negd"] = np.broadcast_to(-d, (P, NS))
    c = np.arange(G * OM)
    k = (c % OM) // 2
    parts["koff"] = np.broadcast_to(np.where(c % OM < 2 * K, np.where(c % 2 == 0, k % 3 - 1, k // 3 - 1), 0), (P, G * OM))
    before = p[:, None] <= p[None, :]
    parts["tri_f"], parts["tri_b"] = before * 1.0, before.T * 1.0
    parts["neg_f"], parts["neg_b"] = np.where(before, 0, NEG), np.where(before.T, 0, NEG)
    parts["strict"] = (p[:, None] < p[None, :]) * 1.0
    parts["first"] = np.broadcast_to(8 - np.arange(8), (P, 8))
    w = np.arange(P)
    parts["pick"] = w[None, :] % 32 == (w[None, :] // 32) * 8 + p[:, None] // 16
    parts["eps5"] = np.full((P, 1), 1e-5)
    parts["quad"] = p[:, None] // 32 == np.arange(NB)
    return {n: np.asarray(a, np.float32) for n, a in parts.items()}


@contextmanager
def stage_semaphores(nc, tag):
    used = []

    def sem(name):
        used.append(nc.alloc_semaphore(tag + name))
        nc.gpsimd.sem_inc(used[-1], 1)
        return used[-1]

    yield sem
    nc.clear_and_free_semaphores(used)
    nc.all_engine_barrier()


class Chain:

    def __init__(self, eng, sem, base=0):
        self.eng, self.sem, self.base, self.n = eng, sem, base, 0

    def __call__(self, ins):
        ins.then_inc(self.sem, 1)
        self.n += 1
        self.eng.wait_ge(self.sem, 1 + self.base + self.n)


def deform_layer(nc, d, X, C, near, far_flag):
    tag = "near_" if near else "wide_"
    D0, D1 = (REACH - NEAR, REACH + NEAR + 1) if near else (0, NS)
    ND = D1 - D0
    UT = NT // 2
    UN = UT * P
    GK = G * K
    with stage_semaphores(nc, tag) as sem, ExitStack() as ctx:
        def sb(name, shape, dt=F32):
            return ctx.enter_context(nc.sbuf_tensor(tag + name, shape, dt))

        VP = sb("values_padded", [P, 3 * L])
        XN = sb("x_normed", [P, L])
        OMT = sb("offsets_masks", [P, NT * G * OM])
        om3 = OMT[:, :].rearrange("p (t c) -> p t c", t=NT)
        HY = sb("hat_y", [P, UT, G, K])
        HYM = sb("hat_y_mask_valid", [P, UT, G, K])
        AXX = sb("distance", [P, UT, G, K])
        AY = AXX
        HX = sb("hat_x", [P, 2, UT, G, K])
        PP = sb("tap_weights", [P, UT * G, K])
        HYP = PP[:, :, :].rearrange("p (t g) k -> p t g k", t=UT)
        W = sb("shift_weights", [P, UT * G])
        PR = sb("weighted_values", [P, UN])
        YB, SG = PR, XN[:, 0:UN]
        WW16 = XN[:, UN:2 * UN]
        WV, WO, WF = sb("w_value", [P, P]), sb("w_out", [P, P]), sb("w_off", [P, G * OM])
        BOFF = sb("b_off", [P, G * OM])
        COL = sb("columns", [P, 6])
        INV = sb("bn_scale", [P, 1])
        BB = sb("bn_shift", [P, 1])
        T1 = sb("t1", [P, 1])
        ST = sb("stats", [P, 8, 6])
        MV = sb("mean_var", [P, 2])
        RH = sb("group_in", [P, 2])
        MG = sb("group_mean", [P, 2])
        MM = sb("group_mean2", [P, 1])
        VE = sb("group_var", [P, 1])
        SD = sb("group_std", [P, 1])
        RS = sb("group_rstd", [P, 1])
        NBI = sb("group_shift", [P, 1])
        RMX = sb("reach_by_image", [P, NB])
        RM1 = sb("reach", [P, 1])
        RMA = sb("reach_all", [P, 1])
        ZR = sb("zeros", [P, BANK], BF16)
        wp = ctx.enter_context(nc.psum_tensor(tag + "weights_spread", [P, UN], F32))
        acc = ctx.enter_context(nc.psum_tensor(tag + "out_sum", [P, UN], F32))

        loaded, cleared, bn_ready = sem("loaded"), sem("cleared"), sem("bn_ready")
        rh_ready, gst_ready, ve_ready, sd_ready = sem("rh_ready"), sem("gst_ready"), sem("ve_ready"), sem("sd_ready")
        xn_ready, val_ready, val_stored = sem("xn_ready"), sem("val_ready"), sem("val_stored")
        offs_ready, om_stored, om_ready = sem("offs_ready"), sem("om_stored"), sem("om_ready")
        ay_ready, hy_ready, hyp_ready, hym_ready = sem("ay_ready"), sem("hy_ready"), sem("hyp_ready"), sem("hym_ready")
        ax_ready, hx_ready, pp_ready, w_ready = sem("ax_ready"), sem("hx_ready"), sem("pp_ready"), sem("w_ready")
        wide_ready = sem("wide_ready")
        spread, prod_ready, mm_done, unit_done = sem("spread"), sem("prod_ready"), sem("mm_done"), sem("unit_done")
        y_ready, sig_ready, ys_ready, x_done = sem("y_ready"), sem("sig_ready"), sem("ys_ready"), sem("x_done")
        prep, flag_sem = sem("vector_prep"), sem("flag")
        sq_ready, reach_ready, vector_end = sem("sq_ready"), sem("reach_ready"), sem("vector_end")
        block = ctx.enter_context(nc.Block())

        cols = ("b_value", "b_out", "bn_gamma", "bn_beta", "bn_mean", "bn_var")
        n_loads = 1 + 4 + len(cols) + (1 if near else 0)

        @block.sync
        def _(sp):
            sp.dma_start(X[:, :].rearrange("p (b n) -> p b n", b=NB), d["x"].rearrange("b c h w -> c b (h w)")).then_inc(loaded, 16)
            sp.dma_start(WV[:, :], d["L0_conv_w_value"]).then_inc(loaded, 16)
            sp.dma_start(WO[:, :], d["L0_conv_w_out"]).then_inc(loaded, 16)
            sp.dma_start(WF[:, :], d["L0_conv_w_off"]).then_inc(loaded, 16)
            sp.dma_start(BOFF[:, :], d["L0_conv_b_off"].partition_broadcast(P)).then_inc(loaded, 16)
            for i, n in enumerate(cols):
                sp.dma_start(COL[:, i:i + 1], d["L0_conv_" + n].rearrange("(c a) -> c a", a=1)).then_inc(loaded, 16)
            if near:
                sp.dma_start(C["all"], d["consts"]).then_inc(loaded, 16)
            sp.wait_ge(loaded, 1 + 16 * n_loads)

        @block.gpsimd
        def _(pool):
            pool.memset(VP[:, 0:L], 0.0).then_inc(cleared, 1)
            pool.memset(VP[:, 2 * L:3 * L], 0.0).then_inc(cleared, 1)
            pool.memset(ZR[:, :], 0.0).then_inc(cleared, 1)
            if near:
                pool.wait_ge(reach_ready, 1 + 1)
                pool.partition_all_reduce(RMA[:, :], RM1[:, :], P, bass.bass_isa.ReduceOp.max).then_inc(flag_sem, 1)

        @block.vector
        def _(v):
            v.wait_ge(loaded, 1 + 16 * n_loads)
            v.wait_ge(cleared, 1 + 3)
            one = Chain(v, bn_ready)
            v.tensor_tensor(BOFF[:, :], BOFF[:, :], C["koff"], ALU.add).then_inc(prep, 1)
            one(v.tensor_scalar(T1[:, :], COL[:, 5:6], 1e-5, None, ALU.add))
            v.wait_ge(sq_ready, 1 + 1)
            one(v.reciprocal(INV[:, :], SD[:, :]))
            one(v.tensor_tensor(INV[:, :], INV[:, :], COL[:, 2:3], ALU.mult))
            one(v.tensor_tensor(BB[:, :], COL[:, 1:2], COL[:, 4:5], ALU.subtract))
            one(v.scalar_tensor_tensor(BB[:, :], BB[:, :], INV[:, 0:1], COL[:, 3:4], ALU.mult, ALU.add))
            KP = 7
            with v.Fori(0, NB) as b:
                ch = Chain(v, prep, b * KP + 1)
                for i in range(8):
                    last = v.bn_stats(ST[:, i, :], X[:, bass.ds(b * L + i * BANK, BANK)])
                ch(last)
                v.tensor_copy(VE[:, :], T1[:, :])
                ch(v.bn_aggr(MV[:, :], ST[:, :, :].rearrange("p a s -> p (a s)")))
                v.tensor_copy(RH[:, 0:1], MV[:, 0:1])
                v.scalar_tensor_tensor(RH[:, 1:2], MV[:, 0:1], MV[:, 0:1], MV[:, 1:2], ALU.mult, ALU.add).then_inc(rh_ready, 1)
                v.wait_ge(gst_ready, 1 + b + 1)
                ch(v.tensor_copy(MG[:, :], wp[:, 0:2]))
                ch(v.tensor_tensor(MM[:, :], MG[:, 0:1], MG[:, 0:1], ALU.mult))
                v.scalar_tensor_tensor(VE[:, :], MG[:, 1:2], 1e-5, MM[:, :], ALU.add, ALU.subtract).then_inc(ve_ready, 1)
                v.wait_ge(sd_ready, 1 + b + 1)
                ch(v.reciprocal(RS[:, :], SD[:, :]))
                ch(v.scalar_tensor_tensor(NBI[:, :], MG[:, 0:1], -1.0, RS[:, :], ALU.mult, ALU.mult))
                v.tensor_scalar(XN[:, :], X[:, bass.ds(b * L, L)], RS[:, 0:1], NBI[:, 0:1], ALU.mult, ALU.add).then_inc(xn_ready, 1)
                for j in range(16):
                    v.wait_ge(offs_ready, 1 + b * 16 + j + 1)
                    v.tensor_tensor(om3[:, 2 * j:2 * j + 2, :], acc[:, (j % 4) * BANK:(j % 4 + 1) * BANK].rearrange("p (t c) -> p t c", t=2),
                                    BOFF[:, :].unsqueeze(1).to_broadcast([P, 2, G * OM]), ALU.add).then_inc(om_stored, 1)
                v.wait_ge(om_stored, 1 + b * 16 + 16)
                ch(v.tensor_reduce(RMX[:, bass.ds(b, 1)], OMT[:, :].rearrange("p (a c) -> p a c", c=OM)[:, :, 0:2 * K], AX.XY, ALU.max,
                                   apply_absolute_value=True))
                v.sem_inc(om_ready, 1)
                assert ch.n == KP
                with v.Fori(0, 2) as u:
                    U = b * 2 + u
                    with v.Fori(D0, D1) as dy:
                        DD = U * ND + dy - D0
                        v.wait_ge(val_stored, 1 + b * 8 + 8)
                        v.wait_ge(hy_ready, 1 + DD + 1)
                        v.tensor_tensor(HYP[:, :, :, :], HY[:, :, :, :], OMT[:, bass.ds(u * UT * G * OM, UT * G * OM)].rearrange("p (t g c) -> p t g c", t=UT, g=G)[:, :, :, 2 * K:3 * K], ALU.mult).then_inc(hyp_ready, 1)
                        v.wait_ge(hyp_ready, 1 + DD + 1)
                        v.tensor_tensor(HYM[:, :, :, :].rearrange("p t g k -> p t (g k)"), HYP[:, :, :, :].rearrange("p t g k -> p t (g k)"),
                                        C["vy"][:, bass.ds(u * 2 * UT + dy, 2 * UT)].rearrange("p (t two) -> p t two", two=2)[:, :, 0:1].to_broadcast([P, UT, GK]), ALU.mult).then_inc(hym_ready, 1)

                        def weigh(dx, r):
                            S = DD * ND + dx - D0
                            v.wait_ge(hym_ready, 1 + DD + 1)
                            v.wait_ge(hx_ready, 1 + S + 1)
                            v.wait_ge(w_ready, 1 + S)
                            v.tensor_tensor(PP[:, :, :].rearrange("p a k -> p (a k)"), HYM[:, :, :, :].rearrange("p t g k -> p (t g k)"), HX[:, r, :, :, :].rearrange("p t g k -> p (t g k)"), ALU.mult).then_inc(pp_ready, 1)
                            v.wait_ge(pp_ready, 1 + S + 1)
                            v.wait_ge(wide_ready, 1 + S * 2)
                            v.tensor_reduce(W[:, :], PP[:, :, :], AX.X, ALU.add).then_inc(w_ready, 1)

                        def multiply(dx):
                            S = DD * ND + dx - D0
                            for h in range(2):
                                v.wait_ge(spread, 1 + S * 2 + h + 1)
                                v.wait_ge(mm_done, 1 + S * 2 + h + 1)
                                v.tensor_tensor(PR[:, h * UN // 2:(h + 1) * UN // 2], wp[:, h * UN // 2:(h + 1) * UN // 2],
                                                VP[:, bass.ds(u * UN + dy * WW + dx + (L + h * UN // 2 - REACH * WW - REACH), UN // 2)], ALU.mult).then_inc(prod_ready, 1)

                        weigh(D0, 0)
                        with v.Fori(0, (ND - 1) // 2) as pair:
                            dx = D0 + pair * 2
                            for r in range(2):
                                weigh(dx + r + 1, (r + 1) % 2)
                                multiply(dx + r)
                        multiply(D1 - 1)
                    v.wait_ge(sig_ready, 1 + U + 1)
                    v.tensor_tensor(YB[:, :], YB[:, :], SG, ALU.mult).then_inc(ys_ready, 1)
                    v.wait_ge(ys_ready, 1 + U + 1)
                    v.tensor_tensor(X[:, bass.ds(b * L + u * UN, UN)], X[:, bass.ds(b * L + u * UN, UN)], YB[:, :], ALU.add).then_inc(x_done, 1)
            if near:
                end = Chain(v, vector_end)
                end(v.tensor_reduce(RM1[:, :], RMX[:, :], AX.X, ALU.max))
                v.sem_inc(reach_ready, 1)
                v.wait_ge(flag_sem, 1 + 1)
                end(v.tensor_scalar(RM1[:, :], RMA[:, :], float(NEAR), None, ALU.is_gt))
                end(v.tensor_copy(far_flag, RM1[:, :]))

        @block.scalar
        def _(a):
            a.wait_ge(bn_ready, 1 + 1)
            a.activation(SD[:, :], T1[:, :], ACT.Sqrt).then_inc(sq_ready, 1)
            a.wait_ge(bn_ready, 1 + 5)
            with a.Fori(0, NB) as b:
                a.wait_ge(ve_ready, 1 + b + 1)
                a.activation(SD[:, :], VE[:, :], ACT.Sqrt).then_inc(sd_ready, 1)
                for j in range(8):
                    a.wait_ge(val_ready, 1 + b * 8 + j + 1)
                    a.activation(VP[:, L + j * BANK:L + (j + 1) * BANK], wp[:, (j % 4) * BANK:(j % 4 + 1) * BANK], ACT.Identity, bias=COL[:, 0:1]).then_inc(val_stored, 1)
                a.wait_ge(om_ready, 1 + b + 1)
                with a.Fori(0, 2) as u:
                    U = b * 2 + u
                    taps = OMT[:, bass.ds(u * UT * G * OM, UT * G * OM)].rearrange("p (a c) -> p a c", c=OM)
                    with a.Fori(D0, D1) as dy:
                        DD = U * ND + dy - D0
                        a.wait_ge(hx_ready, 1 + DD * ND)
                        a.activation(AY[:, :, :, :].rearrange("p t g k -> p (t g) k"), taps[:, :, 1:2 * K:2], ACT.Abs, bias=C["negd"][:, bass.ds(dy, 1)]).then_inc(ay_ready, 1)
                        a.wait_ge(ay_ready, 1 + DD + 1)
                        a.wait_ge(hyp_ready, 1 + DD)
                        a.activation(HY[:, :, :, :], AY[:, :, :, :], ACT.Relu, bias=1.0, scale=-1.0).then_inc(hy_ready, 1)

                        def hat(dx, r, behind):
                            S = DD * ND + dx - D0
                            a.wait_ge(hx_ready, 1 + S)
                            a.activation(AXX[:, :, :, :].rearrange("p t g k -> p (t g) k"), taps[:, :, 0:2 * K:2], ACT.Abs, bias=C["negd"][:, bass.ds(dx, 1)]).then_inc(ax_ready, 1)
                            a.wait_ge(ax_ready, 1 + S + 1)
                            a.wait_ge(pp_ready, 1 + S - behind)
                            a.activation(HX[:, r, :, :, :], AXX[:, :, :, :], ACT.Relu, bias=C["vx"][:, bass.ds(dx, 1)], scale=C["nvx"][:, bass.ds(dx, 1)]).then_inc(hx_ready, 1)

                        def widen(dx):
                            S = DD * ND + dx - D0
                            a.wait_ge(w_ready, 1 + S + 1)
                            a.wait_ge(spread, 1 + S * 2)
                            for h in range(2):
                                a.activation(WW16[:, h * UN // 2:(h + 1) * UN // 2].rearrange("p (a r) -> p a r", r=P // G),
                                             W[:, h * P // 2:(h + 1) * P // 2].unsqueeze(2).to_broadcast([P, P // 2, P // G]), ACT.Copy).then_inc(wide_ready, 1)

                        a.wait_ge(hy_ready, 1 + DD + 1)
                        hat(D0, 0, 0)
                        with a.Fori(0, (ND - 1) // 2) as pair:
                            dx = D0 + pair * 2
                            for r in range(2):
                                hat(dx + r + 1, (r + 1) % 2, 1)
                                widen(dx + r)
                        widen(D1 - 1)
                    a.wait_ge(unit_done, 1 + U + 1)
                    a.wait_ge(x_done, 1 + U)
                    a.activation(YB[:, :], acc[:, :], ACT.Identity, bias=BB[:, 0:1], scale=INV[:, 0:1]).then_inc(y_ready, 1)
                    a.wait_ge(y_ready, 1 + U + 1)
                    a.activation(SG, YB[:, :], ACT.Sigmoid).then_inc(sig_ready, 1)

        @block.tensor
        def _(t):
            t.wait_ge(loaded, 1 + 16 * n_loads)
            t.wait_ge(cleared, 1 + 3)
            t.sem_inc(mm_done, 2)
            with t.Fori(0, NB) as b:
                t.wait_ge(rh_ready, 1 + b + 1)
                t.wait_ge(prod_ready, 1 + b * (4 * ND * ND))
                t.matmul(wp[:, 0:2], C["gavg"], RH[:, :], start=True, stop=True).then_inc(gst_ready, 1)
                t.wait_ge(xn_ready, 1 + b + 1)
                for j in range(8):
                    if j >= 4:
                        t.wait_ge(val_stored, 1 + b * 8 + j - 3)
                    t.matmul(wp[:, (j % 4) * BANK:(j % 4 + 1) * BANK], WV[:, :], XN[:, j * BANK:(j + 1) * BANK], start=True, stop=True).then_inc(val_ready, 1)
                t.wait_ge(y_ready, 1 + b * 2)
                for j in range(16):
                    if j >= 4:
                        t.wait_ge(om_stored, 1 + b * 16 + j - 3)
                    for i in range(2):
                        last = t.matmul(acc[:, (j % 4) * BANK + i * G * OM:(j % 4) * BANK + (i + 1) * G * OM], XN[:, (2 * j + i) * P:(2 * j + i + 1) * P], WF[:, :], start=True, stop=True)
                    last.then_inc(offs_ready, 1)
                with t.Fori(0, 2) as u:
                    U = b * 2 + u
                    t.wait_ge(om_stored, 1 + b * 16 + 16)
                    t.wait_ge(val_stored, 1 + b * 8 + 8)
                    t.wait_ge(y_ready, 1 + U)
                    for q in range(4):
                        t.matmul(acc[:, q * BANK:(q + 1) * BANK], ZR[:, 0:P], ZR[:, :], start=True, stop=False)
                    with t.Fori(D0, D1) as dy:
                        DD = U * ND + dy - D0

                        def spread_weights(dx, h):
                            S = DD * ND + dx - D0
                            t.wait_ge(wide_ready, 1 + S * 2 + h + 1)
                            for i in range(h * UT // 2, (h + 1) * UT // 2):
                                last = t.transpose(wp[:, i * P:(i + 1) * P], WW16[:, i * P:(i + 1) * P], C["ident"])
                            last.then_inc(spread, 1)

                        def add_products(dx, h):
                            S = DD * ND + dx - D0
                            for q in range(2 * h, 2 * h + 2):
                                last = t.matmul(acc[:, q * BANK:(q + 1) * BANK], WO[:, :], PR[:, q * BANK:(q + 1) * BANK], start=False, stop=False)
                            last.then_inc(mm_done, 1)

                        t.wait_ge(prod_ready, 1 + DD * ND * 2)
                        for h in range(2):
                            spread_weights(D0, h)
                        with t.Fori(0, (ND - 1) // 2) as pair:
                            dx = D0 + pair * 2
                            for r in range(2):
                                for h in range(2):
                                    t.wait_ge(prod_ready, 1 + (DD * ND + dx + r - D0) * 2 + h + 1)
                                    spread_weights(dx + r + 1, h)
                                    add_products(dx + r, h)
                        for h in range(2):
                            t.wait_ge(prod_ready, 1 + (DD * ND + ND - 1) * 2 + h + 1)
                            add_products(D1 - 1, h)
                    for q in range(4):
                        last = t.matmul(acc[:, q * BANK:(q + 1) * BANK], ZR[:, 0:P], ZR[:, :], start=False, stop=True)
                    last.then_inc(unit_done, 1)


DM, DI, DC = 32, 64, 4
ZW = 4 * DI
XO, BO, CO, ZO = 0, DI, 2 * DI, 3 * DI
NC = NT


def mamba_layer(nc, d, X, C):
    with stage_semaphores(nc, "l1_") as sem, ExitStack() as ctx:
        def sb(name, shape, dt=F32):
            return ctx.enter_context(nc.sbuf_tensor("l1_" + name, shape, dt))

        WP = WW + 2
        O1 = sb("lin1_padded", [P, (HH + 2) * WP])
        O1v = O1[:, :].rearrange("p (h w) -> p h w", w=WP)
        O2 = sb("conv_silu", [P, L])
        S4 = [sb("rows_fwd", [P, L + DC - 1]), sb("rows_bwd", [P, L + DC - 1])]
        S0 = [0, DC - 1]
        YST = O1[:, 0:L]
        YT = O2
        S2 = sb("scan_out", [P, L])
        LW, W4, FO = sb("lin1_w", [P, P]), sb("conv4_w", [P, P]), sb("fc_out_by_image", [P, NB, P])
        DG = sb("dw_diag", [P, 9, P])
        DW = sb("dw_w", [P, 9])
        FI = sb("fc_in_4", [P, DC, DM])
        WA = [sb("w_in_f", [P, ZW + 1]), sb("w_in_b", [P, ZW + 1])]
        CW = sb("conv_w", [P, 2, (ZW - DI) * DC])
        BI = sb("bias_rows", [P, 2, ZW])
        WOU = sb("w_out_4", [P, 4, DM])
        VEC = sb("vec", [P, 12])
        HB = sb("half_dw_b", [P, 1])
        NEA = sb("minus_exp_A", [P, 2])
        THB, VH = sb("tanh_rows", [P, 2, BANK]), sb("half_rows", [P, 2, BANK])
        DX, DE, DT, AV, NCS = (sb(n, [P, 2 * NC]) for n in ("dt_raw", "dt_exp", "dt", "decay_log", "minus_decay_sum"))
        LH, AB, XH, TH, ZS = (sb(n, [P, 2, w]) for n, w in (("rows_chunk", P), ("decay_wide", P), ("half_zxbc", ZW), ("tanh_zxbc", ZW), ("zxbc", ZW)))
        BT, CT, ECS, CE, HST = (sb(n, [DI, 2, w]) for n, w in (("B_T", P), ("C_T", P), ("decay_in", P), ("C_decayed", P), ("state", DI)))
        TM, LT, GL = (sb(n, [P, 2, P]) for n in ("decay_masked", "decay", "CB_decay"))
        BD, Y1 = sb("B_decayed", [P, 2, DI]), sb("y_plus_Dx", [P, 2, DI])
        MSQ, RST = sb("mean_square", [P, 2 * NC]), sb("rms_inv", [P, 2 * NC])
        ST = sb("stats", [P, NB * 8, 6])
        MV, SC, SH, RV = sb("bn_mean_var", [P, 2]), sb("bn_scale", [P, 1]), sb("bn_shift", [P, 1]), sb("bn_var_eps", [P, 1])
        ON, SG = sb("normed", [P, 2, BANK]), sb("gate", [P, 2, BANK])

        pa, pb = (ctx.enter_context(nc.psum_tensor("l1_p_" + n, [P, 2, BANK], F32)) for n in ("in", "scan"))
        dp = ctx.enter_context(nc.psum_tensor("l1_p_dt", [P, BANK], F32))
        zx, cr = ([pa[:, r, o:o + w] for r in range(2)] for o, w in ((0, ZW), (ZW, P)))
        btp, ctp, gp = ([pb[:, r, o:o + P] for r in range(2)] for o in (0, P, 2 * P))
        yp, hp = ([pb[:, r, o:o + DI] for r in range(2)] for o in (3 * P, 3 * P + DI))
        pf = ctx.enter_context(nc.psum_tensor("l1_p_front", [P, 2, BANK], F32))

        loaded, cleared, wprep, aprep = sem("loaded"), sem("cleared"), sem("weights_ready"), sem("A_ready")
        f_ready, f_used, o1_ready, th_front, vh_ready, o2_ready = (sem(n) for n in ("front_ready", "front_used", "o1_ready", "tanh_front", "half_front", "o2_ready"))
        s4a, s4v, dtp_ready, dx_ready, dab_ready, de_ready, ln_ready, dt_ready, av_ready, cs_ready, ncs_ready = (
            sem(n) for n in ("rows_by_scalar", "rows_by_vector", "dt_projected", "dt_biased", "dt_abs", "dt_exp", "dt_log", "dt_ready", "decay_log_ready", "decay_sum", "ncs_ready"))
        lh_ready, cr_ready, xh_ready, th_ready, zs_ready, bc_ready, bt_ready, g_ready, t_ready, lt_ready = (
            sem(n) for n in ("chunk_copied", "projected", "xh_ready", "tanh_ready", "zs_ready", "bc_transposed", "bc_ready", "g_ready", "masked", "decay_ready"))
        gl_ready, y_ready, h_ready, y1_ready, y2_ready = (sem(n) for n in ("gl_ready", "y_ready", "h_ready", "y1_ready", "y2_ready"))
        sq_ready, ms_ready, rln_ready, rs_ready, yn_ready, yt_ready, yt_stored, s2_ready, s2_stored = (
            sem(n) for n in ("squares", "mean_square_ready", "rms_log", "rms_ready", "y_normed", "y_T", "y_T_stored", "scan_projected", "scan_stored"))
        o_ready, st_ready, rv_ready, sd_ready, sc_ready, on_ready, o4_ready, sg_ready, x_done = (
            sem(n) for n in ("o_ready", "stats_ready", "bn_var", "bn_std", "bn_scale", "normed_ready", "conv4_ready", "gate_ready", "x_done"))

        block = ctx.enter_context(nc.Block())
        col = ("lin1_b", "dw_b", "bn_g", "bn_b", "conv4_b")
        n_loads = 2 + 1 + NB + DC + 2 * 3 * DC + 2 + 2 + DC * 2 + len(col) + 2 + 6

        def scan_at(dr, c):
            return c if dr == 0 else (NC - 1) - c

        @block.sync
        def _(sp):
            def load(dst, src):
                sp.dma_start(dst, src, allow_slow_non_contiguous=True).then_inc(loaded, 16)
            load(LW[:, :], d["L1_conv_lin1_w"])
            load(W4[:, :], d["L1_conv_conv4_w"])
            load(DW[:, :], d["L1_conv_dw_w"].rearrange("c a h w -> c (a h w)"))
            sp.wait_ge(cleared, 1 + 1)
            for b in range(NB):
                load(FO[32 * b:32 * b + 32, b, :], d["L1_conv_fc_out_w"])
            for j in range(DC):
                load(FI[:, j, :], d["L1_conv_fc_in_w"])
            for dr in range(2):
                for j in range(DC):
                    q, w_in = slice(32 * j, 32 * j + 32), d["L1_conv_mam_in_w"][dr]
                    load(WA[dr][q, XO:ZO], w_in[:, DI:ZW])
                    load(WA[dr][q, ZO:ZW], w_in[:, 0:DI])
                    load(WA[dr][q, ZW:ZW + 1], w_in[:, ZW:ZW + 1])
                load(CW[:, dr, :], d["L1_conv_mam_conv_w"][dr].rearrange("c j -> (c j)").partition_broadcast(P))
                load(BI[:, dr, XO:ZO], d["L1_conv_mam_conv_b"][dr].partition_broadcast(P))
                for j in range(DC):
                    load(WOU[DI * dr:DI * dr + DI, j, :], d["L1_conv_mam_out_w"][dr])
                load(VEC[DI * dr:DI * dr + DI, 5:6], d["L1_conv_mam_norm_w"][dr].rearrange("(c a) -> c a", a=1))
                load(VEC[:, 6 + dr:7 + dr], d["L1_conv_mam_dt_bias"][dr].partition_broadcast(P))
                load(VEC[:, 8 + dr:9 + dr], d["L1_conv_mam_A_log"][dr].partition_broadcast(P))
                load(VEC[:, 10 + dr:11 + dr], d["L1_conv_mam_D"][dr].partition_broadcast(P))
            for i, n in enumerate(col):
                load(VEC[:, i:i + 1], d["L1_conv_" + n].rearrange("(c a) -> c a", a=1))
            sp.wait_ge(loaded, 1 + 16 * n_loads)

        @block.gpsimd
        def _(pool):
            pool.memset(FO[:, :, :], 0.0).then_inc(cleared, 1)
            pool.memset(O1[:, :], 0.0).then_inc(cleared, 1)
            pool.memset(S2[:, :], 0.0).then_inc(cleared, 1)
            for dr in range(2):
                pool.memset(S4[dr][:, :], 0.0).then_inc(cleared, 1)
            pool.memset(BI[:, :, ZO:ZW], 0.0).then_inc(cleared, 1)
            with pool.Fori(0, NB) as b:
                with pool.Fori(0, NC) as c:
                    n = b * NC + c
                    pool.wait_ge(av_ready, 1 + b + 1)
                    pool.wait_ge(cr_ready, 1 + 2 * n)
                    for r in range(2):
                        at = scan_at(r, c)
                        pool.tensor_copy(LH[:, r, :], S4[r][:, bass.ds(S0[r] + at * P, P)])
                        pool.tensor_copy(AB[:, r, :], AV[:, bass.ds(r * NC + at, 1)].to_broadcast([P, P])).then_inc(lh_ready, 1)

        @block.vector
        def _(v):
            v.wait_ge(loaded, 1 + 16 * n_loads)
            v.wait_ge(cleared, 1 + 6)
            for k in range(9):
                v.tensor_scalar(DG[:, k, :], C["ident"], DW[:, k:k + 1], None, ALU.mult)
            for dr in range(2):
                for j in range(DC):
                    q = slice(32 * j, 32 * j + 32)
                    v.scalar_tensor_tensor(WA[dr][q, XO:ZO], WA[dr][q, XO:ZO], 0.5, CW[q, dr, :].rearrange("p (c j) -> p c j", j=DC)[:, :, j], ALU.mult, ALU.mult)
                    if j < DC - 1:
                        v.memset(WA[dr][q, ZO:ZW], 0.0)
                        v.memset(WA[dr][q, ZW:ZW + 1], 0.0)
                    else:
                        v.tensor_scalar(WA[dr][q, ZO:ZW], WA[dr][q, ZO:ZW], 0.5, None, ALU.mult)
            v.tensor_scalar(BI[:, :, :], BI[:, :, :], 0.5, None, ALU.mult)
            v.tensor_scalar(HB[:, :], VEC[:, 1:2], 0.5, None, ALU.mult).then_inc(wprep, 1)
            v.wait_ge(aprep, 1 + 1)
            v.tensor_scalar(NEA[:, :], NEA[:, :], -1.0, None, ALU.mult).then_inc(wprep, 1)
            v.wait_ge(wprep, 1 + 2)
            with v.Fori(0, NB) as b:
                for j in range(8):
                    v.wait_ge(f_ready, 1 + b * 24 + 8 + j + 1)
                    v.tensor_scalar(VH[:, j % 2, :], pf[:, j % 2, :], 0.5, HB[:, 0:1], ALU.mult, ALU.add).then_inc(vh_ready, 1)
                    v.wait_ge(th_front, 1 + b * 8 + j + 1)
                    v.scalar_tensor_tensor(O2[:, j * BANK:(j + 1) * BANK], THB[:, j % 2, :], 1.0, VH[:, j % 2, :], ALU.add, ALU.mult).then_inc(o2_ready, 1)
                for j in range(1, 8, 2):
                    v.wait_ge(f_ready, 1 + b * 24 + 16 + j + 1)
                    for i in range(DC):
                        for r, o in ((0, DC - 1 - i), (1, i)):
                            last = v.tensor_copy(S4[r][32 * i:32 * i + 32, j * BANK + o:(j + 1) * BANK + o], pf[32 * i:32 * i + 32, j % 2, :])
                    last.then_inc(s4v, 1)
                v.wait_ge(dtp_ready, 1 + b + 1)
                for r in range(2):
                    last = v.tensor_scalar(DX[:, r * NC:(r + 1) * NC], dp[:, r * NC:(r + 1) * NC], VEC[:, 6 + r:7 + r], None, ALU.add)
                last.then_inc(dx_ready, 1)
                v.wait_ge(ln_ready, 1 + b + 1)
                v.scalar_tensor_tensor(DT[:, :], DX[:, :], 0.0, DE[:, :], ALU.max, ALU.add).then_inc(dt_ready, 1)
                v.wait_ge(dt_ready, 1 + b + 1)
                for r in range(2):
                    last = v.tensor_scalar(AV[:, r * NC:(r + 1) * NC], DT[:, r * NC:(r + 1) * NC], NEA[:, r:r + 1], None, ALU.mult)
                last.then_inc(av_ready, 1)
                v.wait_ge(cs_ready, 1 + b + 1)
                v.tensor_scalar(NCS[:, :], dp[:, 2 * NC:4 * NC], -1.0, None, ALU.mult).then_inc(ncs_ready, 1)
                v.memset(HST[:, :, :], 0.0)
                with v.Fori(0, NC) as c:
                    n = 2 * (b * NC + c)
                    for r in range(2):
                        v.wait_ge(cr_ready, 1 + n + r + 1)
                        v.tensor_tensor(XH[:, r, :], zx[r], BI[:, r, :], ALU.add).then_inc(xh_ready, 1)
                    for r in range(2):
                        v.tensor_tensor(TM[:, r, :], cr[r], C["neg_" + "fb"[r]], ALU.add).then_inc(t_ready, 1)
                    for r in range(2):
                        v.wait_ge(th_ready, 1 + n + r + 1)
                        v.scalar_tensor_tensor(ZS[:, r, :], TH[:, r, :], 1.0, XH[:, r, :], ALU.add, ALU.mult).then_inc(zs_ready, 1)
                    for r in range(2):
                        last_t = P - 1 if r == 0 else 0
                        dt = DT[:, bass.ds(r * NC + scan_at(r, c), 1)]
                        v.wait_ge(g_ready, 1 + n + r + 1)
                        v.wait_ge(lt_ready, 1 + n + r + 1)
                        v.tensor_tensor(CE[:, r, :], CT[:, r, :], ECS[:, r, :], ALU.mult)
                        v.scalar_tensor_tensor(GL[:, r, :], gp[r], dt, LT[:, r, :], ALU.mult, ALU.mult)
                        v.tensor_scalar(BD[:, r, :], ZS[:, r, BO:CO], LT[:, r, last_t:last_t + 1], dt, ALU.mult, ALU.mult).then_inc(gl_ready, 1)
                    for r in range(2):
                        last_t = P - 1 if r == 0 else 0
                        v.wait_ge(y_ready, 1 + n + r + 1)
                        v.scalar_tensor_tensor(HST[:, r, :], HST[:, r, :], ECS[:, r, last_t:last_t + 1], hp[r][0:DI, :], ALU.mult, ALU.add).then_inc(h_ready, 1)
                        v.scalar_tensor_tensor(Y1[:, r, :], ZS[:, r, XO:BO], VEC[:, 10 + r:11 + r], yp[r], ALU.mult, ALU.add).then_inc(y1_ready, 1)
                    for r in range(2):
                        v.wait_ge(y1_ready, 1 + n + r + 1)
                        v.tensor_tensor(YST[:, bass.ds(scan_at(r, c) * P + r * DI, DI)], Y1[:, r, :], ZS[:, r, ZO:ZW], ALU.mult).then_inc(y2_ready, 1)
                v.wait_ge(sq_ready, 1 + b + 1)
                v.tensor_reduce(MSQ[:, :], O2[:, :].rearrange("p (a k) -> p a k", k=DI), AX.X, ALU.add).then_inc(ms_ready, 1)
                v.wait_ge(rs_ready, 1 + b + 1)
                v.tensor_tensor(YST.rearrange("p (a k) -> p a k", k=DI), YST.rearrange("p (a k) -> p a k", k=DI), RST[:, :].unsqueeze(2).to_broadcast([P, 2 * NC, DI]), ALU.mult).then_inc(yn_ready, 1)
                for j in range(8):
                    v.wait_ge(yt_ready, 1 + b * 8 + j + 1)
                    v.tensor_scalar(YT[:, j * BANK:(j + 1) * BANK], pf[:, j % 2, :], VEC[:, 5:6], None, ALU.mult).then_inc(yt_stored, 1)
                for j in range(8):
                    v.wait_ge(s2_ready, 1 + b * 8 + j + 1)
                    v.scalar_tensor_tensor(S2[:, j * BANK:(j + 1) * BANK], pf[:, j % 2, :], C["quad"][:, bass.ds(b, 1)], S2[:, j * BANK:(j + 1) * BANK], ALU.mult, ALU.add).then_inc(s2_stored, 1)
                v.wait_ge(yt_ready, 1 + b * 8 + 8)
                v.memset(O1[:, 0:L], 0.0).then_inc(x_done, 1)
            for i in range(NB * 8):
                v.wait_ge(o_ready, 1 + i + 1)
                v.bn_stats(ST[:, i, :], pf[:, i % 2, :]).then_inc(st_ready, 1)
            ch = Chain(v, st_ready, NB * 8)
            v.wait_ge(st_ready, 1 + NB * 8)
            ch(v.bn_aggr(MV[:, :], ST[:, :, :].rearrange("p a s -> p (a s)")))
            v.tensor_scalar(RV[:, :], MV[:, 1:2], 1e-5, None, ALU.add).then_inc(rv_ready, 1)
            v.wait_ge(sd_ready, 1 + 1)
            ch(v.reciprocal(SC[:, :], RV[:, :]))
            ch(v.tensor_tensor(SC[:, :], SC[:, :], VEC[:, 2:3], ALU.mult))
            ch(v.tensor_tensor(SH[:, :], SC[:, :], MV[:, 0:1], ALU.mult))
            v.tensor_tensor(SH[:, :], VEC[:, 3:4], SH[:, :], ALU.subtract).then_inc(sc_ready, 1)
            for i in range(NB * 8):
                v.wait_ge(sg_ready, 1 + i + 1)
                v.scalar_tensor_tensor(X[:, i * BANK:(i + 1) * BANK], SG[:, i % 2, :], 1.0, X[:, i * BANK:(i + 1) * BANK], ALU.add, ALU.mult).then_inc(x_done, 1)

        @block.scalar
        def _(a):
            a.wait_ge(loaded, 1 + 16 * n_loads)
            a.activation(NEA[:, :], VEC[:, 8:10], ACT.Exp).then_inc(aprep, 1)
            a.wait_ge(wprep, 1 + 2)
            with a.Fori(0, NB) as b:
                for j in range(8):
                    a.wait_ge(f_ready, 1 + b * 24 + j + 1)
                    a.activation(O1v[:, 1 + 8 * j:9 + 8 * j, 1:WW + 1], pf[:, j % 2, :].rearrange("p (h w) -> p h w", w=WW), ACT.Identity, bias=VEC[:, 0:1]).then_inc(o1_ready, 1)
                for j in range(8):
                    a.wait_ge(vh_ready, 1 + b * 8 + j + 1)
                    a.activation(THB[:, j % 2, :], VH[:, j % 2, :], ACT.Tanh).then_inc(th_front, 1)
                for j in range(0, 8, 2):
                    a.wait_ge(f_ready, 1 + b * 24 + 16 + j + 1)
                    for i in range(DC):
                        for r, o in ((0, DC - 1 - i), (1, i)):
                            last = a.activation(S4[r][32 * i:32 * i + 32, j * BANK + o:(j + 1) * BANK + o], pf[32 * i:32 * i + 32, j % 2, :], ACT.Copy)
                    last.then_inc(s4a, 1)
                a.wait_ge(dx_ready, 1 + b + 1)
                a.activation(DE[:, :], DX[:, :], ACT.Abs).then_inc(dab_ready, 1)
                a.wait_ge(dab_ready, 1 + b + 1)
                a.activation(DE[:, :], DE[:, :], ACT.Exp, scale=-1.0).then_inc(de_ready, 1)
                a.wait_ge(de_ready, 1 + b + 1)
                a.activation(DE[:, :], DE[:, :], ACT.Ln, bias=1.0).then_inc(ln_ready, 1)
                a.wait_ge(ncs_ready, 1 + b + 1)
                a.activation(RST[:, 0:1], NCS[:, 0:1], ACT.Tanh)
                with a.Fori(0, NC) as c:
                    n = 2 * (b * NC + c)
                    for r in range(2):
                        a.wait_ge(xh_ready, 1 + n + r + 1)
                        a.activation(TH[:, r, :], XH[:, r, :], ACT.Tanh).then_inc(th_ready, 1)
                    for r in range(2):
                        a.wait_ge(t_ready, 1 + n + r + 1)
                        a.activation(LT[:, r, :], TM[:, r, :], ACT.Exp, bias=NCS[:, bass.ds(r * NC + scan_at(r, c), 1)])
                        a.activation(ECS[:, r, :], cr[r][0:DI, :], ACT.Exp).then_inc(lt_ready, 1)
                    for r in range(2):
                        a.wait_ge(bc_ready, 1 + n + r + 1)
                        a.activation(BT[:, r, :], btp[r][0:DI, :], ACT.Copy)
                        a.activation(CT[:, r, :], ctp[r][0:DI, :], ACT.Copy).then_inc(bt_ready, 1)
                a.wait_ge(y2_ready, 1 + (b + 1) * 2 * NC)
                a.activation(O2[:, :], YST, ACT.Square).then_inc(sq_ready, 1)
                a.wait_ge(ms_ready, 1 + b + 1)
                a.activation(MSQ[:, :], MSQ[:, :], ACT.Ln, bias=C["eps5"], scale=1.0 / DI).then_inc(rln_ready, 1)
                a.wait_ge(rln_ready, 1 + b + 1)
                a.activation(RST[:, :], MSQ[:, :], ACT.Exp, scale=-0.5).then_inc(rs_ready, 1)
            a.wait_ge(rv_ready, 1 + 1)
            a.activation(RV[:, :], RV[:, :], ACT.Sqrt).then_inc(sd_ready, 1)
            a.wait_ge(sc_ready, 1 + 1)
            for i in range(NB * 8 + 1):
                if i < NB * 8:
                    a.wait_ge(o_ready, 1 + NB * 8 + i + 1)
                    if i >= 2:
                        a.wait_ge(o4_ready, 1 + i - 1)
                    a.activation(ON[:, i % 2, :], pf[:, i % 2, :], ACT.Identity, bias=SH[:, 0:1], scale=SC[:, 0:1]).then_inc(on_ready, 1)
                if i > 0:
                    k = i - 1
                    a.wait_ge(o4_ready, 1 + k + 1)
                    if k >= 2:
                        a.wait_ge(x_done, 1 + NB + k - 1)
                    a.activation(SG[:, k % 2, :], pa[:, k % 2, :], ACT.Sigmoid, bias=VEC[:, 4:5]).then_inc(sg_ready, 1)

        @block.tensor
        def _(t):
            t.wait_ge(loaded, 1 + 16 * n_loads)
            t.wait_ge(wprep, 1 + 2)
            with t.Fori(0, NB) as b:
                for j in range(8):
                    if j >= 2:
                        t.wait_ge(o1_ready, 1 + b * 8 + j - 1)
                    if j == 0:
                        t.wait_ge(x_done, 1 + b)
                    t.matmul(pf[:, j % 2, :], LW[:, :], X[:, bass.ds(b * L + j * BANK, BANK)], start=True, stop=True).then_inc(f_ready, 1)
                for j in range(8):
                    if j == 0:
                        t.wait_ge(o1_ready, 1 + b * 8 + 8)
                    if j >= 2:
                        t.wait_ge(o2_ready, 1 + b * 8 + j - 1)
                    for k in range(9):
                        last = t.matmul(pf[:, j % 2, :], DG[:, k, :], O1v[:, 8 * j + k // 3:8 * j + k // 3 + 8, k % 3:k % 3 + WW], start=k == 0, stop=k == 8)
                    last.then_inc(f_ready, 1)
                for j in range(8):
                    if j < 2:
                        t.wait_ge(o2_ready, 1 + b * 8 + 8)
                    else:
                        t.wait_ge(s4v if j % 2 else s4a, 1 + b * 4 + j // 2)
                    t.matmul(pf[:, j % 2, :], FI[:, :, :].rearrange("p a b -> p (a b)"), O2[:, j * BANK:(j + 1) * BANK], start=True, stop=True).then_inc(f_ready, 1)
                t.wait_ge(s4a, 1 + b * 4 + 4)
                t.wait_ge(s4v, 1 + b * 4 + 4)
                for r in range(2):
                    for c in range(NC):
                        last = t.matmul(dp[:, r * NC + c:r * NC + c + 1], S4[r][:, S0[r] + c * P:S0[r] + (c + 1) * P], WA[r][:, ZW:ZW + 1], start=True, stop=True)
                last.then_inc(dtp_ready, 1)
                t.wait_ge(av_ready, 1 + b + 1)
                for r in range(2):
                    last = t.matmul(dp[:, (2 + r) * NC:(3 + r) * NC], C["tri_" + "fb"[r]], AV[:, r * NC:(r + 1) * NC], start=True, stop=True)
                last.then_inc(cs_ready, 1)
                with t.Fori(0, NC) as c:
                    n = 2 * (b * NC + c)
                    for r in range(2):
                        t.wait_ge(lh_ready, 1 + n + r + 1)
                        t.matmul(zx[r], LH[:, r, :], WA[r][:, 0:ZW], start=True, stop=True)
                        t.matmul(cr[r], AB[:, r, :], C["tri_" + "fb"[r]], start=True, stop=True).then_inc(cr_ready, 1)
                    for r in range(2):
                        t.wait_ge(zs_ready, 1 + n + r + 1)
                        t.transpose(btp[r], ZS[:, r, BO:BO + P], C["ident"])
                        t.transpose(ctp[r], ZS[:, r, CO:CO + P], C["ident"]).then_inc(bc_ready, 1)
                    for r in range(2):
                        t.wait_ge(bt_ready, 1 + n + r + 1)
                        t.matmul(gp[r], BT[:, r, :], CT[:, r, :], start=True, stop=True).then_inc(g_ready, 1)
                    for r in range(2):
                        t.wait_ge(gl_ready, 1 + n + r + 1)
                        t.wait_ge(h_ready, 1 + n)
                        t.matmul(yp[r], GL[:, r, :], ZS[:, r, XO:BO], start=True, stop=False)
                        t.matmul(yp[r], CE[:, r, :], HST[:, r, :], start=False, stop=True)
                        t.matmul(hp[r][0:DI, :], BD[:, r, :], ZS[:, r, XO:BO], start=True, stop=True).then_inc(y_ready, 1)
                for j in range(8):
                    if j < 2:
                        t.wait_ge(yn_ready, 1 + b + 1)
                    else:
                        t.wait_ge(yt_stored, 1 + b * 8 + j - 1)
                    for i in range(4):
                        last = t.transpose(pf[:, j % 2, i * P:(i + 1) * P], YST[:, (4 * j + i) * P:(4 * j + i + 1) * P], C["ident"])
                    last.then_inc(yt_ready, 1)
                for j in range(8):
                    if j < 2:
                        t.wait_ge(yt_stored, 1 + b * 8 + 8)
                    else:
                        t.wait_ge(s2_stored, 1 + b * 8 + j - 1)
                    t.matmul(pf[:, j % 2, :], WOU[:, :, :].rearrange("p a b -> p (a b)"), YT[:, j * BANK:(j + 1) * BANK], start=True, stop=True).then_inc(s2_ready, 1)
            t.wait_ge(s2_stored, 1 + NB * 8)
            for turn in range(2):
                for i in range(NB * 8):
                    if turn == 0 and i >= 2:
                        t.wait_ge(st_ready, 1 + i - 1)
                    if turn == 1:
                        t.wait_ge(sc_ready, 1 + 1)
                        if i >= 2:
                            t.wait_ge(on_ready, 1 + i - 1)
                    t.matmul(pf[:, i % 2, :], FO[:, i // 8, :], S2[:, (i % 8) * BANK:(i % 8 + 1) * BANK], start=True, stop=True).then_inc(o_ready, 1)
                    if turn == 1:
                        if i >= 2:
                            t.wait_ge(sg_ready, 1 + i - 1)
                        t.wait_ge(on_ready, 1 + i + 1)
                        t.matmul(pa[:, i % 2, :], W4[:, :], ON[:, i % 2, :], start=True, stop=True).then_inc(o4_ready, 1)


TT = NB * NT
GT = 8
GW = GT * P
NG = TT // GT
INV2PI, TWOPI = float(1.0 / (2.0 * np.pi)), 6.283185
ROUND = 1.5 * 2.0 ** 23


class Norm:

    def __init__(self, sb):
        self.stats = sb("norm_stats", [P, TT * 6])
        self.mean2, self.diff, self.var, self.std, self.scale, self.shift = (
            sb("norm_" + n, [P, TT]) for n in ("mean2", "diff", "var", "std", "scale", "shift"))

    def vector(self, v, ch, var_ready, std_ready, eps=1e-5, turn=1):
        st = self.stats[:, :].rearrange("p (t s) -> p t s", s=6)
        ch(v.tensor_tensor(self.mean2[:, :], st[:, :, 1], st[:, :, 4], ALU.add))
        ch(v.tensor_tensor(self.diff[:, :], st[:, :, 1], st[:, :, 4], ALU.subtract))
        ch(v.tensor_tensor(self.var[:, :], st[:, :, 2], st[:, :, 5], ALU.add))
        ch(v.tensor_tensor(self.diff[:, :], self.diff[:, :], self.diff[:, :], ALU.mult))
        ch(v.tensor_scalar(self.var[:, :], self.var[:, :], 1.0 / P, eps, ALU.mult, ALU.add))
        v.scalar_tensor_tensor(self.var[:, :], self.diff[:, :], 0.25, self.var[:, :], ALU.mult, ALU.add).then_inc(var_ready, 1)
        v.wait_ge(std_ready, 1 + turn)
        ch(v.reciprocal(self.scale[:, :], self.std[:, :]))
        ch(v.scalar_tensor_tensor(self.shift[:, :], self.mean2[:, :], -0.5, self.scale[:, :], ALU.mult, ALU.mult))

    def scalar(self, a, var_ready, std_ready, turn=1):
        a.wait_ge(var_ready, 1 + turn)
        a.activation(self.std[:, :], self.var[:, :], ACT.Sqrt).then_inc(std_ready, 1)

    def apply(self, a, dst, src, tile, k):
        return a.activation(dst, src, ACT.Identity, bias=self.shift[:, bass.ds(tile + k, 1)], scale=self.scale[:, bass.ds(tile + k, 1)])


def to_tokens(nc, T, C, N):
    with stage_semaphores(nc, "tr_") as sem, ExitStack() as ctx:
        XB = ctx.enter_context(nc.sbuf_tensor("tr_block", [P, 2, BANK], F32))
        tp = ctx.enter_context(nc.psum_tensor("tr_psum", [P, 2, BANK], F32))
        copied, turned, stored, chain, var_ready, std_ready = (sem(n) for n in ("copied", "turned", "stored", "vector", "var", "std"))
        with nc.Block() as block:
            @block.gpsimd
            def _(pool):
                with pool.Fori(0, TT // 8) as i:
                    for r in range(2):
                        pool.wait_ge(turned, 1 + i * 2)
                        pool.tensor_copy(XB[:, r, :], T[:, bass.ds(i * 2 * BANK + r * BANK, BANK)]).then_inc(copied, 1)

            @block.tensor
            def _(t):
                with t.Fori(0, TT // 8) as i:
                    for r in range(2):
                        t.wait_ge(copied, 1 + i * 2 + r + 1)
                        t.wait_ge(stored, 1 + i * 2)
                        for k in range(4):
                            last = t.transpose(tp[:, r, k * P:(k + 1) * P], XB[:, r, k * P:(k + 1) * P], C["ident"])
                        last.then_inc(turned, 1)

            @block.vector
            def _(v):
                with v.Fori(0, TT // 8) as i:
                    for r in range(2):
                        v.wait_ge(turned, 1 + i * 2 + r + 1)
                        for k in range(4):
                            v.bn_stats(N.stats[:, bass.ds((i * 8 + r * 4 + k) * 6, 6)], tp[:, r, k * P:(k + 1) * P])
                        v.tensor_copy(T[:, bass.ds(i * 2 * BANK + r * BANK, BANK)], tp[:, r, :]).then_inc(stored, 1)
                v.wait_ge(stored, 1 + TT // 4)
                N.vector(v, Chain(v, chain), var_ready, std_ready)

            @block.scalar
            def _(a):
                N.scalar(a, var_ready, std_ready)


def quantum_layer(nc, d, T, C, N):
    nf = 2048 // P
    with stage_semaphores(nc, "qa_") as sem, ExitStack() as ctx:
        def sb(name, shape, dt=F32):
            return ctx.enter_context(nc.sbuf_tensor("qa_" + name, shape, dt))

        V = sb("x1", [P, TT * P])
        Q9 = sb("q_and_one", [P, TT * 9 + 36])
        q9 = Q9[:, 0:TT * 9].rearrange("p (t k) -> p t k", k=9)
        U, A, KR, CS = (sb(n, [P, 2, GW]) for n in ("normed", "angle", "turns", "cosine"))
        QT = sb("q_T", [P, 2, BANK])
        W1S, W1T = sb("w1_b1", [P, nf, 32]), sb("w1_T", [P, nf // 4, P])
        W2S, W2T = V[:, 0:nf * P], sb("w2_T", [P, nf, P])
        FS = A
        TH8, PH8, CP8, PK8 = (sb(n, [P, 8]) for n in ("theta", "phi", "cos_phi", "phi_turns"))
        G1, B1, G2, B2R = (sb(n, [P, P]) for n in ("gamma1", "beta1", "gamma2", "beta2"))
        B2 = sb("b2", [P, 1])
        QS = sb("q_block", [P, 2, 4, 4, 32])
        hp = ctx.enter_context(nc.psum_tensor("qa_hidden", [P, 4, BANK], F32))
        fo = ctx.enter_context(nc.psum_tensor("qa_out", [P, 2, BANK], F32))
        qp, fp = (ctx.enter_context(nc.psum_tensor("qa_" + n, [P, BANK], F32)) for n in ("q_turned", "out_turned"))
        cleared, loaded, w_turned, w_stored, weights_ready = sem("cleared"), sem("loaded"), sem("w_turned"), sem("w_stored"), sem("weights_ready")

        with nc.Block() as block:
            @block.sync
            def _(sp):
                def load(dst, src):
                    sp.dma_start(dst, src, allow_slow_non_contiguous=True).then_inc(loaded, 16)
                load(W2S, d["L2_attn_w2"])
                sp.wait_ge(cleared, 1 + 1)
                load(W1S[:, :, 0:8], d["L2_attn_w1"].rearrange("(n p) k -> p n k", p=P))
                load(W1S[:, :, 8:9], d["L2_attn_b1"].rearrange("(n p a) -> p n a", p=P, a=1))
                load(B2[:, :], d["L2_attn_b2"].rearrange("(c a) -> c a", a=1))
                load(TH8[:, :], d["L2_attn_theta_attn"].partition_broadcast(P))
                load(PH8[:, :], d["L2_attn_phi_ffn"].partition_broadcast(P))
                for dst, n in ((G1, "gamma1"), (B1, "beta1"), (G2, "gamma2"), (B2R, "beta2")):
                    load(dst[:, :], d["L2_attn_" + n].partition_broadcast(P))
                sp.wait_ge(loaded, 1 + 160)

            @block.gpsimd
            def _(pool):
                pool.memset(W1S[:, :, :], 0.0).then_inc(cleared, 1)
                pool.memset(Q9[:, TT * 9:], 0.0).then_inc(cleared, 1)
                pool.memset(QS[:, :, :, :, :], 0.0).then_inc(cleared, 1)

            @block.tensor
            def _(t):
                t.wait_ge(loaded, 1 + 160)
                for i in range(nf // 4):
                    if i >= 2:
                        t.wait_ge(w_stored, 1 + 2 * (i - 1))
                    for k in range(4):
                        t.transpose(hp[:, i % 2, k * P:(k + 1) * P], W2S[:, (4 * i + k) * P:(4 * i + k + 1) * P], C["ident"])
                    last = t.transpose(hp[:, 2 + i % 2, 0:P], W1S[:, 4 * i:4 * i + 4, :].rearrange("p a b -> p (a b)"), C["ident"])
                    last.then_inc(w_turned, 1)

            @block.vector
            def _(v):
                v.wait_ge(loaded, 1 + 160)
                ch = Chain(v, weights_ready)
                v.tensor_scalar(TH8[:, :], TH8[:, :], INV2PI, 0.25, ALU.mult, ALU.add)
                ch(v.tensor_scalar(PH8[:, :], PH8[:, :], INV2PI, 0.25, ALU.mult, ALU.add))
                ch(v.tensor_scalar(PK8[:, :], PH8[:, :], ROUND, ROUND, ALU.add, ALU.subtract))
                ch(v.tensor_tensor(PH8[:, :], PH8[:, :], PK8[:, :], ALU.subtract))
                v.memset(q9[:, :, 8:9], 1.0)
                for i in range(nf // 4):
                    v.wait_ge(w_turned, 1 + i + 1)
                    v.tensor_copy(W2T[:, 4 * i:4 * i + 4, :].rearrange("p a b -> p (a b)"), hp[:, i % 2, :]).then_inc(w_stored, 1)
                    v.tensor_copy(W1T[:, i, :], hp[:, 2 + i % 2, 0:P]).then_inc(w_stored, 1)

            @block.scalar
            def _(a):
                a.wait_ge(weights_ready, 1 + 3)
                a.activation(CP8[:, :], PH8[:, :], ACT.Sin, scale=TWOPI)

        u_ready, r_ready, cs_ready, cp_ready, cp_step, v_ready, chain, va, sa = (
            sem(n) for n in ("u_ready", "angle_ready", "cosine_ready", "products_ready", "product_step", "v_ready", "vector_angle", "var1", "std1"))
        c2, c2s = sem("vector_norm1"), sem("v_sum")

        with nc.Block() as block:
            @block.scalar
            def _(a):
                a.activation(CS[:, 0, 0:1], CP8[:, 0:1], ACT.Sin)
                with a.Fori(0, NG // 2) as i:
                    for r in range(2):
                        a.wait_ge(v_ready, 1 + 1 + i * 2 + r)
                        for k in range(GT):
                            last = N.apply(a, U[:, r, k * P:(k + 1) * P], T[:, bass.ds((i * 2 + r) * GW + k * P, P)], (i * 2 + r) * GT, k)
                        last.then_inc(u_ready, 1)
                    for r in range(2):
                        a.wait_ge(r_ready, 1 + i * 2 + r + 1)
                        a.activation(CS[:, r, :], A[:, r, :], ACT.Sin, scale=TWOPI).then_inc(cs_ready, 1)
                N.scalar(a, va, sa)

            @block.gpsimd
            def _(pool):
                with pool.Fori(0, NG // 2) as i:
                    for r in range(2):
                        pool.wait_ge(cs_ready, 1 + i * 2 + r + 1)
                        c = CS[:, r, :].rearrange("p (a k) -> p a k", k=8)
                        for k in range(1, 8):
                            last = pool.tensor_tensor(c[:, :, k], c[:, :, k], c[:, :, k - 1], ALU.mult)
                            if k < 7:
                                last.then_inc(cp_step, 1)
                                pool.wait_ge(cp_step, 1 + (i * 2 + r) * 6 + k)
                        last.then_inc(cp_ready, 1)

            @block.vector
            def _(v):
                v.sem_inc(v_ready, 2)
                with v.Fori(0, NG // 2) as i:
                    ch = Chain(v, chain, i * 4)
                    for r in range(2):
                        v.wait_ge(u_ready, 1 + i * 2 + r + 1)
                        ch(v.scalar_tensor_tensor(A[:, r, :].rearrange("p (a k) -> p a k", k=8), U[:, r, :].rearrange("p (a k) -> p a k", k=8), INV2PI,
                                                  TH8[:, :].unsqueeze(1).to_broadcast([P, GW // 8, 8]), ALU.mult, ALU.add))
                        ch(v.tensor_scalar(KR[:, r, :], A[:, r, :], ROUND, ROUND, ALU.add, ALU.subtract))
                        v.tensor_tensor(A[:, r, :], A[:, r, :], KR[:, r, :], ALU.subtract).then_inc(r_ready, 1)
                    for r in range(2):
                        n = i * 2 + r
                        v.wait_ge(cp_ready, 1 + n + 1)
                        u, c = (z[:, r, :].rearrange("p (a k) -> p a k", k=8) for z in (U, CS))
                        w = V[:, bass.ds(n * GW, GW)].rearrange("p (a k) -> p a k", k=8)
                        v.tensor_tensor(w[:, :, 0:1], u[:, :, 0:1], c[:, :, 7:8], ALU.add)
                        v.tensor_tensor(w[:, :, 1:8], u[:, :, 1:8], c[:, :, 1:8], ALU.add).then_inc(c2s, 1)
                        v.wait_ge(c2s, 1 + n + 1)
                        for k in range(GT):
                            last = v.bn_stats(N.stats[:, bass.ds((n * GT + k) * 6, 6)], V[:, bass.ds(n * GW + k * P, P)])
                        last.then_inc(v_ready, 1)
                v.wait_ge(v_ready, 1 + 2 + NG)
                N.vector(v, Chain(v, c2), va, sa)

        w_ready, x1_ready, g_step, qr, qk, qs_ready = (sem(n) for n in ("w_ready", "x1_ready", "scaled", "q_angle", "q_turns", "q_sine"))
        CQ, KQ = CS[:, :, :].rearrange("p a n -> p (a n)")[:, 0:TT * 8], A[:, :, :].rearrange("p a n -> p (a n)")[:, 0:TT * 8]

        with nc.Block() as block:
            @block.scalar
            def _(a):
                with a.Fori(0, NG // 2) as i:
                    for r in range(2):
                        a.wait_ge(x1_ready, 1 + 1 + i * 2 + r)
                        for k in range(GT):
                            last = N.apply(a, U[:, r, k * P:(k + 1) * P], V[:, bass.ds((i * 2 + r) * GW + k * P, P)], (i * 2 + r) * GT, k)
                        last.then_inc(w_ready, 1)
                a.wait_ge(qr, 1 + 1)
                a.activation(KQ, CQ, ACT.Sin, scale=TWOPI).then_inc(qs_ready, 1)

            @block.vector
            def _(v):
                v.sem_inc(x1_ready, 2)
                with v.Fori(0, NG // 2) as i:
                    for r in range(2):
                        n = i * 2 + r
                        u = U[:, r, :].rearrange("p (t c) -> p t c", c=P)
                        w = V[:, bass.ds(n * GW, GW)].rearrange("p (t c) -> p t c", c=P)
                        v.wait_ge(w_ready, 1 + n + 1)
                        v.tensor_tensor(u, u, G1[:, :].unsqueeze(1).to_broadcast([P, GT, P]), ALU.mult).then_inc(g_step, 1)
                        v.wait_ge(g_step, 1 + 2 * n + 1)
                        v.tensor_tensor(w, u, B1[:, :].unsqueeze(1).to_broadcast([P, GT, P]), ALU.add).then_inc(g_step, 1)
                        v.wait_ge(g_step, 1 + 2 * n + 2)
                        v.tensor_scalar(CQ[:, bass.ds(n * GT * 8, GT * 8)].rearrange("p (t k) -> p t k", k=8), w[:, :, 0:8], INV2PI, 0.25, ALU.mult, ALU.add).then_inc(x1_ready, 1)
                v.wait_ge(x1_ready, 1 + 2 + NG)
                v.tensor_scalar(KQ, CQ, ROUND, ROUND, ALU.add, ALU.subtract).then_inc(qk, 1)
                v.wait_ge(qk, 1 + 1)
                v.tensor_tensor(CQ, CQ, KQ, ALU.subtract).then_inc(qr, 1)
                v.wait_ge(qs_ready, 1 + 1)
                v.tensor_tensor(q9[:, :, 0:8], KQ.rearrange("p (t k) -> p t k", k=8), CP8[:, :].unsqueeze(1).to_broadcast([P, TT, 8]), ALU.mult)

        qb_ready, qt_turned, qt_ready, h_ready, ha, hv, fo_ready, fs_ready, ft_ready, v2_ready, c4, vb, sb_ = (
            sem(n) for n in ("q_copied", "q_turned", "q_T_ready", "hidden", "hidden_by_scalar", "hidden_by_vector", "ffn_out", "ffn_stored", "ffn_turned", "x1_ffn", "vector_norm2", "var2", "std2"))
        vsum = sem("x1_sum")
        UNITS = TT // 4
        UN_ = 4
        NQ = nf // 4

        def hidden_rows(s_, g):
            return (KR, U)[s_ % 2][:, g // 2, g % 2 * BANK:g % 2 * BANK + BANK]

        with nc.Block() as block:
            @block.gpsimd
            def _(pool):
                def copy(m, r):
                    for g in range(4):
                        last = pool.tensor_copy(QS[:, r, :, g, 0:9], Q9[:, bass.ds(m * 36, 36)].rearrange("p (t k) -> p t k", k=9))
                    last.then_inc(qb_ready, 1)
                copy(0, 0)
                with pool.Fori(0, UNITS // 2) as turn:
                    i = turn * 2
                    for r in range(2):
                        pool.wait_ge(qt_turned, 1 + i + r)
                        copy(i + r + 1, (r + 1) % 2)

            @block.tensor
            def _(t):
                def turn_q(m, r):
                    t.wait_ge(qb_ready, 1 + m + 1)
                    t.wait_ge(qt_ready, 1 + m)
                    for k in range(4):
                        last = t.transpose(qp[:, k * P:(k + 1) * P], QS[:, r, k, :, :].rearrange("p g c -> p (g c)"), C["ident"])
                    last.then_inc(qt_turned, 1)

                def second(i, s_):
                    r, q = s_ // NQ, s_ % NQ
                    t.wait_ge(ha, 1 + i * 2 * NQ + 2 * s_ + 2)
                    t.wait_ge(hv, 1 + i * 2 * NQ + 2 * s_ + 2)
                    if q == 0:
                        t.wait_ge(fs_ready, 1 + i + max(r - 1, 0))
                    for g in range(4):
                        last = t.matmul(fo[:, r % 2, :], W2T[:, 4 * q + g, :], hidden_rows(s_, g), start=q == 0 and g == 0, stop=q == NQ - 1 and g == 3)
                    if q == NQ - 1:
                        last.then_inc(fo_ready, 1)

                def turn_out(i, r):
                    t.wait_ge(fs_ready, 1 + i + r + 1)
                    t.wait_ge(v2_ready, 1 + i + r)
                    for k in range(4):
                        last = t.transpose(fp[:, k * P:(k + 1) * P], FS[:, r % 2, k * P:(k + 1) * P], C["ident"])
                    last.then_inc(ft_ready, 1)

                turn_q(0, 0)
                with t.Fori(0, UNITS // UN_) as turn:
                    i = turn * UN_
                    for s_ in range(UN_ * NQ):
                        r, q = s_ // NQ, s_ % NQ
                        if q == 0:
                            t.wait_ge(qt_ready, 1 + i + r + 1)
                        t.wait_ge(ha, 1 + i * 2 * NQ + 2 * s_)
                        t.wait_ge(hv, 1 + i * 2 * NQ + 2 * s_)
                        for g in range(4):
                            t.matmul(hp[:, g, :], W1T[32 * g:32 * g + 9, q, :], QT[32 * g:32 * g + 9, r % 2, :], start=True, stop=True, tile_position=(32 * g, 0)).then_inc(h_ready, 1)
                        if s_:
                            second(i, s_ - 1)
                        if q == 1 and r:
                            turn_out(i, r - 1)
                        if q == 2:
                            turn_q(i + r + 1, (r + 1) % 2)
                    second(i, UN_ * NQ - 1)
                    turn_out(i, UN_ - 1)

            @block.scalar
            def _(a):
                def store_q(m, r):
                    a.wait_ge(qt_turned, 1 + m + 1)
                    a.activation(QT[:, r, :], qp[:, :], ACT.Copy).then_inc(qt_ready, 1)

                def store_out(i, r):
                    a.wait_ge(fo_ready, 1 + i + r + 1)
                    a.activation(FS[:, r % 2, 0:BANK], fo[:, r % 2, :], ACT.Identity, bias=B2[:, 0:1]).then_inc(fs_ready, 1)

                store_q(0, 0)
                with a.Fori(0, UNITS // UN_) as turn:
                    i = turn * UN_
                    for s_ in range(UN_ * NQ):
                        r, q = s_ // NQ, s_ % NQ
                        for g in (0, 2):
                            a.wait_ge(h_ready, 1 + i * nf + s_ * 4 + g + 1)
                            a.activation(hidden_rows(s_, g), hp[:, g, :], ACT.Relu).then_inc(ha, 1)
                        if q == 0 and r:
                            store_out(i, r - 1)
                        if q == 2:
                            store_q(i + r + 1, (r + 1) % 2)
                    store_out(i, UN_ - 1)
                N.scalar(a, vb, sb_)

            @block.vector
            def _(v):
                def add_out(i, r):
                    n, at = i + r, bass.ds(i * BANK + r * BANK, BANK)
                    v.wait_ge(ft_ready, 1 + n + 1)
                    v.tensor_tensor(V[:, at], V[:, at], fp[:, :], ALU.add).then_inc(vsum, 1)
                    v.wait_ge(vsum, 1 + n + 1)
                    for k in range(4):
                        last = v.bn_stats(N.stats[:, bass.ds(i * 24 + (r * 4 + k) * 6, 6)], V[:, bass.ds(i * BANK + (r * 4 + k) * P, P)])
                    last.then_inc(v2_ready, 1)

                with v.Fori(0, UNITS // UN_) as turn:
                    i = turn * UN_
                    for s_ in range(UN_ * NQ):
                        r, q = s_ // NQ, s_ % NQ
                        for g in (1, 3):
                            v.wait_ge(h_ready, 1 + i * nf + s_ * 4 + g + 1)
                            v.tensor_scalar(hidden_rows(s_, g), hp[:, g, :], 0.0, None, ALU.max).then_inc(hv, 1)
                        if q == 1 and r:
                            add_out(i, r - 1)
                    add_out(i, UN_ - 1)
                v.wait_ge(v2_ready, 1 + UNITS)
                N.vector(v, Chain(v, c4), vb, sb_)

        w5, g5, x5, c5, vc, sc = (sem(n) for n in ("out_normed", "out_step", "out_added", "vector_norm3", "var3", "std3"))

        with nc.Block() as block:
            @block.scalar
            def _(a):
                with a.Fori(0, NG // 2) as i:
                    a.wait_ge(x5, 1 + i * 2)
                    for r in range(2):
                        for k in range(GT):
                            last = N.apply(a, U[:, r, k * P:(k + 1) * P], V[:, bass.ds((i * 2 + r) * GW + k * P, P)], (i * 2 + r) * GT, k)
                        last.then_inc(w5, 1)
                N.scalar(a, vc, sc)

            @block.vector
            def _(v):
                with v.Fori(0, NG // 2) as i:
                    for r in range(2):
                        n = i * 2 + r
                        ch = Chain(v, g5, n * 3)
                        u = U[:, r, :].rearrange("p (t c) -> p t c", c=P)
                        w = T[:, bass.ds(n * GW, GW)]
                        v.wait_ge(w5, 1 + n + 1)
                        ch(v.tensor_tensor(u, u, G2[:, :].unsqueeze(1).to_broadcast([P, GT, P]), ALU.mult))
                        ch(v.tensor_tensor(u, u, B2R[:, :].unsqueeze(1).to_broadcast([P, GT, P]), ALU.add))
                        ch(v.tensor_tensor(w, w, U[:, r, :], ALU.add))
                        for k in range(GT):
                            last = v.bn_stats(N.stats[:, bass.ds((n * GT + k) * 6, 6)], T[:, bass.ds(n * GW + k * P, P)])
                        last.then_inc(x5, 1)
                v.wait_ge(x5, 1 + NG)
                N.vector(v, Chain(v, c5), vc, sc)


EX = 8
BIG = 1.0e30


def moe_layer(nc, d, T, C, N, tag, last_norm):
    with stage_semaphores(nc, tag) as sem, ExitStack() as ctx:
        def sb(name, shape, dt=F32):
            return ctx.enter_context(nc.sbuf_tensor(tag + name, shape, dt))

        UT = sb("normed_T", [P, TT * P])
        UN, UB = sb("normed", [P, 2, BANK]), sb("normed_T_block", [P, 2, BANK])
        RW, RB, EW = sb("router_w", [P, EX]), sb("router_b", [P, EX]), sb("expert_w", [P, EX, P])
        EB, EH, ER = sb("expert_b", [3, EX * P]), sb("expert_b_part", [3, EX * P], BF16), sb("expert_b_parts", [3, EX * P], BF16)
        ON = sb("ones", [3, P], BF16)
        LG, S1, S2, TMP = (sb(n, [P, TT * EX]) for n in ("logits", "first", "second", "scratch"))
        M1, M2, F1 = (sb(n, [P, TT]) for n in ("max1", "max2", "pick"))
        PRD, HS, RD = sb("weighted", [P, 2, EX * P]), sb("half_sum", [P, 2, EX * P // 2]), sb("moe_out", [P, 2, P])
        lg3, s13, s23, tm3 = (z[:, :].rearrange("p (t e) -> p t e", e=EX) for z in (LG, S1, S2, TMP))
        up = ctx.enter_context(nc.psum_tensor(tag + "turned", [P, 2, BANK], F32))
        lp = ctx.enter_context(nc.psum_tensor(tag + "logit_sums", [P, 2, BANK], F32))
        ep = ctx.enter_context(nc.psum_tensor(tag + "experts", [P, 2, 2, BANK], F32))
        loaded, prep, un_ready, turned, ub_ready, lp_ready, lg_ready, kept = (
            sem(n) for n in ("loaded", "bias_parts", "un_ready", "turned", "ut_ready", "logits", "logits_ready", "ut_kept"))

        with nc.Block() as block:
            @block.sync
            def _(sp):
                for dst, src in ((RW[:, :], d[tag + "router_w"]), (RB[:, :], d[tag + "router_b"].partition_broadcast(P)),
                                 (EW[:, :, :], d[tag + "expert_w"].rearrange("e d c -> d e c")),
                                 (EB[:, :], d[tag + "expert_b"].rearrange("e c -> (e c)").partition_broadcast(3))):
                    sp.dma_start(dst, src).then_inc(loaded, 16)
                sp.wait_ge(loaded, 1 + 64)

            @block.scalar
            def _(a):
                with a.Fori(0, TT // 8) as i:
                    for r in range(2):
                        a.wait_ge(turned, 1 + i * 2)
                        for k in range(4):
                            last = N.apply(a, UN[:, r, k * P:(k + 1) * P], T[:, bass.ds((i * 2 + r) * BANK + k * P, P)], (i * 2 + r) * 4, k)
                        last.then_inc(un_ready, 1)

            @block.tensor
            def _(t):
                t.wait_ge(loaded, 1 + 64)
                with t.Fori(0, TT // 8) as i:
                    for r in range(2):
                        n = i * 2 + r
                        t.wait_ge(un_ready, 1 + n + 1)
                        for k in range(4):
                            last = t.transpose(up[:, r, k * P:(k + 1) * P], UN[:, r, k * P:(k + 1) * P], C["ident"])
                        last.then_inc(turned, 1)
                    for r in range(2):
                        n = i * 2 + r
                        t.wait_ge(ub_ready, 1 + n + 1)
                        for k in range(4):
                            last = t.matmul(lp[:, r, k * EX:(k + 1) * EX], UB[:, r, k * P:(k + 1) * P], RW[:, :], start=True, stop=True)
                        last.then_inc(lp_ready, 1)

            @block.gpsimd
            def _(pool):
                with pool.Fori(0, TT // 8) as i:
                    for r in range(2):
                        pool.wait_ge(ub_ready, 1 + i * 2 + r + 1)
                        pool.tensor_copy(UT[:, bass.ds((i * 2 + r) * BANK, BANK)], UB[:, r, :]).then_inc(kept, 1)

            @block.vector
            def _(v):
                v.wait_ge(loaded, 1 + 64)
                ch = Chain(v, prep)
                v.memset(ON[:, :], 1.0)
                ch(v.tensor_copy(EH[:, :], EB[:, :]))
                ch(v.tensor_scalar(ER[:, :], EH[:, :], C["ident"][0:3, 0:1], None, ALU.mult))
                for k in (1, 2):
                    ch(v.tensor_tensor(EB[:, :], EB[:, :], EH[:, :], ALU.subtract))
                    ch(v.tensor_copy(EH[:, :], EB[:, :]))
                    ch(v.scalar_tensor_tensor(ER[:, :], EH[:, :], C["ident"][0:3, k:k + 1], ER[:, :], ALU.mult, ALU.add))
                with v.Fori(0, TT // 8) as i:
                    for r in range(2):
                        n = i * 2 + r
                        v.wait_ge(turned, 1 + n + 1)
                        v.wait_ge(kept, 1 + i * 2)
                        v.wait_ge(lp_ready, 1 + i * 2)
                        v.tensor_copy(UB[:, r, :], up[:, r, :]).then_inc(ub_ready, 1)
                    for r in range(2):
                        n = i * 2 + r
                        v.wait_ge(lp_ready, 1 + n + 1)
                        v.tensor_tensor(LG[:, bass.ds(n * 4 * EX, 4 * EX)].rearrange("p (t e) -> p t e", e=EX), lp[:, r, 0:4 * EX].rearrange("p (t e) -> p t e", e=EX),
                                        RB[:, :].unsqueeze(1).to_broadcast([P, 4, EX]), ALU.add).then_inc(lg_ready, 1)

        chain, diff_ready, e_ready, gates = sem("gate_steps"), sem("gate_diff"), sem("gate_exp"), sem("gates_ready")

        with nc.Block() as block:
            def wide(m):
                return m[:, :].unsqueeze(2).to_broadcast([P, TT, EX])

            @block.vector
            def _(v):
                ch = Chain(v, chain)
                for sel, top in ((s13, M1), (s23, M2)):
                    ch(v.tensor_reduce(top[:, :], lg3, AX.X, ALU.max))
                    ch(v.tensor_tensor(sel, lg3, wide(top), ALU.is_equal))
                    ch(v.tensor_tensor(sel, sel, C["first"].unsqueeze(1).to_broadcast([P, TT, EX]), ALU.mult))
                    ch(v.tensor_reduce(F1[:, :], sel, AX.X, ALU.max))
                    ch(v.tensor_tensor(sel, sel, wide(F1), ALU.is_equal))
                    if top is M1:
                        ch(v.scalar_tensor_tensor(LG[:, :], S1[:, :], -BIG, LG[:, :], ALU.mult, ALU.add))
                v.tensor_tensor(M2[:, :], M2[:, :], M1[:, :], ALU.subtract).then_inc(diff_ready, 1)
                v.wait_ge(e_ready, 1 + 1)
                ch(v.tensor_scalar(F1[:, :], M1[:, :], 1.0, None, ALU.add))
                ch(v.reciprocal(F1[:, :], F1[:, :]))
                ch(v.tensor_tensor(M2[:, :], M1[:, :], F1[:, :], ALU.mult))
                ch(v.tensor_tensor(s13, s13, wide(F1), ALU.mult))
                ch(v.tensor_tensor(s23, s23, wide(M2), ALU.mult))
                v.tensor_tensor(LG[:, :], S1[:, :], S2[:, :], ALU.add).then_inc(gates, 1)

            @block.scalar
            def _(a):
                a.wait_ge(diff_ready, 1 + 1)
                a.activation(M1[:, :], M2[:, :], ACT.Exp).then_inc(e_ready, 1)

        copied, e_out, wv, wa, hs_ready, rd_ready, t_ready, st_ready, c2, vv, ss = (
            sem(n) for n in ("copied", "experts_out", "weighted_by_vector", "weighted_by_scalar", "half_sums", "moe_out", "t_ready", "stats_ready", "vector_norm", "var", "std"))

        with nc.Block() as block:
            @block.gpsimd
            def _(pool):
                with pool.Fori(0, TT // 8) as i:
                    pool.wait_ge(e_out, 1 + i * 8)
                    for r in range(2):
                        pool.tensor_copy(UB[:, r, :], UT[:, bass.ds((i * 2 + r) * BANK, BANK)]).then_inc(copied, 1)
                    for k in range(8):
                        n = i * 8 + k
                        q = k % 2
                        pool.wait_ge(wv, 1 + n + 1)
                        pool.wait_ge(wa, 1 + n + 1)
                        pool.wait_ge(rd_ready, 1 + i * 8 + max(k - 1, 0))
                        pool.tensor_tensor(HS[:, q, :], PRD[:, q, 0:BANK], PRD[:, q, BANK:2 * BANK], ALU.add).then_inc(hs_ready, 1)

            @block.tensor
            def _(t):
                with t.Fori(0, TT // 8) as i:
                    for k in range(8):
                        n = i * 8 + k
                        if k % 4 == 0:
                            t.wait_ge(copied, 1 + i * 2 + k // 4 + 1)
                        t.wait_ge(wv, 1 + i * 8 + max(k - 1, 0))
                        t.wait_ge(wa, 1 + i * 8 + max(k - 1, 0))
                        for h in range(2):
                            t.matmul(ep[:, k % 2, h, :], UB[:, k // 4, (k % 4) * P:(k % 4 + 1) * P], EW[:, 4 * h:4 * h + 4, :].rearrange("p e c -> p (e c)"), start=True, stop=False)
                            last = t.matmul(ep[:, k % 2, h, :], ON[:, :], ER[:, h * BANK:(h + 1) * BANK], start=False, stop=True)
                        last.then_inc(e_out, 1)

            @block.scalar
            def _(a):
                with a.Fori(0, TT // 8) as i:
                    for k in range(8):
                        n = i * 8 + k
                        a.wait_ge(e_out, 1 + n + 1)
                        a.wait_ge(hs_ready, 1 + i * 8 + max(k - 1, 0))
                        for e in range(4, 8):
                            last = a.activation(PRD[:, k % 2, e * P:(e + 1) * P], ep[:, k % 2, 1, (e - 4) * P:(e - 3) * P], ACT.Copy, scale=LG[:, bass.ds(n * EX + e, 1)])
                        last.then_inc(wa, 1)
                if last_norm:
                    N.scalar(a, vv, ss)

            @block.vector
            def _(v):
                with v.Fori(0, TT // 8) as i:
                    for k in range(8 + 1):
                        if k < 8:
                            n = i * 8 + k
                            v.wait_ge(e_out, 1 + n + 1)
                            v.wait_ge(hs_ready, 1 + i * 8 + max(k - 1, 0))
                            v.tensor_tensor(PRD[:, k % 2, 0:BANK].rearrange("p (e c) -> p e c", c=P), ep[:, k % 2, 0, :].rearrange("p (e c) -> p e c", c=P),
                                            LG[:, bass.ds(n * EX, 4)].unsqueeze(2).to_broadcast([P, 4, P]), ALU.mult).then_inc(wv, 1)
                        if k > 0:
                            q = (k - 1) % 2
                            n = i * 8 + k - 1
                            v.wait_ge(hs_ready, 1 + n + 1)
                            v.tensor_reduce(RD[:, q, :], HS[:, q, :].rearrange("p (e c) -> p c e", c=P), AX.X, ALU.add).then_inc(rd_ready, 1)
                            v.wait_ge(rd_ready, 1 + n + 1)
                            v.tensor_tensor(T[:, bass.ds(n * P, P)], T[:, bass.ds(n * P, P)], RD[:, q, :], ALU.add).then_inc(t_ready, 1)
                            if last_norm:
                                v.wait_ge(t_ready, 1 + n + 1)
                                v.bn_stats(N.stats[:, bass.ds(n * 6, 6)], T[:, bass.ds(n * P, P)]).then_inc(st_ready, 1)
                if last_norm:
                    v.wait_ge(st_ready, 1 + TT)
                    N.vector(v, Chain(v, c2), vv, ss)


CHUNK = 2 * BANK
CT_ = CHUNK // P
NCH = L // CHUNK


def additive_attention_layer(nc, d, T, C, N):
    tag = "aa_"
    with stage_semaphores(nc, tag) as sem, ExitStack() as ctx:
        def sb(name, shape, dt=F32):
            return ctx.enter_context(nc.sbuf_tensor(tag + name, shape, dt))

        UN, UT, FR = sb("normed", [P, L]), sb("normed_T", [P, L]), sb("f_8_times", [P, L])
        GB = sb("g_bias", [P, L // 8])
        NR = 8
        TH = sb("tanh", [P, NR, CHUNK])
        ET = sb("weights", [P, 2, CHUNK])
        DEN, DR, OT = sb("denominators", [P, CHUNK]), sb("denominators_inv", [P, CHUNK]), sb("out_T", [P, CHUNK])
        UBK = sb("normed_block", [P, 2, P])
        WF, WG = sb("w_f", [P, 8, 16]), sb("w_g", [P, 8, P])
        W2C, B1C, B2C = sb("w2_col", [P, 1]), sb("b1_col", [P, 1]), sb("b2_col", [P, 1])
        W2S = sb("w2_spread", [P, 4, 32])
        ONE = sb("ones", [P, P])
        ZR = sb("zeros", [P, BANK], BF16)
        sp_ = ctx.enter_context(nc.psum_tensor(tag + "scores", [P, 2, CHUNK], F32))
        op = ctx.enter_context(nc.psum_tensor(tag + "out_sum", [P, CHUNK], F32))
        dp = ctx.enter_context(nc.psum_tensor(tag + "den_sum", [P, 2, BANK], F32))

        loaded, cleared, wready = sem("loaded"), sem("cleared"), sem("weights_ready")
        un_ready, un_turned, ut_ready, f_ready, f_stored, g_sum, g_ready = (sem(n) for n in ("un_ready", "un_turned", "ut_ready", "f_ready", "f_stored", "g_sum", "g_ready"))
        ub_ready, th_ready, th_used, e_ready, em_ready, o_done = (sem(n) for n in ("keys_copied", "tanh_ready", "tanh_used", "exp_ready", "weights_summed", "tile_added"))
        masked, den_zero, o_ready, den_ready, dr_ready, dr_step, ot_ready, ot_turned, t_ready, st_ready, c2, vv, ss = (
            sem(n) for n in ("masked", "den_zero", "chunk_out", "den_ready", "den_inv", "den_step", "ot_ready", "ot_turned", "t_ready", "stats_ready", "vector_norm", "var", "std"))
        TILES = sum((c + 1) * CT_ for c in range(NCH))

        def plan(c):
            return sum((x + 1) * CT_ for x in range(c)), c * CT_

        with nc.Block() as block:
            @block.sync
            def _(sp):
                def load(dst, src):
                    sp.dma_start(dst, src, allow_slow_non_contiguous=True).then_inc(loaded, 16)
                w1 = d["L3_attn_W1"]
                sp.wait_ge(cleared, 1 + 1)
                for j in range(8):
                    load(WF[:, j, :], w1[0:P, :])
                    load(WG[:, j, 16 * j:16 * j + 16], w1[P:2 * P, :])
                    load(B1C[16 * j:16 * j + 16, :], d["L3_attn_b1"].rearrange("(c a) -> c a", a=1))
                    load(W2C[16 * j:16 * j + 16, :], d["L3_attn_w2"])
                load(B2C[:, :], d["L3_attn_b2"].partition_broadcast(P))
                sp.wait_ge(loaded, 1 + 16 * 33)

            @block.gpsimd
            def _(pool):
                pool.memset(WG[:, :, :], 0.0).then_inc(cleared, 1)
                pool.memset(ONE[:, :], 1.0).then_inc(cleared, 1)
                pool.memset(ZR[:, :], 0.0).then_inc(cleared, 1)
                pool.wait_ge(cleared, 1 + 3)
                with pool.Fori(0, NB) as b:
                    for c in range(NCH):
                        first, full = plan(c)
                        n0 = b * TILES + first
                        if full:
                            with pool.Fori(0, full, 2) as j:
                                pool.wait_ge(un_ready, 1 + (b + 1) * 8)
                                pool.wait_ge(o_done, 1 + n0 + j)
                                for r in range(2):
                                    pool.tensor_copy(UBK[:, r, :], UN[:, bass.ds(j * P + r * P, P)]).then_inc(ub_ready, 1)
                        for j in range(CT_):
                            rows = UN[:, (full + j) * P:(full + j + 1) * P]
                            pool.wait_ge(un_ready, 1 + (b + 1) * 8)
                            if j % 2 == 0:
                                pool.wait_ge(o_done, 1 + n0 + full + j)
                            pool.tensor_tensor(UBK[:, j % 2, :], rows, ONE[:, :], ALU.mult).then_inc(ub_ready, 1)

            @block.scalar
            def _(a):
                a.wait_ge(loaded, 1 + 16 * 33)
                a.activation(GB[:, 0:1], B2C[:, :], ACT.Exp)
                with a.Fori(0, NB) as b:
                    a.wait_ge(o_ready, 1 + b * NCH)
                    for q in range(8):
                        for k in range(4):
                            last = N.apply(a, UN[:, (4 * q + k) * P:(4 * q + k + 1) * P], T[:, bass.ds(b * L + (4 * q + k) * P, P)], b * NT, 4 * q + k)
                        last.then_inc(un_ready, 1)
                    a.wait_ge(g_ready, 1 + b + 1)
                    a.wait_ge(f_stored, 1 + (b + 1) * 8)

                    def exps(n, q, lo):
                        a.wait_ge(th_used, 1 + n * 4 + 4 + NR // 4)
                        a.activation(ET[:, q, 0:CHUNK - lo], sp_[:, q, 0:CHUNK - lo], ACT.Exp, bias=B2C[:, 0:1]).then_inc(e_ready, 1)

                    def order():
                        return [4 * q + t for t in range(4) for q in range(4)]

                    for c in range(NCH):
                        first, full = plan(c)
                        n0 = b * TILES + first
                        if full:
                            with a.Fori(0, full, 4) as j:
                                for r in range(4):
                                    for s_, blk in enumerate(order()):
                                        if s_ == 4 and r > 0:
                                            a.wait_ge(o_done, 1 + n0 + j + max(r - 2, 0))
                                            exps(n0 + j + r - 1, (r - 1) % 2, 0)
                                        if s_ % 4 == 0:
                                            a.wait_ge(th_used, 1 + (n0 + j + r) * 4 + s_ // 4 + 1)
                                        a.activation(TH[:, s_ % NR, :], FR[:, c * CHUNK:(c + 1) * CHUNK], ACT.Tanh, bias=GB[:, bass.ds((j + r) * 16 + blk, 1)]).then_inc(th_ready, 1)
                                a.wait_ge(o_done, 1 + n0 + j + 2)
                                exps(n0 + j + 3, 1, 0)
                        for j in range(CT_ + 1):
                            for s_, blk in enumerate(order()):
                                if j < CT_:
                                    lo = j * P
                                    if s_ == 4 and j > 0:
                                        a.wait_ge(o_done, 1 + n0 + full + max(j - 2, 0))
                                        exps(n0 + full + j - 1, (j - 1) % 2, (j - 1) * P)
                                    if s_ % 4 == 0:
                                        a.wait_ge(th_used, 1 + (n0 + full + j) * 4 + s_ // 4 + 1)
                                    a.activation(TH[:, s_ % NR, 0:CHUNK - lo], FR[:, c * CHUNK + lo:(c + 1) * CHUNK], ACT.Tanh, bias=GB[:, (full + j) * 16 + blk:(full + j) * 16 + blk + 1]).then_inc(th_ready, 1)
                            if j == CT_:
                                a.wait_ge(o_done, 1 + n0 + full + j - 2)
                                exps(n0 + full + j - 1, (j - 1) % 2, (j - 1) * P)
                N.scalar(a, vv, ss)

            @block.tensor
            def _(t):
                t.wait_ge(loaded, 1 + 16 * 33)
                t.wait_ge(cleared, 1 + 3)
                t.wait_ge(wready, 1 + 4)
                t.sem_inc(th_used, NR // 4)
                with t.Fori(0, NB) as b:
                    for q in range(8):
                        t.wait_ge(un_ready, 1 + b * 8 + q + 1)
                        if q >= 2:
                            t.wait_ge(ut_ready, 1 + b * 8 + q - 1)
                        elif q == 0:
                            t.wait_ge(t_ready, 1 + b * 2 * NCH)
                        for k in range(4):
                            last = t.transpose(dp[:, q % 2, k * P:(k + 1) * P], UN[:, (4 * q + k) * P:(4 * q + k + 1) * P], C["ident"])
                        last.then_inc(un_turned, 1)
                    t.wait_ge(ut_ready, 1 + b * 8 + 8)
                    for q in range(8):
                        if q >= 2:
                            t.wait_ge(f_stored, 1 + b * 8 + q - 1)
                        t.matmul(dp[:, q % 2, :], WF[:, :, :].rearrange("p j a -> p (j a)"), UT[:, q * BANK:(q + 1) * BANK], start=True, stop=True).then_inc(f_ready, 1)
                    t.wait_ge(f_stored, 1 + b * 8 + 8)
                    for j in range(8):
                        last = t.matmul(dp[:, 0, :], WG[:, j, :], UT[:, j:L:8], start=j == 0, stop=j == 7)
                    last.then_inc(g_sum, 1)

                    def scores(n, q4, lo):
                        w = CHUNK - lo
                        for tt in range(4):
                            t.wait_ge(th_ready, 1 + n * 16 + tt * 4 + 4)
                            for h in range(0, w, BANK):
                                e = min(w, h + BANK)
                                for q in range(4):
                                    last = t.matmul(sp_[32 * q:32 * q + 32, q4, h:e], W2S[:, tt, :], TH[:, (4 * tt + q) % NR, h:e], start=tt == 0, stop=tt == 3, tile_position=(0, 32 * q))
                            last.then_inc(th_used, 1)
                            yield tt

                    def add_tile(n, q4, lo):
                        t.wait_ge(em_ready, 1 + n + 1)
                        t.wait_ge(ub_ready, 1 + n + 1)
                        for h in range(2):
                            s0 = max(lo, h * BANK)
                            if s0 < (h + 1) * BANK:
                                last = t.matmul(op[:, s0:(h + 1) * BANK], UBK[:, q4, :], ET[:, q4, s0 - lo:(h + 1) * BANK - lo], start=False, stop=False)
                        last.then_inc(o_done, 1)

                    for c in range(NCH):
                        first, full = plan(c)
                        n0 = b * TILES + first
                        t.wait_ge(ot_ready, 1 + b * NCH + c)
                        t.wait_ge(g_ready, 1 + b + 1)
                        for h in range(2):
                            t.matmul(op[:, h * BANK:(h + 1) * BANK], ZR[:, 0:P], ZR[:, :], start=True, stop=False)
                        if full:
                            with t.Fori(0, full, 4) as j:
                                for r in range(4):
                                    for tt in scores(n0 + j + r, r % 2, 0):
                                        if tt == 1 and r > 0:
                                            add_tile(n0 + j + r - 1, (r - 1) % 2, 0)
                                add_tile(n0 + j + 3, 1, 0)
                        for j in range(CT_):
                            for tt in scores(n0 + full + j, j % 2, j * P):
                                if tt == 1 and j > 0:
                                    add_tile(n0 + full + j - 1, (j - 1) % 2, (j - 1) * P)
                        add_tile(n0 + full + CT_ - 1, (CT_ - 1) % 2, (CT_ - 1) * P)
                        for h in range(2):
                            last = t.matmul(op[:, h * BANK:(h + 1) * BANK], ZR[:, 0:P], ZR[:, :], start=False, stop=True)
                        last.then_inc(o_ready, 1)
                        t.wait_ge(t_ready, 1 + (b * NCH + c) * 2)
                        for h in range(2):
                            last = t.matmul(dp[:, h, :], ONE[:, :], DEN[:, h * BANK:(h + 1) * BANK], start=True, stop=True)
                        last.then_inc(den_ready, 1)
                        t.wait_ge(ot_ready, 1 + b * NCH + c + 1)
                        for h in range(2):
                            for k in range(4):
                                last = t.transpose(dp[:, h, k * P:(k + 1) * P], OT[:, (4 * h + k) * P:(4 * h + k + 1) * P], C["ident"])
                            last.then_inc(ot_turned, 1)

            @block.vector
            def _(v):
                v.wait_ge(loaded, 1 + 16 * 33)
                for k in range(4):
                    v.tensor_scalar(W2S[:, k, :], C["pick"][:, 32 * k:32 * k + 32], W2C[:, 0:1], None, ALU.mult).then_inc(wready, 1)
                with v.Fori(0, NB) as b:
                    for q in range(8):
                        v.wait_ge(un_turned, 1 + b * 8 + q + 1)
                        v.tensor_copy(UT[:, q * BANK:(q + 1) * BANK], dp[:, q % 2, :]).then_inc(ut_ready, 1)
                    for q in range(8):
                        v.wait_ge(f_ready, 1 + b * 8 + q + 1)
                        v.tensor_copy(FR[:, q * BANK:(q + 1) * BANK], dp[:, q % 2, :]).then_inc(f_stored, 1)
                    v.wait_ge(g_sum, 1 + b + 1)
                    v.tensor_scalar(GB[:, :], dp[:, 0, :], B1C[:, 0:1], None, ALU.add).then_inc(g_ready, 1)

                    def sum_tile(n, q, lo):
                        v.tensor_tensor(DEN[:, lo:CHUNK], DEN[:, lo:CHUNK], ET[:, q, 0:CHUNK - lo], ALU.add).then_inc(em_ready, 1)

                    for c in range(NCH):
                        first, full = plan(c)
                        n0 = b * TILES + first
                        v.wait_ge(den_ready, 1 + b * NCH + c)
                        v.memset(DEN[:, :], 0.0).then_inc(den_zero, 1)
                        if full:
                            with v.Fori(0, full, 2) as j:
                                for r in range(2):
                                    v.wait_ge(den_zero, 1 + b * NCH + c + 1)
                                    v.wait_ge(e_ready, 1 + n0 + j + r + 1)
                                    v.wait_ge(em_ready, 1 + n0 + j + r)
                                    sum_tile(n0 + j + r, r, 0)
                        for j in range(CT_):
                            n = n0 + full + j
                            v.wait_ge(e_ready, 1 + n + 1)
                            v.wait_ge(em_ready, 1 + n)
                            v.wait_ge(den_zero, 1 + b * NCH + c + 1)
                            v.tensor_tensor(ET[:, j % 2, 0:P], ET[:, j % 2, 0:P], C["strict"], ALU.mult).then_inc(masked, 1)
                            v.wait_ge(masked, 1 + (b * NCH + c) * CT_ + j + 1)
                            sum_tile(n, j % 2, j * P)
                        v.wait_ge(den_ready, 1 + b * NCH + c + 1)
                        ch = Chain(v, dr_step, (b * NCH + c) * 2)
                        ch(v.tensor_scalar(DR[:, :], dp[:, :, :].rearrange("p a n -> p (a n)"), 1e-10, None, ALU.add))
                        ch(v.reciprocal(DR[:, :], DR[:, :]))
                        v.wait_ge(o_ready, 1 + b * NCH + c + 1)
                        v.tensor_tensor(OT[:, :], op[:, :], DR[:, :], ALU.mult).then_inc(ot_ready, 1)
                        for h in range(2):
                            at = b * L + c * CHUNK + h * BANK
                            v.wait_ge(ot_turned, 1 + (b * NCH + c) * 2 + h + 1)
                            v.tensor_tensor(T[:, bass.ds(at, BANK)], T[:, bass.ds(at, BANK)], dp[:, h, :], ALU.add).then_inc(t_ready, 1)
                            v.wait_ge(t_ready, 1 + (b * NCH + c) * 2 + h + 1)
                            for k in range(4):
                                last = v.bn_stats(N.stats[:, bass.ds((b * NT + c * CT_ + 4 * h + k) * 6, 6)], T[:, bass.ds(at + k * P, P)])
                            last.then_inc(st_ready, 1)
                v.wait_ge(st_ready, 1 + 2 * NB * NCH)
                N.vector(v, Chain(v, c2), vv, ss)


def to_channels(nc, T, C, out):
    with stage_semaphores(nc, "out_") as sem, ExitStack() as ctx:
        XB = ctx.enter_context(nc.sbuf_tensor("out_block", [P, 2, BANK], F32))
        tp = ctx.enter_context(nc.psum_tensor("out_psum", [P, 2, BANK], F32))
        copied, turned, stored, sent = (sem(n) for n in ("copied", "turned", "stored", "sent"))
        with nc.Block() as block:
            @block.gpsimd
            def _(pool):
                with pool.Fori(0, TT // 8) as i:
                    for r in range(2):
                        pool.wait_ge(turned, 1 + i * 2)
                        pool.tensor_copy(XB[:, r, :], T[:, bass.ds(i * 2 * BANK + r * BANK, BANK)]).then_inc(copied, 1)

            @block.tensor
            def _(t):
                with t.Fori(0, TT // 8) as i:
                    for r in range(2):
                        t.wait_ge(copied, 1 + i * 2 + r + 1)
                        t.wait_ge(stored, 1 + i * 2)
                        for k in range(4):
                            last = t.transpose(tp[:, r, k * P:(k + 1) * P], XB[:, r, k * P:(k + 1) * P], C["ident"])
                        last.then_inc(turned, 1)

            @block.vector
            def _(v):
                with v.Fori(0, TT // 8) as i:
                    for r in range(2):
                        v.wait_ge(turned, 1 + i * 2 + r + 1)
                        v.tensor_copy(T[:, bass.ds(i * 2 * BANK + r * BANK, BANK)], tp[:, r, :]).then_inc(stored, 1)

            @block.sync
            def _(sp):
                for b in range(NB):
                    sp.wait_ge(stored, 1 + (b + 1) * NT // 4)
                    sp.dma_start(out.rearrange("b c h w -> b c (h w)")[b], T[:, b * L:(b + 1) * L]).then_inc(sent, 16)
                sp.wait_ge(sent, 1 + 16 * NB)


def build(nc, d, out, offsets):
    with ExitStack() as ctx:
        X = ctx.enter_context(nc.sbuf_tensor("x_rows", [P, NB * L], F32))
        n_c = sum(n for _, n in offsets.values())
        CT = ctx.enter_context(nc.sbuf_tensor("consts_sb", [P, n_c], F32))
        C = {n: CT[:, o:o + w] for n, (o, w) in offsets.items()}
        C["all"] = CT[:, :]
        FLAG = ctx.enter_context(nc.sbuf_tensor("far_flag", [P, 1], I32))
        deform_layer(nc, d, X, C, True, FLAG[:, :])
        far = nc.values_load(FLAG[0:1, 0:1], min_val=0, max_val=1)
        with nc.If(far > 0):
            deform_layer(nc, d, X, C, False, None)
        mamba_layer(nc, d, X, C)
        N = Norm(lambda n, shape: ctx.enter_context(nc.sbuf_tensor(n, shape, F32)))
        to_tokens(nc, X, C, N)
        quantum_layer(nc, d, X, C, N)
        moe_layer(nc, d, X, C, N, "L2_ffn_", True)
        additive_attention_layer(nc, d, X, C, N)
        moe_layer(nc, d, X, C, N, "L3_ffn_", False)
        to_channels(nc, X, C, out)


def kernel(**inputs):
    import concourse.bacc as _bacc
    from concourse.bass_utils import run_bass_kernel_spmd as _run

    nc = _bacc.Bacc("TRN2", target_bir_lowering=False, num_devices=1)
    arrays, d = {}, {}
    parts = constants()
    offsets, at = {}, 0
    for n, a in parts.items():
        offsets[n] = (at, a.shape[1])
        at += a.shape[1]
    arrays["in_consts"] = np.concatenate(list(parts.values()), axis=1)
    for n, a in inputs.items():
        arrays["in_" + n] = np.ascontiguousarray(a)
    for n, a in arrays.items():
        d[n[3:]] = nc.dram_tensor(n, a.shape, F32, kind="ExternalInput").ap()
    out = nc.dram_tensor("out_x", inputs["x"].shape, F32, kind="ExternalOutput").ap()
    build(nc, d, out, offsets)
    r = _run(nc, [arrays], core_ids=[0])
    return r.results[0]["out_x"]
```
